# Optimizing a Trainium2 kernel written in Bass

```python
import numpy as np
import jax
import jax.numpy as jnp

def _softmax(x, axis=-1):
    return jax.nn.softmax(x, axis=axis)

def _gelu(x):
    return jax.nn.gelu(x, approximate=True)

def _silu(x):
    return jax.nn.silu(x)

def _sigmoid(x):
    return jax.nn.sigmoid(x)

def _layernorm(x, axis=-1, eps=1e-05):
    m = jnp.mean(x, axis=axis, keepdims=True)
    v = jnp.var(x, axis=axis, keepdims=True)
    return (x - m) / jnp.sqrt(v + eps)

def _scatter_add(tgt, idx, src, axis=0):
    return tgt.at[idx].add(src)

def _segment_sum(src, seg, n):
    return jax.ops.segment_sum(src, seg, n)
kernel_name = 'mk_adj_preln_d1_adj_r2_36bb79'

def setup_inputs(seed: int=0):
    np.random.seed(seed)
    _w = jnp.asarray

    def _rec_inputs():
        import jax
        import jax.numpy as jnp
        _gk = jax.random.key(seed)
        x = -7.737e-05 + 0.05006 * jax.random.normal(jax.random.fold_in(_gk, 1), (4096, 64), jnp.float32)
        _a = jax.random.bernoulli(jax.random.fold_in(_gk, 2), 0.00390625, (4096, 4096))
        _a = jnp.logical_or(_a, jnp.swapaxes(_a, -1, -2))
        _a = jnp.logical_or(_a, jnp.eye(4096, dtype=bool))
        _af = _a.astype(jnp.float32)
        adj = _af
        return (x, adj)
    x, adj = _rec_inputs()

    def _L0_gnn_setup():
        import jax, jax.numpy as jnp
        import numpy as np
        N = 2048
        D = 64
        NUM_LAYERS = 2
        THETA0 = 0.000244
        THETA_MAX = 0.0003
        LAM = 0.1
        TAU = 1.0
        EPS = 1e-06
        H_DENSITY = 0.005

        def _safe_norm(x, axis):
            return jnp.sqrt(jnp.maximum(jnp.sum(x * x, axis=axis), 1e-16))

        def _layer(x, H, W, Theta, Wq, bq, Wv, bv, iteration):
            scale = D ** (-0.5)
            theta_base = THETA0 + (1.0 - np.exp(-LAM * iteration)) * (THETA_MAX - THETA0)
            th_comp = theta_base
            th_edge = min(theta_base, 0.8)
            th_node = min(theta_base, 0.7)
            structural = _safe_norm(x @ W, axis=1)
            Q = x @ Wq + bq
            V = x @ Wv + bv
            edge_feat = H.T @ V
            att = Q @ edge_feat.T * scale * H
            att = jax.nn.softmax(att, axis=1)
            att_scores = att.mean(axis=0)
            importance = 0.5 * structural + 0.5 * att_scores
            comp_scores = jax.nn.softmax(importance / TAU)
            comp_mask = comp_scores >= th_comp
            x_comp = x * comp_mask[:, None]
            nrm = jnp.maximum(_safe_norm(x_comp, axis=1), 1e-08)
            xn = x_comp / nrm[:, None]
            cos = xn @ xn.T
            edge_scores = jax.nn.softmax(cos * H / TAU, axis=1)
            edge_mask = (edge_scores >= th_edge) & comp_mask[:, None]
            H_pruned = H * edge_mask
            connectivity = H_pruned.sum(axis=1)
            feat_mag = _safe_norm(x_comp, axis=1)
            node_scores = jax.nn.softmax(connectivity * feat_mag / TAU)
            connected = (H_pruned * edge_mask).sum(axis=1) > 0
            node_mask = (node_scores >= th_node) & connected
            x_final = x_comp * node_mask[:, None]
            vdeg = jnp.maximum(H_pruned.sum(axis=1), EPS)
            edeg = jnp.maximum(H_pruned.sum(axis=0), EPS)
            dv_isqrt = 1.0 / jnp.sqrt(vdeg)
            de_inv = 1.0 / edeg
            transformed = x_final @ W
            agg = H_pruned.T * dv_isqrt[None, :] @ transformed
            agg = agg * de_inv[:, None]
            msg = dv_isqrt[:, None] * (H_pruned @ agg)
            msg = msg @ Theta
            return jax.nn.relu(msg)
        key = jax.random.key(seed)
        ks = jax.random.split(key, 8)
        xav = 0.125
        X = jax.random.normal(ks[0], (N, D), jnp.float32) * 0.05
        W = jax.random.normal(ks[1], (D, D), jnp.float32) * xav
        Theta = jax.random.normal(ks[2], (D, D), jnp.float32) * xav
        Wq = jax.random.normal(ks[3], (D, D), jnp.float32) * xav
        bq = jnp.zeros((D,), jnp.float32)
        Wv = jax.random.normal(ks[4], (D, D), jnp.float32) * xav
        bv = jnp.zeros((D,), jnp.float32)
        H = (jax.random.uniform(ks[7], (N, N)) < H_DENSITY).astype(jnp.float32)
        return {'X': X, 'W': W, 'Theta': Theta, 'Wq': Wq, 'bq': bq, 'Wv': Wv, 'bv': bv, 'H': H}
    _L0_gnn_all = _L0_gnn_setup()
    _L0_gnn_in = {k: v for k, v in _L0_gnn_all.items() if k in ('W', 'Theta', 'Wq', 'bq', 'Wv', 'bv')}
    del _L0_gnn_all
    return {'x': x, 'adj': adj, 'L0_gnn_W': _L0_gnn_in['W'], 'L0_gnn_Theta': _L0_gnn_in['Theta'], 'L0_gnn_Wq': _L0_gnn_in['Wq'], 'L0_gnn_bq': _L0_gnn_in['bq'], 'L0_gnn_Wv': _L0_gnn_in['Wv'], 'L0_gnn_bv': _L0_gnn_in['bv']}

def reference(x, adj, L0_gnn_W, L0_gnn_Theta, L0_gnn_Wq, L0_gnn_bq, L0_gnn_Wv, L0_gnn_bv):
    import jax
    import jax.numpy as jnp

    def _L0_gnn_ref(X, W, Theta, Wq, bq, Wv, bv, H):
        import jax, jax.numpy as jnp
        import numpy as np
        N = 2048
        D = 64
        NUM_LAYERS = 2
        THETA0 = 0.000244
        THETA_MAX = 0.0003
        LAM = 0.1
        TAU = 1.0
        EPS = 1e-06
        H_DENSITY = 0.005

        def _safe_norm(x, axis):
            return jnp.sqrt(jnp.maximum(jnp.sum(x * x, axis=axis), 1e-16))

        def _layer(x, H, W, Theta, Wq, bq, Wv, bv, iteration):
            scale = D ** (-0.5)
            theta_base = THETA0 + (1.0 - np.exp(-LAM * iteration)) * (THETA_MAX - THETA0)
            th_comp = theta_base
            th_edge = min(theta_base, 0.8)
            th_node = min(theta_base, 0.7)
            structural = _safe_norm(x @ W, axis=1)
            Q = x @ Wq + bq
            V = x @ Wv + bv
            edge_feat = H.T @ V
            att = Q @ edge_feat.T * scale * H
            att = jax.nn.softmax(att, axis=1)
            att_scores = att.mean(axis=0)
            importance = 0.5 * structural + 0.5 * att_scores
            comp_scores = jax.nn.softmax(importance / TAU)
            comp_mask = comp_scores >= th_comp
            x_comp = x * comp_mask[:, None]
            nrm = jnp.maximum(_safe_norm(x_comp, axis=1), 1e-08)
            xn = x_comp / nrm[:, None]
            cos = xn @ xn.T
            edge_scores = jax.nn.softmax(cos * H / TAU, axis=1)
            edge_mask = (edge_scores >= th_edge) & comp_mask[:, None]
            H_pruned = H * edge_mask
            connectivity = H_pruned.sum(axis=1)
            feat_mag = _safe_norm(x_comp, axis=1)
            node_scores = jax.nn.softmax(connectivity * feat_mag / TAU)
            connected = (H_pruned * edge_mask).sum(axis=1) > 0
            node_mask = (node_scores >= th_node) & connected
            x_final = x_comp * node_mask[:, None]
            vdeg = jnp.maximum(H_pruned.sum(axis=1), EPS)
            edeg = jnp.maximum(H_pruned.sum(axis=0), EPS)
            dv_isqrt = 1.0 / jnp.sqrt(vdeg)
            de_inv = 1.0 / edeg
            transformed = x_final @ W
            agg = H_pruned.T * dv_isqrt[None, :] @ transformed
            agg = agg * de_inv[:, None]
            msg = dv_isqrt[:, None] * (H_pruned @ agg)
            msg = msg @ Theta
            return jax.nn.relu(msg)
        x = X
        for it in range(NUM_LAYERS):
            x = _layer(x, H, W, Theta, Wq, bq, Wv, bv, it)
        return x
    h = jnp.maximum(_layernorm(x, axis=-1), 0.0)
    x = x + _L0_gnn_ref(h, L0_gnn_W, L0_gnn_Theta, L0_gnn_Wq, L0_gnn_bq, L0_gnn_Wv, L0_gnn_bv, adj)
    return x

_drawn_inputs = setup_inputs


def setup_inputs(seed=0):
    import zlib

    import numpy as np

    out = dict(_drawn_inputs(seed))
    spreads = {'L0_gnn_bq': (0.0, 0.1), 'L0_gnn_bv': (0.0, 0.1)}
    factors = {'adj': 4.04, 'L0_gnn_W': 3.762, 'L0_gnn_Theta': 3.667}
    for name, (base, spread) in spreads.items():
        noise = np.random.default_rng([zlib.crc32(name.encode()), seed]).standard_normal(out[name].shape)
        drawn = base * np.exp(spread * noise) if base else spread * noise
        out[name] = jnp.asarray(drawn.astype(out[name].dtype))
    for name, factor in factors.items():
        out[name] = (out[name] * factor).astype(out[name].dtype)
    return out
```

```python
from contextlib import ExitStack

import concourse.bass as bass
from concourse import mybir

ALU = mybir.AluOpType
ACT = mybir.ActivationFunctionType
F32 = mybir.dt.float32
BF16 = mybir.dt.bfloat16
FP8 = mybir.dt.float8e4
U8 = mybir.dt.uint8
I32 = mybir.dt.int32
AX_X = mybir.AxisListType.X
RMAX = bass.bass_isa.ReduceOp.max
RADD = bass.bass_isa.ReduceOp.add
ds = bass.ds

P = 128
UNROLL = 4
LN_EPS = 1e-5
DEG_EPS = 1e-6
NORM_FLOOR = 1e-16
NORM_MIN = 1e-8
THRESHOLDS = (0.000244, 0.000244 + (1.0 - 2.718281828459045 ** -0.1) * (0.0003 - 0.000244))
NEVER = 1e30
DVE_STEPS = 91
EDGE_BYTE = 64.0
EDGE_FP8 = 2.0
NO_EDGE = 255.0
LEAST_VALUE, MOST_VALUE = 0.5, 1e9


class Tile:

    def __init__(self, first, q):
        self.first, self.q = first, q
        self.t = first + UNROLL * q

    def div(self, n):
        return self.first // n + (UNROLL // n) * self.q

    def mod(self, n):
        return self.first % n


def alone(eng, passed):
    eng.sem_inc(passed, 1)


def tiles(eng, first, last, body, passed):
    turns = (last - first) // UNROLL
    if turns > 0:
        alone(eng, passed)
        with eng.Fori(0, turns) as q:
            for i in range(UNROLL):
                body(Tile(first + i, q))
    for i in range(first + turns * UNROLL, last):
        body(Tile(i, 0))


class Order:

    def __init__(self, eng, sem, base=0):
        self.eng, self.sem, self.base, self.n = eng, sem, base, 0

    def __call__(self, instruction):
        instruction.then_inc(self.sem, 1)
        self.n += 1
        self.eng.wait_ge(self.sem, self.base + self.n)


def gnn_kernel(nc, x, adj, W, Theta, Wq, bq, Wv, bv, out):
    N, D = x.shape
    NT = N // P
    HALF = N // 2
    JB = HALF // P
    NC = 4
    CW = N // NC
    BANK = 512
    D3 = 3 * D
    DS = D3 + 1
    LAYERS = len(THRESHOLDS)
    WORDS = N // 4
    WG = WORDS // P
    assert D == 64 and NT % UNROLL == 0 and JB * 256 == 8 * BANK

    with ExitStack() as ctx:
        def sb(name, shape, dt):
            return ctx.enter_context(nc.sbuf_tensor(name, shape, dt))

        def sem(name):
            return ctx.enter_context(nc.semaphore(name))

        edges_d = nc.dram_tensor("edges_d", (NT, P, N), U8).ap()
        gaps_d = nc.dram_tensor("gaps_d", (NT, P, N), U8).ap()
        pruned_d = nc.dram_tensor("pruned_d", (NT, P, N), U8).ap()
        prunedT_d = nc.dram_tensor("prunedT_d", (NT, P, N), U8).ap()
        prunedf_d = nc.dram_tensor("prunedf_d", (NT, P, N), F32).ap()
        adj_t = adj.rearrange("(t p) n -> t p n", p=P)

        logits = sb("logits", [P, 2, N], F32)
        expo = sb("expo", [P, 2, N], F32)
        rs_buf = sb("rs_buf", [P, NT * 6 * D], BF16)
        stat = sb("stat", [P, NT, 3, P], BF16)
        xcur = sb("xcur", [P, NT, D], F32)
        ywt = sb("ywt", [P, NT, D], F32)
        parts = sb("parts", [P, NT, 4 * D], BF16)
        parts2 = sb("parts2", [P, NT, 4 * D], BF16)
        slots = sb("slots", [P, UNROLL, N], U8)
        pr = sb("pr", [P, 2, N], U8)
        prT = sb("prT", [P, 2, N], U8)
        staged = sb("staged", [P, UNROLL, 4 * D], BF16)
        ident_f = sb("ident_f", [P, P], F32)
        ident_b = sb("ident_b", [P, P], BF16)
        zeros = sb("zeros", [P, BANK], BF16)
        half_ones = sb("half_ones", [P, P], BF16)
        neg_ones = sb("neg_ones", [P, P], BF16)
        ones_c = sb("ones_c", [P, 1], F32)
        edge_c = sb("edge_c", [P, 1], F32)
        w_all = sb("w_all", [D + 1, 4 * D], F32)
        wT = sb("wT", [D, D], F32)
        theta_s = sb("theta_s", [D, D], F32)
        value = sb("value", [P, 4], F32)
        flag = sb("flag", [P, 1], I32)
        th_all = sb("th_all", [P, LAYERS], F32)
        th_cur = sb("th_cur", [P, 1], F32)
        gsc = sb("gsc", [P, 4], F32)
        mx = sb("mx", [P, 2, NC], F32)
        nmx = sb("nmx", [P, 2], F32)
        emx = sb("emx", [P, 2], F32)
        rsum = sb("rsum", [P, 2], F32)
        rinv = sb("rinv", [P, 2], F32)
        thr = sb("thr", [P, 2], F32)
        msum = sb("msum", [P, 2, D], F32)
        halfst = sb("halfst", [P, NT], F32)
        xsq = sb("xsq", [P, NT], F32)
        imp = sb("imp", [P, NT], F32)
        ex = sb("ex", [P, NT], F32)
        cmask = sb("cmask", [P, NT], F32)
        never = sb("never", [P, NT], F32)
        fmag = sb("fmag", [P, NT], F32)
        rnrm = sb("rnrm", [P, NT], F32)
        conn = sb("conn", [P, NT], F32)
        dvs = sb("dvs", [P, NT], F32)
        dvout = sb("dvout", [P, NT], F32)
        nmask = sb("nmask", [P, NT], F32)
        edges_n = sb("edges_n", [P, NT], F32)
        gaps_n = sb("gaps_n", [P, NT], F32)
        zero_bound = sb("zero_bound", [P, NT], F32)
        gap_exp = sb("gap_exp", [P, 2], F32)
        whole_sum = sb("whole_sum", [P, 2], F32)
        fac = sb("fac", [P, JB], F32)
        red = sb("red", [P, 8], F32)

        ps = ctx.enter_context(nc.psum_tensor("ps", [P, 8, BANK], F32))

        tmp = expo[:, :, :].rearrange("p a (b t d) -> p (a b) t d", b=2, d=D)
        rows4 = [logits[:, 0, :], logits[:, 1, :], expo[:, 0, :], expo[:, 1, :]]
        x_all = logits[:, :, :].rearrange("p a (t c) -> p (a t) c", c=4 * D)
        col_row = expo[:, 1, 0:2 * BANK]
        src_st = rs_buf[:, :].rearrange("p (t c) -> p t c", c=6 * D)
        rhs_a = rs_buf[:, 0:N]
        rhs_b = rs_buf[:, N:2 * N]
        xTa = parts2[:, :, :].rearrange("p t c -> p (t c)").bitcast(F32)[0:D + 1, :]
        marks = rs_buf[:, 0:2 * N].rearrange("p (a n) -> p a n", a=2)
        ring_h = slots[:, :, 0:HALF]
        gtile = slots[:, :, :].rearrange("p a n -> p (a n)").bitcast(F32)
        planes = expo[:, 1, :].bitcast(BF16)[:, 0:3 * HALF].rearrange("p (k n) -> p k n", k=3)
        blkT = logits[:, 0, 0:BANK]
        planesT = expo[:, 1, :].bitcast(BF16)[:, 0:3 * BANK].rearrange("p (k n) -> p k n", k=3)


        def many(name, n):
            return [sem(f"{name}{i}") for i in range(n)]

        passed = sem("passed")
        consts = sem("consts")
        tables_in = sem("tables_in")
        value_in = sem("value_in")
        x_in = sem("x_in")
        row_in = many("row_in", UNROLL)
        row_byte = sem("row_byte")
        row_mark = sem("row_mark")
        row_chk = sem("row_chk")
        edges_out = sem("edges_out")
        edges_sent = sem("edges_sent")
        row_count = sem("row_count")
        flag_set = sem("flag_set")
        wtheta_ps = sem("wtheta_ps")
        wtheta_in = sem("wtheta_in")
        ln_sq = sem("ln_sq")
        ln_v = sem("ln_v")
        ln_x = sem("ln_x")
        dve_pre = sem("dve_pre")
        dve_step = sem("dve_step")
        sc_set = sem("sc_set")
        xT_ps = sem("xT_ps")
        xT_even = sem("xT_even")
        xT_odd = sem("xT_odd")
        xT_one = sem("xT_one")
        all_ps = sem("all_ps")
        all_v = sem("all_v")
        all_a = sem("all_a")
        squares = sem("squares")
        parts_ready = sem("parts_ready")
        src_ready = sem("src_ready")
        parts2_ready = sem("parts2_ready")
        staged_in = sem("staged_in")
        half_in = many("half_in", UNROLL)
        half_used = sem("half_used")
        sweep_ps = sem("sweep_ps")
        sweep_read = sem("sweep_read")
        turned = sem("turned")
        turn_v = sem("turn_v")
        turn_a = sem("turn_a")
        full_in = many("full_in", UNROLL)
        qk_ready = sem("qk_ready")
        qk_used = sem("qk_used")
        nmax_ready = sem("nmax_ready")
        exp_done = sem("exp_done")
        rinv_ready = sem("rinv_ready")
        e_used = sem("e_used")
        thr_ready = sem("thr_ready")
        tr_done = sem("tr_done")
        ev_done = sem("ev_done")
        count_ps = sem("count_ps")
        count_read = sem("count_read")
        gaps_a = sem("gaps_a")
        gaps_v = sem("gaps_v")
        gaps_out = sem("gaps_out")
        gaps_sent = sem("gaps_sent")
        sum_ready = sem("sum_ready")
        max_ready = sem("max_ready")
        pr_out = sem("pr_out")
        pr_sent = sem("pr_sent")
        prT_out = sem("prT_out")
        prT_sent = sem("prT_sent")
        col_read = sem("col_read")
        att_ps = sem("att_ps")
        red_in = sem("red_in")
        red_out = sem("red_out")
        sm_in = sem("sm_in")
        sm_out = sem("sm_out")
        root_in = sem("root_in")
        root_out = sem("root_out")
        turned_in = many("turned_in", UNROLL)
        e_tile = sem("e_tile")
        msg_sum = sem("msg_sum")
        msg_out = sem("msg_out")
        x_again = sem("x_again")
        y_ready = sem("y_ready")
        y_out = sem("y_out")
        g_half_in = many("g_half_in", 2)
        g_half_free = sem("g_half_free")
        g_step = sem("g_step")
        g_step_t = sem("g_step_t")
        g_planes = sem("g_planes")
        g_full_in = sem("g_full_in")
        g_turned = sem("g_turned")
        g_split = sem("g_split")

        SC_B, SC_C, SC_D = 0, 1, 2

        block = ctx.enter_context(nc.Block())

        def loop(eng, first, last, body):
            tiles(eng, first, last, body, passed)

        def dtile(dram, T):
            return dram[ds(T.t, 1), :, :].rearrange("a p n -> (a p) n")

        def dhalf(dram, T, h):
            return dram[ds(T.t, 1), :, h * HALF:(h + 1) * HALF].rearrange("a p n -> (a p) n")

        def node(a, T):
            return a[:, ds(T.t, 1)]

        def paths(eng, layer):
            eng.wait_ge(flag_set, 1)
            fast = eng.value_load(flag[0:1, 0:1], min_val=0, max_val=1)
            with eng.If(fast == 1):
                with eng.Fori(0, LAYERS) as lay:
                    layer(True, lay)
            with eng.Else():
                with eng.Fori(0, LAYERS) as lay:
                    layer(False, lay)

        @block.sync
        def _(sp):
            with nc.allow_non_contiguous_dma(reason="small tables"):
                sp.dma_start(value[:, 0:1], adj[0:1, 0:1].to_broadcast([P, 1])).then_inc(value_in, 16)
            def row(T):
                i = T.mod(UNROLL)
                sp.wait_ge(row_mark, T.t + 1)
                alone(sp, passed)
                sp.dma_start(rows4[i], dtile(adj_t, T)).then_inc(row_in[i], 16)
            loop(sp, 0, NT, row)

            def layer(fast, lay):
                halves = lay * (4 * NT)
                fulls = lay * (2 * NT)

                def half_sweeps(source, phase):
                    for h in range(2):
                        def half(T, h=h):
                            n = halves + (2 * phase + h) * NT + T.t
                            if fast:
                                sp.wait_ge(half_used, n + 1)
                                alone(sp, passed)
                                i = T.mod(UNROLL)
                                sp.dma_start(ring_h[:, i, :], dhalf(source, T, h)).then_inc(half_in[i], 16)
                            else:
                                sp.wait_ge(g_half_free, n + 1)
                                alone(sp, passed)
                                i = T.mod(2)
                                sp.dma_start(gtile[:, i * HALF:(i + 1) * HALF],
                                             dhalf(source, T, h)).then_inc(g_half_in[i], 16)
                        loop(sp, 0, NT, half)

                def whole(source, wait, into, signals):
                    def one(T):
                        wait(T)
                        alone(sp, passed)
                        i = T.mod(UNROLL) if fast else 0
                        sp.dma_start(into(i), dtile(source, T)).then_inc(signals[i], 16)
                    loop(sp, 0, NT, one)

                def slot(i):
                    return slots[:, i, :] if fast else gtile

                sp.wait_ge(edges_sent, NT + UNROLL)
                sp.wait_ge(e_tile, lay * NT + UNROLL)
                alone(sp, passed)
                half_sweeps(edges_d if fast else adj_t, 0)

                sp.wait_ge(half_used, halves + 2 * NT + UNROLL)

                def slot_masked(T):
                    sp.wait_ge(nmax_ready, fulls + T.t + (1 if fast else UNROLL))
                    if fast:
                        sp.wait_ge(gaps_a, lay * NT + T.t + 1)
                        sp.wait_ge(gaps_v, lay * NT + T.t + 1)
                whole(edges_d if fast else adj_t, slot_masked,
                      slot, full_in if fast else [g_full_in])
                sp.wait_ge(nmax_ready, fulls + NT + UNROLL)
                if fast:
                    sp.wait_ge(gaps_sent, (lay + 1) * NT + 2)
                    alone(sp, passed)
                whole(gaps_d if fast else adj_t,
                      lambda T: (sp.wait_ge(nmax_ready, fulls + NT + T.t + 1) if fast else
                                 sp.wait_ge(e_used, fulls + NT + T.t + 2)),
                      slot, full_in if fast else [g_full_in])

                sp.wait_ge(e_used, fulls + 2 * NT + 2)
                sp.wait_ge(pr_sent, (lay + 1) * NT + 2)
                alone(sp, passed)
                half_sweeps(pruned_d if fast else prunedf_d, 1)

                sp.wait_ge(half_used, halves + 4 * NT + UNROLL)
                if fast:
                    sp.wait_ge(prT_sent, (lay + 1) * NT + 2)
                    alone(sp, passed)
                whole(prunedT_d if fast else prunedf_d,
                      lambda T: sp.wait_ge(e_tile, lay * NT + T.t + (1 if fast else UNROLL)),
                      slot, turned_in if fast else [g_full_in])

            paths(sp, layer)
            sp.wait_ge(msg_out, LAYERS * NT + 2)
            with nc.allow_non_contiguous_dma(reason="rows of 256 bytes"):
                sp.dma_start(tmp[:, 0], x.rearrange("(t p) d -> p t d", p=P)).then_inc(x_again, 16)
                sp.wait_ge(y_ready, 1)
                sp.dma_start(out.rearrange("(t p) d -> p t d", p=P), tmp[:, 1]).then_inc(y_out, 16)
            sp.wait_ge(y_out, 16)

        @block.gpsimd
        def _(pool):
            for s, n in ((row_mark, UNROLL), (row_chk, 2), (half_used, UNROLL), (turn_v, 2), (turn_a, 2),
                         (qk_used, 2), (nmax_ready, UNROLL), (exp_done, 2), (e_used, 2), (tr_done, 2),
                         (ev_done, 1), (e_tile, UNROLL), (msg_sum, UNROLL), (msg_out, 2), (g_half_free, 2),
                         (edges_sent, UNROLL), (row_count, UNROLL), (count_ps, 2), (count_read, 2),
                         (gaps_a, UNROLL), (gaps_v, UNROLL),
                         (gaps_sent, 2), (pr_sent, 2), (prT_sent, 2)):
                pool.sem_inc(s, n)
            nc.gpsimd.memset(w_all[:, :], 0.0).then_inc(consts, 1)
            nc.gpsimd.memset(ident_f[:, :], 0.0).then_inc(consts, 1)
            nc.gpsimd.memset(zeros[:, :], 0.0).then_inc(consts, 1)
            nc.gpsimd.memset(half_ones[:, :], 1.0 / EDGE_FP8).then_inc(consts, 1)
            nc.gpsimd.memset(neg_ones[:, :], -1.0).then_inc(consts, 1)
            nc.gpsimd.memset(ones_c[:, :], 1.0).then_inc(consts, 1)
            nc.gpsimd.memset(edge_c[:, :], EDGE_BYTE).then_inc(consts, 1)
            for n, th in enumerate(THRESHOLDS):
                nc.gpsimd.memset(th_all[:, n:n + 1], th).then_inc(consts, 1)
            nc.gpsimd.memset(parts[:, :, :], 1.0).then_inc(consts, 1)
            pool.wait_ge(consts, 8 + LAYERS)
            nc.gpsimd.affine_select(out=ident_f[:, :], in_=ident_f[:, :], compare_op=ALU.not_equal, fill=1.0,
                                    base=0, pattern=[[-1, P]], channel_multiplier=1).then_inc(consts, 1)
            pool.wait_ge(consts, 9 + LAYERS)
            nc.gpsimd.tensor_copy(ident_b[:, :], ident_f[:, :]).then_inc(consts, 1)

            with nc.allow_non_contiguous_dma(reason="small tables"):
                for dst, src in ((w_all[0:D, 0:D], W), (w_all[0:D, D:2 * D], Wv), (w_all[0:D, 2 * D:3 * D], Wq),
                                 (w_all[D:D + 1, D:2 * D], bv.rearrange("(a d) -> a d", a=1)),
                                 (w_all[D:D + 1, 2 * D:3 * D], bq.rearrange("(a d) -> a d", a=1)),
                                 (theta_s[:, :], Theta), (wT[:, :], W.rearrange("a b -> b a"))):
                    nc.gpsimd.dma_start(dst, src).then_inc(tables_in, 16)
                nc.gpsimd.dma_start(xcur[:, :, :], x.rearrange("(t p) d -> p t d", p=P)).then_inc(x_in, 16)

            def store_edges(T):
                pool.wait_ge(row_byte, T.t + 1)
                alone(pool, passed)
                i = T.mod(UNROLL)
                nc.gpsimd.dma_start(dtile(edges_d, T), slots[:, i, :]).then_inc(edges_out, 16)
                pool.wait_ge(edges_out, 16 * (T.t + 1))
                pool.sem_inc(edges_sent, 1)
            loop(pool, 0, NT, store_edges)

            def layer(fast, lay):
                halves = lay * (4 * NT)
                fulls = lay * (2 * NT)

                def stage(phase):
                    pool.wait_ge(parts_ready, 2 * lay + phase + 1)
                    alone(pool, passed)
                    for h in range(2):
                        def one(T, h=h):
                            n = halves + (2 * phase + h) * NT + T.t
                            pool.wait_ge(half_used, n + 1)
                            alone(pool, passed)
                            nc.gpsimd.tensor_copy(staged[:, T.mod(UNROLL), 0:DS],
                                                  parts[:, ds(T.t, 1), 0:DS].rearrange("p a c -> p (a c)")
                                                  ).then_inc(staged_in, 1)
                        loop(pool, 0, NT, one)

                def reduce_over_partitions(n, op):
                    pool.wait_ge(red_in, 4 * lay + n + 1)
                    alone(pool, passed)
                    nc.gpsimd.partition_all_reduce(red[:, 4 + n:5 + n], red[:, n:n + 1], P, op).then_inc(red_out, 1)

                pool.wait_ge(xT_ps, lay + 1)
                alone(pool, passed)
                nc.gpsimd.memset(xTa[D:D + 1, :], 1.0).then_inc(xT_one, 1)
                stage(0)
                if fast:
                    def store_gaps(T):
                        pool.wait_ge(gaps_a, lay * NT + T.t + 1 + UNROLL)
                        pool.wait_ge(gaps_v, lay * NT + T.t + 1 + UNROLL)
                        alone(pool, passed)
                        nc.gpsimd.dma_start(dtile(gaps_d, T), pr[:, T.mod(2), :]).then_inc(gaps_out, 16)
                        pool.wait_ge(gaps_out, 16 * (lay * NT + T.t + 1))
                        pool.sem_inc(gaps_sent, 1)
                    loop(pool, 0, NT, store_gaps)
                reduce_over_partitions(0, RMAX)
                reduce_over_partitions(1, RADD)

                def store(T):
                    i = T.mod(2)
                    pool.wait_ge(e_used, fulls + NT + T.t + 3)
                    alone(pool, passed)
                    if fast:
                        nc.gpsimd.dma_start(dtile(pruned_d, T), pr[:, i, :]).then_inc(pr_out, 16)
                    else:
                        nc.gpsimd.dma_start(dtile(prunedf_d, T), logits[:, i, :]).then_inc(pr_out, 16)
                    pool.wait_ge(pr_out, 16 * (lay * NT + T.t + 1))
                    pool.sem_inc(pr_sent, 1)
                    if fast:
                        pool.wait_ge(ev_done, lay * NT + T.t + 2)
                        alone(pool, passed)
                        nc.gpsimd.dma_start(dtile(prunedT_d, T), prT[:, i, :]).then_inc(prT_out, 16)
                        pool.wait_ge(prT_out, 16 * (lay * NT + T.t + 1))
                        pool.sem_inc(prT_sent, 1)
                loop(pool, 0, NT, store)

                reduce_over_partitions(2, RMAX)
                reduce_over_partitions(3, RADD)
                stage(1)

            paths(pool, layer)

        @block.scalar
        def _(act):
            act.wait_ge(ln_v, 1)
            nc.scalar.activation(ywt[:, :, :], xcur[:, :, :], ACT.Square).then_inc(ln_sq, 1)
            act.wait_ge(ln_v, 2)
            nc.scalar.activation(xsq[:, :], xsq[:, :], ACT.Sqrt).then_inc(ln_sq, 1)

            def count_edges(T):
                act.wait_ge(row_byte, T.t + 1)
                act.wait_ge(row_count, T.t + 3)
                nc.scalar.activation(prT[:, T.mod(2), :], slots[:, T.mod(UNROLL), :], ACT.Copy,
                                     accum_out=node(edges_n, T)).then_inc(row_count, 1)
            loop(act, 0, NT, count_edges)

            def layer(fast, lay):
                fulls = lay * (2 * NT)
                turns = lay * 40

                def copy_turned(first, dests):
                    for m, dest in enumerate(dests):
                        def one(T, m=m, dest=dest):
                            if T.mod(2) == 0:
                                return
                            act.wait_ge(turned, 2 * turns + first + 8 * m + T.t + 1)
                            nc.scalar.copy(dest(T), ps[:, T.mod(4), :].rearrange("p (a c) -> p a c", c=P)
                                           ).then_inc(turn_a, 1)
                        loop(act, 0, NT // 4, one)

                act.wait_ge(xT_ps, lay + 1)
                nc.scalar.copy(xTa[0:D, :].rearrange("p (a two c) -> p a two c", two=2, c=P)[:, :, 1, :],
                               ps[D:P, 0:4, :].rearrange("p b (a c) -> p (b a) c", c=P)).then_inc(xT_odd, 1)
                for r in range(2):
                    for b in range(1, 8, 2):
                        act.wait_ge(all_ps, 16 * lay + 8 * r + b + 1)
                        nc.scalar.copy(x_all[:, 16 * r + 2 * b:16 * r + 2 * b + 2, :],
                                       ps[:, b, :].rearrange("p (a c) -> p a c", a=2)).then_inc(all_a, 1)
                act.wait_ge(all_v, 8 * (lay + 1))
                act.wait_ge(all_a, 8 * (lay + 1))
                nc.scalar.activation(tmp[:, 2], x_all[:, :, 0:D], ACT.Square).then_inc(squares, 1)
                nc.scalar.activation(tmp[:, 3], xcur[:, :, :], ACT.Square).then_inc(squares, 1)

                def root(n, dst, src):
                    act.wait_ge(root_in, 3 * lay + n + 1)
                    nc.scalar.activation(dst, src, ACT.Sqrt).then_inc(root_out, 1)

                def node_exp(n):
                    act.wait_ge(sm_in, 2 * lay + n + 1)
                    nc.scalar.activation(ex[:, :], imp[:, :], ACT.Exp, bias=red[:, 4 + 2 * n:5 + 2 * n],
                                         accum_out=red[:, 2 * n + 1:2 * n + 2]).then_inc(sm_out, 1)

                root(0, halfst[:, :], halfst[:, :])
                copy_turned(0, [lambda T, m=m: stat[:, ds(4 * T.t, 4), m, :] for m in range(3)])
                copy_turned(24, [lambda T: rhs_a[:, ds(4 * P * T.t, 4 * P)].rearrange("p (a c) -> p a c", c=P),
                                 lambda T: rhs_b[:, ds(4 * P * T.t, 4 * P)].rearrange("p (a c) -> p a c", c=P)])

                def row_exp(T, phase):
                    i, n = T.mod(2), fulls + phase * NT + T.t
                    act.wait_ge(nmax_ready, n + 1 + UNROLL)
                    act.wait_ge(e_used, n + 1)
                    if fast and phase:
                        nc.scalar.activation(gap_exp[:, i:i + 1], nmx[:, i:i + 1], ACT.Exp)
                    nc.scalar.activation(expo[:, i, :], logits[:, i, :], ACT.Exp, bias=nmx[:, i:i + 1],
                                         accum_out=rsum[:, i:i + 1]).then_inc(exp_done, 1)

                def attention(T):
                    row_exp(T, 0)
                    if fast:
                        act.wait_ge(gaps_sent, lay * NT + T.t + 1)
                        nc.scalar.activation(pr[:, T.mod(2), 0:HALF], slots[:, T.mod(UNROLL), 0:HALF], ACT.Copy,
                                             bias=NO_EDGE, scale=-NO_EDGE / EDGE_BYTE).then_inc(gaps_a, 1)
                loop(act, 0, NT, attention)
                act.wait_ge(e_used, fulls + NT + 2)
                for g in range(4):
                    last = nc.scalar.copy(col_row[32 * g:32 * g + 1, :].rearrange("p (a c) -> p a c", a=2),
                                          ps[32 * g:32 * g + 1, 4:6, :])
                    last.then_inc(col_read, 1)
                node_exp(0)
                root(1, fmag[:, :], fmag[:, :])
                copy_turned(40, [lambda T, m=m: stat[:, ds(4 * T.t, 4), m, :] for m in range(3)])
                copy_turned(64, [lambda T: rhs_a[:, ds(4 * P * T.t, 4 * P)].rearrange("p (a c) -> p a c", c=P),
                                 lambda T: rhs_b[:, ds(4 * P * T.t, 4 * P)].rearrange("p (a c) -> p a c", c=P)])

                def copy_pruned(T, back):
                    i = (T.first - back) % 2
                    t = T.t - back
                    act.wait_ge(tr_done, lay * NT + t + 3)
                    act.wait_ge(prT_sent, lay * NT + t + 1)
                    act.wait_ge(count_ps, lay * NT + t + 1)
                    nc.scalar.copy(prT[:, i, :], ps[:, 6:8, :].rearrange("p a c -> p (a c)").bitcast(U8)
                                   ).then_inc(ev_done, 1)

                if fast:
                    loop(act, 0, 2, lambda T: row_exp(T, 1))

                    def both(T):
                        copy_pruned(T, 2)
                        row_exp(T, 1)
                    loop(act, 2, NT, both)
                    for t in (NT, NT + 1):
                        copy_pruned(Tile(t, 0), 2)
                else:
                    loop(act, 0, NT, lambda T: row_exp(T, 1))
                node_exp(1)
                root(2, dvs[:, :], dvs[:, :])

                def message(T):
                    i = T.mod(2)
                    act.wait_ge(msg_sum, lay * NT + T.t + 1 + UNROLL)
                    nc.scalar.activation(xcur[:, ds(T.t, 1), :].rearrange("p a d -> p (a d)"), msum[:, i, :],
                                         ACT.Relu, scale=node(dvout, T)).then_inc(msg_out, 1)
                loop(act, 0, NT, message)

            paths(act, layer)

        @block.vector
        def _(dve):
            step = Order(dve, dve_pre)

            def per_node(a):
                return a.unsqueeze(2).to_broadcast([P, a.shape[1], D])

            dve.wait_ge(x_in, 16)
            step(nc.vector.tensor_reduce(xsq[:, :], xcur[:, :, :], AX_X, ALU.add))
            step(nc.vector.tensor_scalar(xsq[:, :], xsq[:, :], 1.0 / D, None, ALU.mult))
            nc.vector.tensor_tensor(xcur[:, :, :], xcur[:, :, :], per_node(xsq[:, :]), ALU.subtract).then_inc(ln_v, 1)
            dve.wait_ge(ln_sq, 1)
            step(nc.vector.tensor_reduce(xsq[:, :], ywt[:, :, :], AX_X, ALU.add))
            nc.vector.tensor_scalar(xsq[:, :], xsq[:, :], 1.0 / D, LN_EPS, ALU.mult, ALU.add).then_inc(ln_v, 1)
            dve.wait_ge(ln_sq, 2)
            step(nc.vector.reciprocal(xsq[:, :], xsq[:, :]))
            step(nc.vector.tensor_tensor(xcur[:, :, :], xcur[:, :, :], per_node(xsq[:, :]), ALU.mult))
            nc.vector.tensor_scalar(xcur[:, :, :], xcur[:, :, :], 0.0, None, ALU.max).then_inc(ln_x, 1)
            dve.wait_ge(wtheta_ps, 1)
            nc.vector.tensor_copy(w_all[0:D, 3 * D:4 * D], ps[0:D, 0, 0:D]).then_inc(wtheta_in, 1)

            dve.wait_ge(value_in, 16)

            def edge_bytes(T):
                i = T.mod(UNROLL)
                dve.wait_ge(row_in[i], 16 * (T.div(UNROLL) + 1))
                dve.wait_ge(row_chk, T.t + 1)
                dve.wait_ge(edges_sent, T.t + 1)
                dve.wait_ge(row_count, T.t + 1)
                nc.vector.tensor_scalar(slots[:, i, :], rows4[i], value[:, 0:1], EDGE_BYTE,
                                        ALU.is_equal, ALU.mult).then_inc(row_byte, 1)
                nc.vector.tensor_scalar(marks[:, T.mod(2), :], rows4[i], 0.0, None,
                                        ALU.not_equal).then_inc(row_mark, 1)
            loop(dve, 0, NT, edge_bytes)
            dve.wait_ge(row_chk, NT + 2)
            dve.wait_ge(row_count, NT + UNROLL)
            step(nc.vector.tensor_scalar(gaps_n[:, :], edges_n[:, :], -1.0 / EDGE_BYTE, float(N), ALU.mult, ALU.add))
            step(nc.vector.tensor_scalar(zero_bound[:, :], gaps_n[:, :], 0.0, 3.0e38, ALU.is_equal, ALU.mult))
            step(nc.vector.tensor_reduce(value[:, 1:2], ps[:, :, :].rearrange("p a c -> p (a c)"), AX_X, ALU.min))
            step(nc.vector.tensor_scalar(value[:, 1:2], value[:, 1:2], 0.0, None, ALU.is_equal))
            step(nc.vector.tensor_scalar(value[:, 2:3], value[:, 0:1], LEAST_VALUE, None, ALU.is_ge))
            step(nc.vector.tensor_scalar(value[:, 3:4], value[:, 0:1], MOST_VALUE, None, ALU.is_le))
            step(nc.vector.tensor_tensor(value[:, 1:2], value[:, 1:2], value[:, 2:3], ALU.mult))
            step(nc.vector.tensor_tensor(value[:, 1:2], value[:, 1:2], value[:, 3:4], ALU.mult))
            step(nc.vector.tensor_copy(th_cur[:, :], th_all[:, 0:1]))
            nc.vector.tensor_copy(flag[:, :], value[:, 1:2]).then_inc(flag_set, 1)

            def layer(fast, lay):
                fulls = lay * (2 * NT)
                halves = lay * (4 * NT)
                turns = lay * 40
                step = Order(dve, dve_step, lay * DVE_STEPS)

                def split(src, first, second, third, rest):
                    step(nc.vector.tensor_copy(first, src))
                    step(nc.vector.tensor_tensor(rest, src, first, ALU.subtract))
                    step(nc.vector.tensor_copy(second, rest))
                    step(nc.vector.tensor_tensor(rest, rest, second, ALU.subtract))
                    step(nc.vector.tensor_copy(third, rest))

                def split_left(src):
                    def part(n):
                        return src_st[:, :, n * D:(n + 1) * D]
                    split(src, part(0), part(2), part(5), tmp[:, 0])
                    step(nc.vector.tensor_copy(part(1), part(0)))
                    step(nc.vector.tensor_copy(part(3), part(2)))
                    step(nc.vector.tensor_copy(part(4), part(0)))

                def copy_turned(first, dests):
                    for m, dest in enumerate(dests):
                        def one(T, m=m, dest=dest):
                            if T.mod(2):
                                return
                            dve.wait_ge(turned, 2 * turns + first + 8 * m + T.t + 1)
                            nc.vector.tensor_copy(dest(T), ps[:, T.mod(4), :].rearrange("p (a c) -> p a c", c=P)
                                                  ).then_inc(turn_v, 1)
                        loop(dve, 0, NT // 4, one)

                def to_stat(m):
                    return lambda T: stat[:, ds(4 * T.t, 4), m, :]

                def to_rhs(rhs):
                    return lambda T: rhs[:, ds(4 * P * T.t, 4 * P)].rearrange("p (a c) -> p a c", c=P)

                def planes_of(phase, h):
                    def one(T):
                        k = (2 * phase + h) * NT
                        n = halves + k + T.t
                        i = T.mod(2)
                        g = gtile[:, i * HALF:(i + 1) * HALF]
                        own = Order(dve, g_step, 4 * n)
                        dve.wait_ge(g_half_in[i], 16 * (lay * (2 * NT) + k // 2 + T.div(2) + 1))
                        dve.wait_ge(half_used, n + UNROLL)
                        own(nc.vector.tensor_copy(planes[:, 0, :], g))
                        own(nc.vector.tensor_tensor(g, g, planes[:, 0, :], ALU.subtract))
                        own(nc.vector.tensor_copy(planes[:, 1, :], g))
                        own(nc.vector.tensor_tensor(g, g, planes[:, 1, :], ALU.subtract))
                        nc.vector.tensor_copy(planes[:, 2, :], g).then_inc(g_planes, 1)
                        dve.wait_ge(g_planes, n + 1)
                        dve.sem_inc(g_half_free, 1)
                    loop(dve, 0, NT, one)

                def sums_of_sweep(phase, h, dst):
                    dve.wait_ge(sweep_ps, 4 * lay + 2 * phase + h + 1)
                    blocks = ps[:, :, :].rearrange("p b (u c) -> p (b u) c", u=2)
                    if phase:
                        step(nc.vector.tensor_scalar(fac[:, :], blocks[:, :, D3], gsc[:, SC_D:SC_D + 1], DEG_EPS,
                                                     ALU.mult, ALU.max))
                    nc.vector.tensor_reduce(dst, blocks[:, :, 0:D3].rearrange("p b (k d) -> p b d k", k=3),
                                            AX_X, ALU.add).then_inc(sweep_read, 1)
                    dve.wait_ge(sweep_read, 4 * lay + 2 * phase + h + 1)
                    if phase:
                        step(nc.vector.reciprocal(fac[:, :], fac[:, :]))
                        step(nc.vector.tensor_scalar(fac[:, :], fac[:, :], gsc[:, SC_D:SC_D + 1], None, ALU.mult))
                        step(nc.vector.tensor_tensor(dst, dst, per_node(fac[:, :]), ALU.mult))

                def norm_root(n, a):
                    nc.vector.tensor_scalar(a, a, NORM_FLOOR if n < 2 else DEG_EPS, None,
                                            ALU.max).then_inc(root_in, 1)
                    dve.wait_ge(root_out, 3 * lay + n + 1)

                def node_softmax(n):
                    nc.vector.tensor_reduce(red[:, 2 * n:2 * n + 1], imp[:, :], AX_X, ALU.max).then_inc(red_in, 1)
                    dve.wait_ge(red_out, 4 * lay + 2 * n + 1)
                    nc.vector.tensor_scalar(red[:, 4 + 2 * n:5 + 2 * n], red[:, 4 + 2 * n:5 + 2 * n], -1.0, None,
                                            ALU.mult).then_inc(sm_in, 1)
                    dve.wait_ge(sm_out, 2 * lay + n + 1)
                    dve.sem_inc(red_in, 1)
                    dve.wait_ge(red_out, 4 * lay + 2 * n + 2)
                    step(nc.vector.tensor_tensor(red[:, 5 + 2 * n:6 + 2 * n], red[:, 5 + 2 * n:6 + 2 * n],
                                                 th_cur[:, :], ALU.mult))
                    return red[:, 5 + 2 * n:6 + 2 * n]

                if fast:
                    step(nc.vector.tensor_tensor(gsc[:, SC_B:SC_B + 1], value[:, 0:1], value[:, 0:1], ALU.mult))
                    step(nc.vector.tensor_scalar(gsc[:, SC_B:SC_B + 1], gsc[:, SC_B:SC_B + 1],
                                                 D ** -0.5 / EDGE_BYTE / EDGE_FP8, None, ALU.mult))
                    step(nc.vector.tensor_scalar(gsc[:, SC_C:SC_C + 1], value[:, 0:1], 1.0 / EDGE_BYTE, None,
                                                 ALU.mult))
                    step(nc.vector.tensor_scalar(gsc[:, SC_D:SC_D + 1], value[:, 0:1], 1.0 / EDGE_FP8, None,
                                                 ALU.mult))
                else:
                    step(nc.vector.memset(gsc[:, SC_B:SC_B + 1], D ** -0.5))
                    step(nc.vector.memset(gsc[:, SC_C:SC_C + 1], 1.0))
                    step(nc.vector.memset(gsc[:, SC_D:SC_D + 1], 1.0))
                    step(nc.vector.memset(gsc[:, 3:4], 1.0))

                dve.wait_ge(xT_ps, lay + 1)
                nc.vector.tensor_copy(xTa[0:D, :].rearrange("p (a two c) -> p a two c", two=2, c=P)[:, :, 0, :],
                                      ps[0:D, 0:4, :].rearrange("p b (a c) -> p (b a) c", c=P)).then_inc(xT_even, 1)
                for r in range(2):
                    for b in range(0, 8, 2):
                        dve.wait_ge(all_ps, 16 * lay + 8 * r + b + 1)
                        nc.vector.tensor_copy(x_all[:, 16 * r + 2 * b:16 * r + 2 * b + 2, :],
                                              ps[:, b, :].rearrange("p (a c) -> p a c", a=2)).then_inc(all_v, 1)
                dve.wait_ge(all_v, 8 * (lay + 1))
                dve.wait_ge(all_a, 8 * (lay + 1))
                split(x_all[:, :, D:2 * D], parts[:, :, 0:D], parts[:, :, D:2 * D], parts[:, :, 2 * D:D3], tmp[:, 0])
                dve.sem_inc(parts_ready, 1)
                dve.wait_ge(squares, 2 * lay + 2)
                step(nc.vector.tensor_reduce(halfst[:, :], tmp[:, 2], AX_X, ALU.add))
                step(nc.vector.tensor_reduce(xsq[:, :], tmp[:, 3], AX_X, ALU.add))
                norm_root(0, halfst[:, :])
                step(nc.vector.tensor_scalar(halfst[:, :], halfst[:, :], 0.5, None, ALU.mult))
                step(nc.vector.tensor_copy(ywt[:, :, :], x_all[:, :, 3 * D:4 * D]))
                split_left(x_all[:, :, 2 * D:3 * D])
                dve.sem_inc(src_ready, 1)

                def to_parts2(h, cols):
                    return parts2[:, h * JB:(h + 1) * JB, cols * D:(cols + 1) * D]
                for h in range(2):
                    if not fast:
                        planes_of(0, h)
                    sums_of_sweep(0, h, tmp[:, 1, 0:JB, :])
                    split(tmp[:, 1, 0:JB, :], to_parts2(h, 0), to_parts2(h, 1), to_parts2(h, 2), tmp[:, 0, 0:JB, :])
                    step(nc.vector.tensor_copy(to_parts2(h, 3), to_parts2(h, 0)))
                dve.sem_inc(parts2_ready, 1)
                copy_turned(0, [to_stat(m) for m in range(3)])
                copy_turned(24, [to_rhs(rhs_a), to_rhs(rhs_b)])

                def adjacency(T):
                    return slots[:, T.mod(UNROLL), :] if fast else gtile

                def mask_rows(T, phase):
                    i, k = T.mod(2), phase * NT
                    factor = value[:, 0:1] if fast and phase else gsc[:, phase:phase + 1]
                    if fast:
                        dve.wait_ge(full_in[T.mod(UNROLL)], 16 * (lay * (2 * NT // UNROLL) + k // UNROLL + T.div(UNROLL) + 1))
                    else:
                        dve.wait_ge(g_full_in, 16 * (lay * (3 * NT) + k + T.t + 1))
                        if phase:
                            dve.wait_ge(pr_sent, lay * NT + T.t + 1)
                    dve.wait_ge(exp_done, fulls + k + T.t + 1)
                    for c in range(NC):
                        n = NC * (fulls + k + T.t) + c
                        dve.wait_ge(qk_ready, n + 1)
                        alone(dve, passed)
                        nc.vector.tensor_tensor_reduce(
                            logits[:, i, c * CW:(c + 1) * CW],
                            ps[:, 2 * (c % 2):2 * (c % 2) + 2, :].rearrange("p a n -> p (a n)"),
                            adjacency(T)[:, c * CW:(c + 1) * CW], factor, -3.0e38,
                            ALU.subtract if fast and phase else ALU.mult, ALU.max, mx[:, i, c:c + 1]).then_inc(qk_used, 1)
                    dve.wait_ge(qk_used, NC * (fulls + k + T.t + 1) + 2)
                    if fast and phase:
                        nc.vector.tensor_reduce(emx[:, i:i + 1], mx[:, i, :], AX_X, ALU.max, negate=True
                                                ).then_inc(max_ready, 1)
                        dve.wait_ge(max_ready, lay * NT + T.t + 1)
                        nc.vector.tensor_scalar(nmx[:, i:i + 1], emx[:, i:i + 1], node(zero_bound, T), None, ALU.min
                                                ).then_inc(nmax_ready, 1)
                    else:
                        nc.vector.tensor_reduce(nmx[:, i:i + 1], mx[:, i, :], AX_X, ALU.max, negate=True
                                                ).then_inc(nmax_ready, 1)

                def inverse_sum(T, back):
                    i, t = (T.first - back) % 2, T.t - back
                    dve.wait_ge(exp_done, fulls + t + 3)
                    nc.vector.reciprocal(rinv[:, i:i + 1], rsum[:, i:i + 1]).then_inc(rinv_ready, 1)

                def gap_bytes(T):
                    if fast:
                        dve.wait_ge(gaps_sent, lay * NT + T.t + 1)
                        nc.vector.tensor_scalar(pr[:, T.mod(2), HALF:N], slots[:, T.mod(UNROLL), HALF:N],
                                                -NO_EDGE / EDGE_BYTE, NO_EDGE, ALU.mult, ALU.add
                                                ).then_inc(gaps_v, 1)
                mask_rows(Tile(0, 0), 0)
                gap_bytes(Tile(0, 0))

                def attention(T):
                    mask_rows(T, 0)
                    inverse_sum(T, 1)
                    gap_bytes(T)
                loop(dve, 1, NT, attention)
                inverse_sum(Tile(NT, 0), 1)

                dve.wait_ge(att_ps, lay + 1)

                def by_quadrant(a):
                    return a.rearrange("p (b g r) -> p g b r", b=2, g=4)
                step(nc.vector.tensor_scalar(by_quadrant(imp[:, :]),
                                             ps[:, 0:4, 0:8].rearrange("p g (b r) -> p g b r", b=2),
                                             0.5 / N, None, ALU.mult))
                step(nc.vector.tensor_tensor(imp[:, :], imp[:, :], halfst[:, :], ALU.add))
                bound = node_softmax(0)
                step(nc.vector.tensor_scalar(cmask[:, :], ex[:, :], bound, None, ALU.is_ge))
                step(nc.vector.tensor_scalar(never[:, :], cmask[:, :], -NEVER, NEVER, ALU.mult, ALU.add))
                step(nc.vector.tensor_tensor(fmag[:, :], xsq[:, :], cmask[:, :], ALU.mult))
                norm_root(1, fmag[:, :])
                step(nc.vector.tensor_scalar(rnrm[:, :], fmag[:, :], NORM_MIN, None, ALU.max))
                step(nc.vector.reciprocal(rnrm[:, :], rnrm[:, :]))
                step(nc.vector.tensor_tensor(rnrm[:, :], rnrm[:, :], cmask[:, :], ALU.mult))
                step(nc.vector.tensor_tensor(tmp[:, 1], xcur[:, :, :], per_node(rnrm[:, :]), ALU.mult))
                split_left(tmp[:, 1])
                for n, m in ((0, 0), (1, 2), (2, 5), (3, 0)):
                    step(nc.vector.tensor_copy(parts2[:, :, n * D:(n + 1) * D], src_st[:, :, m * D:(m + 1) * D]))
                dve.sem_inc(src_ready, 1)
                dve.sem_inc(parts2_ready, 1)
                copy_turned(40, [to_stat(m) for m in range(3)])
                copy_turned(64, [to_rhs(rhs_a), to_rhs(rhs_b)])

                def prune(T, back):
                    first, t = T.first - back, T.t - back
                    i = first % 2
                    then = Tile(first, T.q)
                    dve.wait_ge(exp_done, fulls + NT + t + 3)
                    if fast:
                        nc.vector.tensor_scalar(whole_sum[:, i:i + 1], gap_exp[:, i:i + 1], node(gaps_n, then),
                                                rsum[:, i:i + 1], ALU.mult, ALU.add).then_inc(sum_ready, 1)
                        dve.wait_ge(sum_ready, lay * NT + t + 1)
                    total = whole_sum if fast else rsum
                    nc.vector.tensor_scalar(thr[:, i:i + 1], total[:, i:i + 1], th_cur[:, 0:1], node(never, then),
                                            ALU.mult, ALU.add).then_inc(thr_ready, 1)
                    dve.wait_ge(thr_ready, lay * NT + t + 1)
                    if fast:
                        dve.wait_ge(tr_done, lay * NT + t + 1)
                        dve.wait_ge(pr_sent, lay * NT + t + 1)
                        nc.vector.tensor_scalar(pr[:, i, :], expo[:, i, :], thr[:, i:i + 1], EDGE_BYTE,
                                                ALU.is_ge, ALU.mult).then_inc(e_used, 1)
                    else:
                        nc.vector.scalar_tensor_tensor(out=logits[:, i, :], in0=expo[:, i, :],
                                                       scalar=thr[:, i:i + 1], in1=gtile, op0=ALU.is_ge,
                                                       op1=ALU.mult, accum_out=node(conn, then)).then_inc(e_used, 1)

                def keep_count(T, back):
                    then = Tile(T.first - back, T.q)
                    dve.wait_ge(count_ps, lay * NT + then.t + 3)
                    nc.vector.tensor_scalar(node(conn, then), ps[:, 4 + then.mod(2), 0:1],
                                            EDGE_BYTE, None, ALU.mult).then_inc(count_read, 1)

                if fast:
                    mask_rows(Tile(0, 0), 1)
                    for t in range(1, 4):
                        mask_rows(Tile(t, 0), 1)
                        prune(Tile(t, 0), 1)

                    def cosines(T):
                        mask_rows(T, 1)
                        prune(T, 1)
                        keep_count(T, 4)
                    loop(dve, 4, NT, cosines)
                    prune(Tile(NT, 0), 1)
                    for t in range(NT, NT + 4):
                        keep_count(Tile(t, 0), 4)
                    dve.wait_ge(count_read, (lay + 1) * NT + 2)
                else:
                    def cosines(T):
                        mask_rows(T, 1)
                        prune(T, 0)
                    loop(dve, 0, NT, cosines)
                dve.wait_ge(e_used, fulls + 2 * NT + 2)

                step(nc.vector.tensor_scalar(conn[:, :], conn[:, :], gsc[:, SC_C:SC_C + 1], None, ALU.mult))
                step(nc.vector.tensor_tensor(imp[:, :], conn[:, :], fmag[:, :], ALU.mult))
                bound = node_softmax(1)
                step(nc.vector.tensor_scalar(nmask[:, :], ex[:, :], bound, None, ALU.is_ge))
                step(nc.vector.tensor_scalar(imp[:, :], conn[:, :], 0.0, None, ALU.is_gt))
                step(nc.vector.tensor_tensor(nmask[:, :], nmask[:, :], imp[:, :], ALU.mult))
                step(nc.vector.tensor_tensor(nmask[:, :], nmask[:, :], cmask[:, :], ALU.mult))
                step(nc.vector.tensor_copy(dvs[:, :], conn[:, :]))
                norm_root(2, dvs[:, :])
                step(nc.vector.reciprocal(dvs[:, :], dvs[:, :]))
                step(nc.vector.tensor_scalar(dvout[:, :], dvs[:, :], gsc[:, SC_D:SC_D + 1], None, ALU.mult))
                step(nc.vector.tensor_tensor(nmask[:, :], nmask[:, :], dvs[:, :], ALU.mult))
                step(nc.vector.tensor_tensor(tmp[:, 1], ywt[:, :, :], per_node(nmask[:, :]), ALU.mult))
                split(tmp[:, 1], parts[:, :, 0:D], parts[:, :, D:2 * D], parts[:, :, 2 * D:D3], tmp[:, 0])
                dve.sem_inc(parts_ready, 1)
                step(nc.vector.tensor_copy(th_cur[:, :], th_all[:, LAYERS - 1:LAYERS]))

                for h in range(2):
                    if not fast:
                        planes_of(1, h)
                    sums_of_sweep(1, h, tmp[:, 1, 0:JB, :])
                    split(tmp[:, 1, 0:JB, :], to_parts2(h, 0), to_parts2(h, 1), to_parts2(h, 2), tmp[:, 0, 0:JB, :])
                dve.sem_inc(parts2_ready, 1)

                def add_parts(T):
                    if not fast:
                        def group(b):
                            n = 8 * (lay * NT + T.t) + b
                            own = Order(dve, g_step_t, 4 * n)
                            dve.wait_ge(g_turned, n + 1)
                            own(nc.vector.tensor_copy(planesT[:, 0, :], ps[:, 7, :]))
                            own(nc.vector.tensor_tensor(blkT, ps[:, 7, :], planesT[:, 0, :], ALU.subtract))
                            own(nc.vector.tensor_copy(planesT[:, 1, :], blkT))
                            own(nc.vector.tensor_tensor(blkT, blkT, planesT[:, 1, :], ALU.subtract))
                            nc.vector.tensor_copy(planesT[:, 2, :], blkT).then_inc(g_split, 1)
                            dve.wait_ge(g_split, n + 1)
                        for b in range(8):
                            group(b)
                    i = T.mod(2)
                    dve.wait_ge(e_tile, lay * NT + T.t + 1 + UNROLL)
                    dve.wait_ge(msg_out, lay * NT + T.t + 1)
                    nc.vector.tensor_reduce(msum[:, i, :], ps[:, T.mod(UNROLL), 0:D3]
                                            .rearrange("p (k d) -> p d k", k=3), AX_X, ALU.add).then_inc(msg_sum, 1)
                loop(dve, 0, NT, add_parts)
                assert step.n == DVE_STEPS, step.n

            paths(dve, layer)
            dve.wait_ge(x_again, 16)
            nc.vector.tensor_tensor(tmp[:, 1], tmp[:, 0], xcur[:, :, :], ALU.add).then_inc(y_ready, 1)

        @block.tensor
        def _(pe):
            pe.wait_ge(consts, 10 + LAYERS)
            pe.wait_ge(tables_in, 16 * 7)
            nc.tensor.matmul(ps[0:D, 0, 0:D], wT[:, :], theta_s[:, :], start=True, stop=True).then_inc(wtheta_ps, 1)
            pe.wait_ge(wtheta_in, 1)

            def clear(banks):
                for b in banks:
                    nc.tensor.matmul(ps[:, b, :], zeros[:, 0:P], zeros[:, :], start=True, stop=False,
                                     skip_group_check=True)

            clear(range(8))

            def compare(T):
                pe.wait_ge(row_mark, T.t + 1 + UNROLL)
                alone(pe, passed)
                for b in range(8):
                    cols = slice(b * BANK, (b + 1) * BANK)
                    nc.tensor.matmul(ps[:, b, :], half_ones[:, :], slots[:, T.mod(UNROLL), cols].bitcast(FP8),
                                     start=False, stop=False, skip_group_check=True)
                for b in range(8):
                    cols = slice(b * BANK, (b + 1) * BANK)
                    last = nc.tensor.matmul(ps[:, b, :], neg_ones[:, :], marks[:, T.mod(2), cols],
                                            start=False, stop=False, skip_group_check=True)
                last.then_inc(row_chk, 1)
            loop(pe, 0, NT, compare)

            def layer(fast, lay):
                fulls = lay * (2 * NT)
                halves = lay * (4 * NT)
                turns = lay * 40

                def sweep(phase, h, columns):
                    width = DS if phase else D3
                    if h:
                        pe.wait_ge(sweep_read, 4 * lay + 2 * phase + h)
                    clear(range(8))

                    def one(T):
                        k = (2 * phase + h) * NT
                        n = halves + k + T.t
                        i = T.mod(UNROLL)
                        if fast:
                            pe.wait_ge(half_in[i], 16 * (lay * NT + k // UNROLL + T.div(UNROLL) + 1))
                            weights = [ring_h[:, i, :].bitcast(FP8)]
                        else:
                            pe.wait_ge(g_planes, n + 1)
                            weights = [planes[:, m, :] for m in range(3)]
                        pe.wait_ge(staged_in, n + 1)
                        alone(pe, passed)
                        for j in range(JB):
                            for w in weights:
                                last = nc.tensor.matmul(ps[:, j // 2, 256 * (j % 2):256 * (j % 2) + width],
                                                        columns(w, j), staged[:, i, 0:width], start=False,
                                                        stop=False, skip_group_check=True)
                        last.then_inc(half_used, 1)
                    loop(pe, 0, NT, one)
                    nc.tensor.matmul(ps[:, 7, :], zeros[:, 0:P], zeros[:, :], start=False, stop=True,
                                     skip_group_check=True).then_inc(sweep_ps, 1)

                def turn(first, blocks):
                    for m, blk in enumerate(blocks):
                        def one(T, m=m, blk=blk):
                            n = first + 8 * m
                            pe.wait_ge(turn_a if T.mod(2) else turn_v, turns + n // 2 + T.div(2) + 1)
                            for i in range(4):
                                last = nc.tensor.matmul(ps[:, T.mod(4), i * P:(i + 1) * P],
                                                        blk(4 * T.t + i), ident_b[:, :], start=(i == 0), stop=True,
                                                        skip_group_check=True)
                            last.then_inc(turned, 1)
                        loop(pe, 0, NT // 4, one)

                def turn_sides(first, n):
                    pe.wait_ge(src_ready, 2 * lay + n + 1)
                    turn(first, [lambda t, m=m: src_st[:, ds(t, 1), m * P:(m + 1) * P].rearrange("p a c -> p (a c)")
                                 for m in range(3)])
                    pe.wait_ge(parts2_ready, 3 * lay + n + 1)
                    turn(first + 24, [lambda t, m=m: parts2[:, ds(t, 1), m * P:(m + 1) * P]
                                      .rearrange("p a c -> p (a c)") for m in range(2)])
                    pe.wait_ge(turn_v, turns + (first + 40) // 2 + 2)
                    pe.wait_ge(turn_a, turns + (first + 40) // 2 + 2)

                def row_logits(T, phase, between=None):
                    for c in range(NC):
                        if c == NC // 2 and between:
                            between(T, 2)
                        n = NC * (fulls + phase * NT + T.t) + c
                        pe.wait_ge(qk_used, n + 1)
                        for m, rhs in enumerate((rhs_a, rhs_a, rhs_b)):
                            for b in range(2):
                                last = nc.tensor.matmul(
                                    ps[:, 2 * (c % 2) + b, :], stat[:, ds(T.t, 1), m, :].rearrange("p a c -> p (a c)"),
                                    rhs[:, c * CW + b * BANK:c * CW + (b + 1) * BANK], start=(m == 0), stop=(m == 2))
                        last.then_inc(qk_ready, 1)

                def column_sums(T, back):
                    i, t = (T.first - back) % 2, T.t - back
                    pe.wait_ge(rinv_ready, lay * NT + t + 1)
                    for j in range(8):
                        g = j % 4
                        last = nc.tensor.matmul(ps[32 * g:32 * g + 1, 4 + j // 4, :], rinv[:, i:i + 1],
                                                expo[:, i, j * BANK:(j + 1) * BANK], start=False, stop=False,
                                                skip_group_check=True)
                    last.then_inc(e_used, 1)

                def count_pruned(T, back):
                    i, t = (T.first - back) % 2, T.t - back
                    pe.wait_ge(ev_done, lay * NT + t + 2)
                    pe.wait_ge(count_read, lay * NT + t + 1)
                    alone(pe, passed)
                    blocks = prT[:, i, :].bitcast(FP8).rearrange("p (g a k) -> p g a k", g=WG, k=4)
                    for j in range(NT):
                        last = nc.tensor.matmul(ps[:, 4 + i, 0:1], blocks[:, j // 4, :, j % 4],
                                                half_ones[:, 0:1], start=(j == 0), stop=(j == NT - 1))
                    last.then_inc(count_ps, 1)

                def turn_pruned(T, back):
                    i, t = (T.first - back) % 2, T.t - back
                    pe.wait_ge(e_used, fulls + NT + t + 3)
                    pe.wait_ge(ev_done, lay * NT + t + 1)
                    words = pr[:, i, :].bitcast(F32)
                    for g in range(WG):
                        last = nc.tensor.transpose(ps[:, 6 + g // 4, P * (g % 4):P * (g % 4) + P],
                                                   words[:, g * P:(g + 1) * P], ident_f[:, :])
                    last.then_inc(tr_done, 1)

                pe.wait_ge(ln_x, 1)
                pe.wait_ge(msg_out, lay * NT + 2)
                for s in range(NT // 2):
                    last = nc.tensor.transpose(ps[:, s // 4, P * (s % 4):P * (s % 4) + P],
                                               xcur[:, 2 * s:2 * s + 2, :].rearrange("p a d -> p (a d)"),
                                               ident_f[:, :])
                last.then_inc(xT_ps, 1)
                pe.wait_ge(xT_even, lay + 1)
                pe.wait_ge(xT_odd, lay + 1)
                pe.wait_ge(xT_one, lay + 1)
                for r in range(2):
                    for b in range(8):
                        if r:
                            pe.wait_ge(all_a if b % 2 else all_v, 8 * lay + b // 2 + 1)
                        for i in range(2):
                            t = 16 * r + 2 * b + i
                            last = nc.tensor.matmul(ps[:, b, 256 * i:256 * (i + 1)], xTa[:, t * P:(t + 1) * P],
                                                    w_all[:, :], start=(i == 0), stop=True, skip_group_check=True)
                        last.then_inc(all_ps, 1)
                pe.wait_ge(all_v, 8 * (lay + 1))
                pe.wait_ge(all_a, 8 * (lay + 1))

                for h in range(2):
                    sweep(0, h, lambda w, j: w[:, j * P:(j + 1) * P])
                pe.wait_ge(sweep_read, 4 * lay + 2)
                turn_sides(0, 0)

                clear((4, 5))
                for t in range(2):
                    row_logits(Tile(t, 0), 0)
                loop(pe, 2, NT, lambda T: row_logits(T, 0, column_sums))
                for t in (NT, NT + 1):
                    column_sums(Tile(t, 0), 2)
                pe.wait_ge(qk_used, NC * (fulls + NT) + 2)
                pe.wait_ge(col_read, 4 * lay + 4)
                for t in range(NT):
                    chunk = t // 4
                    g, b = chunk % 4, chunk // 4
                    off = b * BANK + (t % 4) * P
                    last = nc.tensor.matmul(ps[:, g, 4 * b + t % 4:4 * b + t % 4 + 1],
                                            col_row[32 * g:32 * g + 1, off:off + P], ones_c[32 * g:32 * g + 1, :],
                                            start=True, stop=True, skip_group_check=True)
                last.then_inc(att_ps, 1)
                turn_sides(40, 1)

                if fast:
                    for t in range(4):
                        row_logits(Tile(t, 0), 1, turn_pruned if t >= 2 else None)
                        if t == 3:
                            count_pruned(Tile(t, 0), 3)

                    def cosines(T):
                        row_logits(T, 1, turn_pruned)
                        count_pruned(T, 3)
                    loop(pe, 4, NT, cosines)
                    for t in range(NT, NT + 3):
                        if t < NT + 2:
                            turn_pruned(Tile(t, 0), 2)
                        count_pruned(Tile(t, 0), 3)
                    pe.wait_ge(ev_done, (lay + 1) * NT + 1)
                    pe.wait_ge(count_read, (lay + 1) * NT + 2)
                else:
                    loop(pe, 0, NT, lambda T: row_logits(T, 1))
                pe.wait_ge(qk_used, NC * (fulls + 2 * NT) + 2)

                def word_columns(w, j):
                    g, k = j // 4, j % 4
                    return w[:, 4 * P * g:4 * P * (g + 1)].rearrange("p (b k) -> p b k", k=4)[:, :, k]
                for h in range(2):
                    sweep(1, h, word_columns)
                pe.wait_ge(sweep_read, 4 * lay + 4)
                pe.wait_ge(parts2_ready, 3 * lay + 3)

                def messages(T):
                    i = T.mod(UNROLL)
                    pe.wait_ge(msg_sum, lay * NT + T.t + 1)
                    dst = ps[:, i, 0:D3]
                    if fast:
                        pe.wait_ge(turned_in[i], 16 * (lay * (NT // UNROLL) + T.div(UNROLL) + 1))
                        alone(pe, passed)
                        blocks = slots[:, i, :].bitcast(FP8).rearrange("p (g a k) -> p g a k", g=WG, k=4)
                        for j in range(NT):
                            last = nc.tensor.matmul(dst, blocks[:, j // 4, :, j % 4], parts2[:, j, 0:D3],
                                                    start=(j == 0), stop=(j == NT - 1))
                    else:
                        pe.wait_ge(g_full_in, 16 * (lay * (3 * NT) + 2 * NT + T.t + 1))
                        for g in range(WG):
                            n = 8 * (lay * NT + T.t) + g
                            for k in range(4):
                                last = nc.tensor.transpose(ps[:, 7, k * P:(k + 1) * P], word_columns(gtile, 4 * g + k),
                                                           ident_f[:, :])
                            last.then_inc(g_turned, 1)
                            pe.wait_ge(g_split, n + 1)
                            for k in range(4):
                                for m in range(3):
                                    last = nc.tensor.matmul(dst, planesT[:, m, k * P:(k + 1) * P],
                                                            parts2[:, 4 * g + k, 0:D3],
                                                            start=(g == 0 and k == 0 and m == 0),
                                                            stop=(g == WG - 1 and k == 3 and m == 2))
                    last.then_inc(e_tile, 1)
                loop(pe, 0, NT, messages)

            paths(pe, layer)


_INS = ["x", "adj", "L0_gnn_W", "L0_gnn_Theta", "L0_gnn_Wq", "L0_gnn_bq", "L0_gnn_Wv", "L0_gnn_bv"]
_OUTS = [((4096, 64), "float32")]


def kernel(**inputs):
    import numpy as _np
    import concourse.bacc as _bacc
    from concourse import mybir as _mybir
    from concourse.bass_utils import run_bass_kernel_spmd as _run

    nc = _bacc.Bacc("TRN2", target_bir_lowering=False, num_devices=1)
    arrays, args = {}, []
    for name in _INS:
        a = _np.ascontiguousarray(inputs[name])
        arrays[f"in_{name}_dram"] = a
        args.append(nc.dram_tensor(f"in_{name}_dram", a.shape, _mybir.dt.from_np(a.dtype), kind="ExternalInput").ap())
    for i, (shape, dtype) in enumerate(_OUTS):
        dt = _mybir.dt.from_np(_np.dtype(dtype))
        args.append(nc.dram_tensor(f"out_{i}_dram", shape, dt, kind="ExternalOutput").ap())
    gnn_kernel(nc, *args)
    r = _run(nc, [arrays], core_ids=[0])
    return r.results[0]["out_0_dram"]
```

```python
from contextlib import ExitStack

import concourse.bass as bass
from concourse import mybir

ALU = mybir.AluOpType
ACT = mybir.ActivationFunctionType
F32 = mybir.dt.float32
BF16 = mybir.dt.bfloat16
FP8 = mybir.dt.float8e4
U8 = mybir.dt.uint8
U16 = mybir.dt.uint16
I32 = mybir.dt.int32
AX_X = mybir.AxisListType.X
RMAX = bass.bass_isa.ReduceOp.max
RADD = bass.bass_isa.ReduceOp.add
ds = bass.ds

P = 128
UNROLL = 4
LN_EPS = 1e-5
DEG_EPS = 1e-6
NORM_FLOOR = 1e-16
NORM_MIN = 1e-8
THRESHOLDS = (0.000244, 0.000244 + (1.0 - 2.718281828459045 ** -0.1) * (0.0003 - 0.000244))
NEVER = 1e30
DVE_STEPS = 88
EDGE_BYTE = 64.0
EDGE_FP8 = 2.0
NO_EDGE = 255.0
LEAST_VALUE, MOST_VALUE = 0.5, 1e9


class Tile:

    def __init__(self, first, q):
        self.first, self.q = first, q
        self.t = first + UNROLL * q

    def div(self, n):
        return self.first // n + (UNROLL // n) * self.q

    def mod(self, n):
        return self.first % n


def alone(eng, passed):
    eng.sem_inc(passed, 1)


def tiles(eng, first, last, body, passed):
    turns = (last - first) // UNROLL
    if turns > 0:
        alone(eng, passed)
        with eng.Fori(0, turns) as q:
            for i in range(UNROLL):
                body(Tile(first + i, q))
    for i in range(first + turns * UNROLL, last):
        body(Tile(i, 0))


class Order:

    def __init__(self, eng, sem, base=0):
        self.eng, self.sem, self.base, self.n = eng, sem, base, 0

    def __call__(self, instruction):
        instruction.then_inc(self.sem, 1)
        self.n += 1
        self.eng.wait_ge(self.sem, self.base + self.n)


def gnn_kernel(nc, x, adj, W, Theta, Wq, bq, Wv, bv, out):
    N, D = x.shape
    NT = N // P
    HALF = N // 2
    JB = HALF // P
    NC = 4
    CW = N // NC
    BANK = 512
    D3 = 3 * D
    DS = D3 + 1
    LAYERS = len(THRESHOLDS)
    WORDS = N // 4
    WG = WORDS // P
    assert D == 64 and NT % UNROLL == 0 and JB * 256 == 8 * BANK

    with ExitStack() as ctx:
        def sb(name, shape, dt):
            return ctx.enter_context(nc.sbuf_tensor(name, shape, dt))

        def sem(name):
            return ctx.enter_context(nc.semaphore(name))

        edges_d = nc.dram_tensor("edges_d", (NT, P, N), U8).ap()
        gaps_d = nc.dram_tensor("gaps_d", (NT, P, N), U8).ap()
        pruned_d = nc.dram_tensor("pruned_d", (NT, P, N), U8).ap()
        prunedT_d = nc.dram_tensor("prunedT_d", (NT, P, N), U8).ap()
        prunedf_d = nc.dram_tensor("prunedf_d", (NT, P, N), F32).ap()
        adj_t = adj.rearrange("(t p) n -> t p n", p=P)

        logits = sb("logits", [P, 2, N], F32)
        expo = sb("expo", [P, 2, N], F32)
        rs_buf = sb("rs_buf", [P, NT * 6 * D], BF16)
        stat = sb("stat", [P, NT, 3, P], BF16)
        xcur = sb("xcur", [P, NT, D], F32)
        ywt = sb("ywt", [P, NT, D], F32)
        parts = sb("parts", [P, NT, 4 * D], BF16)
        parts2 = sb("parts2", [P, NT, 4 * D], BF16)
        slots = sb("slots", [P, UNROLL, N], U8)
        pr = sb("pr", [P, 2, N], U8)
        prT = sb("prT", [P, 2, N], U8)
        staged = sb("staged", [P, UNROLL, 4 * D], BF16)
        ident_f = sb("ident_f", [P, P], F32)
        ident_b = sb("ident_b", [P, P], BF16)
        zeros = sb("zeros", [P, BANK], BF16)
        half_ones = sb("half_ones", [P, P], BF16)
        neg_ones = sb("neg_ones", [P, P], BF16)
        w_all = sb("w_all", [D + 1, 4 * D], F32)
        wT = sb("wT", [D, D], F32)
        theta_s = sb("theta_s", [D, D], F32)
        value = sb("value", [P, 4], F32)
        flag = sb("flag", [P, 1], I32)
        th_all = sb("th_all", [P, LAYERS], F32)
        th_cur = sb("th_cur", [P, 1], F32)
        gsc = sb("gsc", [P, 4], F32)
        mx = sb("mx", [P, 2, NC], F32)
        nmx = sb("nmx", [P, 2], F32)
        emx = sb("emx", [P, 2], F32)
        rsum = sb("rsum", [P, 2], F32)
        rinv = sb("rinv", [P, 2], F32)
        thr = sb("thr", [P, 2], F32)
        msum = sb("msum", [P, 2, D], F32)
        halfst = sb("halfst", [P, NT], F32)
        xsq = sb("xsq", [P, NT], F32)
        imp = sb("imp", [P, NT], F32)
        ex = sb("ex", [P, NT], F32)
        cmask = sb("cmask", [P, NT], F32)
        never = sb("never", [P, NT], F32)
        fmag = sb("fmag", [P, NT], F32)
        rnrm = sb("rnrm", [P, NT], F32)
        conn = sb("conn", [P, NT], F32)
        dvs = sb("dvs", [P, NT], F32)
        dvout = sb("dvout", [P, NT], F32)
        nmask = sb("nmask", [P, NT], F32)
        edges_n = sb("edges_n", [P, NT], F32)
        gaps_n = sb("gaps_n", [P, NT], F32)
        zero_bound = sb("zero_bound", [P, NT], F32)
        gap_exp = sb("gap_exp", [P, 2], F32)
        whole_sum = sb("whole_sum", [P, 2], F32)
        fac = sb("fac", [P, JB], F32)
        red = sb("red", [P, 8], F32)

        ps = ctx.enter_context(nc.psum_tensor("ps", [P, 8, BANK], F32))

        tmp = expo[:, :, :].rearrange("p a (b t d) -> p (a b) t d", b=2, d=D)
        rows4 = [logits[:, 0, :], logits[:, 1, :], expo[:, 0, :], expo[:, 1, :]]
        x_all = logits[:, :, :].rearrange("p a n -> p (a n)")[:, 0:NT * D3].rearrange("p (t c) -> p t c", c=D3)
        xWv = ps[:, 4:8, :].rearrange("p b (t d) -> p (b t) d", d=D)
        col_row = prT[:, 0, :].bitcast(F32)
        slots2 = parts2[:, :, :].rearrange("p t (k d) -> p t k d", d=D)
        q_pairs = rs_buf[:, 0:2 * N].rearrange("p (t k d) -> p t k d", k=4, d=D)
        tail_pair = rs_buf[:, 2 * N:3 * N].rearrange("p (t k d) -> p t k d", k=2, d=D)
        parts_pair = parts[:, :, 0:2 * D].rearrange("p t (k d) -> p t k d", d=D)
        rhs_a = rs_buf[:, 0:N]
        rhs_b = rs_buf[:, N:2 * N]
        xTa = parts2[:, :, :].rearrange("p t c -> p (t c)").bitcast(F32)[0:D + 1, :]
        marks = rs_buf[:, 0:2 * N].rearrange("p (a n) -> p a n", a=2)
        ring_h = slots[:, :, 0:HALF]
        gtile = slots[:, :, :].rearrange("p a n -> p (a n)").bitcast(F32)
        planes = expo[:, 1, :].bitcast(BF16)[:, 0:3 * HALF].rearrange("p (k n) -> p k n", k=3)
        blkT = logits[:, 0, 0:BANK]
        planesT = expo[:, 1, :].bitcast(BF16)[:, 0:3 * BANK].rearrange("p (k n) -> p k n", k=3)


        def many(name, n):
            return [sem(f"{name}{i}") for i in range(n)]

        passed = sem("passed")
        consts = sem("consts")
        tables_in = sem("tables_in")
        value_in = sem("value_in")
        x_in = sem("x_in")
        row_in = many("row_in", UNROLL)
        row_byte = sem("row_byte")
        row_mark = sem("row_mark")
        row_chk = sem("row_chk")
        edges_out = sem("edges_out")
        edges_sent = sem("edges_sent")
        row_count = sem("row_count")
        flag_set = sem("flag_set")
        wtheta_ps = sem("wtheta_ps")
        wtheta_in = sem("wtheta_in")
        ln_sq = sem("ln_sq")
        ln_v = sem("ln_v")
        ln_x = sem("ln_x")
        dve_pre = sem("dve_pre")
        dve_step = sem("dve_step")
        sc_set = sem("sc_set")
        xT_ps = sem("xT_ps")
        xT_even = sem("xT_even")
        xT_odd = sem("xT_odd")
        xT_one = sem("xT_one")
        v_ps = sem("v_ps")
        all_ps = sem("all_ps")
        all_a = sem("all_a")
        squares = sem("squares")
        parts_ready = sem("parts_ready")
        src_ready = sem("src_ready")
        parts2_ready = sem("parts2_ready")
        staged_in = sem("staged_in")
        half_in = many("half_in", UNROLL)
        half_used = sem("half_used")
        sweep_ps = sem("sweep_ps")
        sweep_read = sem("sweep_read")
        turned_v = sem("turned_v")
        turned_a = sem("turned_a")
        turn_v = sem("turn_v")
        turn_a = sem("turn_a")
        full_in = many("full_in", UNROLL)
        qk_ready = sem("qk_ready")
        qk_used = sem("qk_used")
        nmax_ready = sem("nmax_ready")
        exp_done = sem("exp_done")
        rinv_ready = sem("rinv_ready")
        e_used = sem("e_used")
        thr_ready = sem("thr_ready")
        tr_done = sem("tr_done")
        ev_done = sem("ev_done")
        count_ps = sem("count_ps")
        count_read = sem("count_read")
        gaps_a = sem("gaps_a")
        gaps_v = sem("gaps_v")
        gaps_out = sem("gaps_out")
        gaps_sent = sem("gaps_sent")
        sum_ready = sem("sum_ready")
        max_ready = sem("max_ready")
        pr_out = sem("pr_out")
        pr_sent = sem("pr_sent")
        prT_out = sem("prT_out")
        col_zero = sem("col_zero")
        col_read_a = sem("col_read_a")
        col_read_v = sem("col_read_v")
        att_ps = sem("att_ps")
        red_in = sem("red_in")
        red_out = sem("red_out")
        sm_in = sem("sm_in")
        sm_out = sem("sm_out")
        root_in = sem("root_in")
        root_out = sem("root_out")
        turned_in = many("turned_in", UNROLL)
        e_tile = sem("e_tile")
        msg_sum = sem("msg_sum")
        msg_out = sem("msg_out")
        x_again = sem("x_again")
        y_ready = sem("y_ready")
        y_out = sem("y_out")
        g_half_in = many("g_half_in", 2)
        g_half_free = sem("g_half_free")
        g_step = sem("g_step")
        g_step_t = sem("g_step_t")
        g_planes = sem("g_planes")
        g_full_in = sem("g_full_in")
        g_turned = sem("g_turned")
        g_split = sem("g_split")

        SC_B, SC_C, SC_D = 0, 1, 2

        block = ctx.enter_context(nc.Block())

        def loop(eng, first, last, body):
            tiles(eng, first, last, body, passed)

        def dtile(dram, T):
            return dram[ds(T.t, 1), :, :].rearrange("a p n -> (a p) n")

        def dhalf(dram, T, h):
            return dram[ds(T.t, 1), :, h * HALF:(h + 1) * HALF].rearrange("a p n -> (a p) n")

        def node(a, T):
            return a[:, ds(T.t, 1)]

        LEFT1, LEFT2, LEFT3, RIGHT1, RIGHT3 = range(5)
        GROUPS = NT // 4

        def turn_plan(side):
            def each(kind):
                return [(kind, a) for a in range(GROUPS)]
            plan = [(k, a, True) for k, a in each(LEFT1) + each(LEFT2)]
            if side == 0:
                for a in range(GROUPS):
                    plan += [(LEFT3, a, True), (RIGHT1, a, False)]
                return plan + [(k, a, a % 2 == 0) for k, a in each(RIGHT3)]
            return plan + [(k, a, a % 2 == 0) for k, a in each(LEFT3) + each(RIGHT1) + each(RIGHT3)]
        TURNS_A = [sum(by_act for _, _, by_act in turn_plan(side)) for side in range(2)]
        TURNS_V = [len(turn_plan(side)) - TURNS_A[side] for side in range(2)]

        def copy_column_sums(copy, g):
            return copy(col_row[32 * g:32 * g + 1, 0:2 * BANK].rearrange("p (a c) -> p a c", a=2),
                        ps[32 * g:32 * g + 1, 4:6, :])

        def turned_to(kind, a):
            if kind <= LEFT3:
                return stat[:, 4 * a:4 * (a + 1), kind, :]
            rhs = rhs_a if kind == RIGHT1 else rhs_b
            return rhs[:, 4 * P * a:4 * P * (a + 1)].rearrange("p (a c) -> p a c", c=P)

        def copy_turned(eng, copy, lay, side):
            act = eng is nc.scalar
            per, ready, done = (TURNS_A, turned_a, turn_a) if act else (TURNS_V, turned_v, turn_v)
            mine = [(kind, a) for kind, a, by_act in turn_plan(side) if by_act == act]
            for n, (kind, a) in enumerate(mine):
                eng.wait_ge(ready, lay * sum(per) + side * per[0] + n + 1)
                copy(turned_to(kind, a), ps[:, (0 if act else 4) + n % 4, :].rearrange("p (a c) -> p a c", c=P)
                     ).then_inc(done, 1)

        def paths(eng, layer):
            eng.wait_ge(flag_set, 1)
            fast = eng.value_load(flag[0:1, 0:1], min_val=0, max_val=1)
            with eng.If(fast == 1):
                with eng.Fori(0, LAYERS) as lay:
                    layer(True, lay)
            with eng.Else():
                with eng.Fori(0, LAYERS) as lay:
                    layer(False, lay)

        @block.sync
        def _(sp):
            with nc.allow_non_contiguous_dma(reason="small tables"):
                sp.dma_start(xcur[:, :, :], x.rearrange("(t p) d -> p t d", p=P)).then_inc(x_in, 16)
                sp.dma_start(value[:, 0:1], adj[0:1, 0:1].to_broadcast([P, 1])).then_inc(value_in, 16)
                sp.wait_ge(consts, 1)
                for dst, src in ((w_all[0:D, 0:D], Wv), (w_all[0:D, D:2 * D], W), (w_all[0:D, 2 * D:3 * D], Wq),
                                 (w_all[D:D + 1, 0:D], bv.rearrange("(a d) -> a d", a=1)),
                                 (w_all[D:D + 1, 2 * D:3 * D], bq.rearrange("(a d) -> a d", a=1)),
                                 (theta_s[:, :], Theta)):
                    sp.dma_start(dst, src).then_inc(tables_in, 16)
            def row(T):
                i = T.mod(UNROLL)
                sp.wait_ge(row_mark, T.t + 1)
                alone(sp, passed)
                sp.dma_start(rows4[i], dtile(adj_t, T)).then_inc(row_in[i], 16)
            loop(sp, 0, NT, row)

            def layer(fast, lay):
                halves = lay * (4 * NT)
                fulls = lay * (2 * NT)

                def half_sweeps(source, phase):
                    for h in range(2):
                        def half(T, h=h):
                            n = halves + (2 * phase + h) * NT + T.t
                            if fast:
                                sp.wait_ge(half_used, n + 1)
                                alone(sp, passed)
                                i = T.mod(UNROLL)
                                sp.dma_start(ring_h[:, i, :], dhalf(source, T, h)).then_inc(half_in[i], 16)
                            else:
                                sp.wait_ge(g_half_free, n + 1)
                                alone(sp, passed)
                                i = T.mod(2)
                                sp.dma_start(gtile[:, i * HALF:(i + 1) * HALF],
                                             dhalf(source, T, h)).then_inc(g_half_in[i], 16)
                        loop(sp, 0, NT, half)

                def store_turned(t, i):
                    sp.wait_ge(ev_done, lay * NT + t + 2)
                    alone(sp, passed)
                    sp.wait_ge(prT_out, 16 * (lay * NT + t + 2))
                    alone(sp, passed)
                    sp.dma_start(prunedT_d[ds(t, 1), :, :].rearrange("a p n -> (a p) n"),
                                 prT[:, i, :]).then_inc(prT_out, 16)

                def whole(source, wait, into, signals):
                    def one(T):
                        wait(T)
                        alone(sp, passed)
                        i = T.mod(UNROLL) if fast else 0
                        sp.dma_start(into(i), dtile(source, T)).then_inc(signals[i], 16)
                    loop(sp, 0, NT, one)

                def slot(i):
                    return slots[:, i, :] if fast else gtile

                sp.wait_ge(edges_sent, NT + UNROLL)
                sp.wait_ge(e_tile, lay * NT + UNROLL)
                alone(sp, passed)
                half_sweeps(edges_d if fast else adj_t, 0)

                sp.wait_ge(half_used, halves + 2 * NT + UNROLL)

                def slot_masked(T):
                    sp.wait_ge(nmax_ready, fulls + T.t + (1 if fast else UNROLL))
                    if fast:
                        sp.wait_ge(gaps_a, lay * NT + T.t + 1)
                        sp.wait_ge(gaps_v, lay * NT + T.t + 1)
                whole(edges_d if fast else adj_t, slot_masked,
                      slot, full_in if fast else [g_full_in])
                sp.wait_ge(nmax_ready, fulls + NT + UNROLL)
                if fast:
                    sp.wait_ge(gaps_sent, (lay + 1) * NT + 2)
                    alone(sp, passed)
                if fast:
                    def gaps_row(T):
                        sp.wait_ge(nmax_ready, fulls + NT + T.t + 1)
                        alone(sp, passed)
                        i = T.mod(UNROLL)
                        sp.dma_start(slot(i), dtile(gaps_d, T)).then_inc(full_in[i], 16)

                    def gaps_row_and_store(T):
                        gaps_row(T)
                        store_turned(T.t - BEHIND, (T.first - BEHIND) % 2)
                    BEHIND = 2 * UNROLL - 1
                    for t in range(BEHIND):
                        gaps_row(Tile(t, 0))
                    loop(sp, BEHIND, NT, gaps_row_and_store)
                    for t in range(NT - BEHIND, NT):
                        store_turned(t, t % 2)
                else:
                    whole(adj_t, lambda T: sp.wait_ge(e_used, fulls + NT + T.t + 2), slot, [g_full_in])

                sp.wait_ge(e_used, fulls + 2 * NT + 2)
                sp.wait_ge(pr_sent, (lay + 1) * NT + 2)
                alone(sp, passed)
                half_sweeps(pruned_d if fast else prunedf_d, 1)

                sp.wait_ge(half_used, halves + 4 * NT + UNROLL)
                alone(sp, passed)
                if fast:
                    sp.wait_ge(prT_out, 16 * ((lay + 1) * NT + 2))
                    alone(sp, passed)
                whole(prunedT_d if fast else prunedf_d,
                      lambda T: sp.wait_ge(e_tile, lay * NT + T.t + (1 if fast else UNROLL)),
                      slot, turned_in if fast else [g_full_in])

            paths(sp, layer)
            sp.wait_ge(msg_out, LAYERS * NT + 2)
            with nc.allow_non_contiguous_dma(reason="rows of 256 bytes"):
                sp.dma_start(tmp[:, 0], x.rearrange("(t p) d -> p t d", p=P)).then_inc(x_again, 16)
                sp.wait_ge(y_ready, 1)
                sp.dma_start(out.rearrange("(t p) d -> p t d", p=P), tmp[:, 1]).then_inc(y_out, 16)
            sp.wait_ge(y_out, 16)

        @block.gpsimd
        def _(pool):
            for s, n in ((row_mark, UNROLL), (row_chk, 2), (half_used, UNROLL), (turn_v, 4), (turn_a, 4), (all_a, 4),
                         (qk_used, 2), (nmax_ready, UNROLL), (exp_done, 2), (e_used, 2), (tr_done, 2),
                         (ev_done, 1), (e_tile, UNROLL), (msg_sum, UNROLL), (msg_out, 2), (g_half_free, 2),
                         (edges_sent, UNROLL), (row_count, UNROLL), (count_ps, 2), (count_read, 2),
                         (gaps_a, UNROLL), (gaps_v, UNROLL),
                         (gaps_sent, 2), (pr_sent, 2), (prT_out, 32)):
                pool.sem_inc(s, n)
            nc.gpsimd.memset(w_all[:, :], 0.0).then_inc(consts, 1)
            nc.gpsimd.memset(ident_f[:, :], 0.0).then_inc(consts, 1)
            nc.gpsimd.memset(zeros[:, :], 0.0).then_inc(consts, 1)
            nc.gpsimd.memset(half_ones[:, :], 1.0 / EDGE_FP8).then_inc(consts, 1)
            nc.gpsimd.memset(neg_ones[:, :], -1.0).then_inc(consts, 1)
            for n, th in enumerate(THRESHOLDS):
                nc.gpsimd.memset(th_all[:, n:n + 1], th).then_inc(consts, 1)
            pool.wait_ge(consts, 5 + LAYERS)
            nc.gpsimd.affine_select(out=ident_f[:, :], in_=ident_f[:, :], compare_op=ALU.not_equal, fill=1.0,
                                    base=0, pattern=[[-1, P]], channel_multiplier=1).then_inc(consts, 1)
            pool.wait_ge(consts, 6 + LAYERS)
            nc.gpsimd.tensor_copy(ident_b[:, :], ident_f[:, :]).then_inc(consts, 1)
            nc.gpsimd.memset(parts[:, :, D3:4 * D], 1.0).then_inc(consts, 1)

            def store_edges(T):
                pool.wait_ge(row_byte, T.t + 1)
                alone(pool, passed)
                i = T.mod(UNROLL)
                nc.gpsimd.dma_start(dtile(edges_d, T), slots[:, i, :]).then_inc(edges_out, 16)
                pool.wait_ge(edges_out, 16 * (T.t + 1))
                pool.sem_inc(edges_sent, 1)
            loop(pool, 0, NT, store_edges)

            def layer(fast, lay):
                halves = lay * (4 * NT)
                fulls = lay * (2 * NT)

                def stage(phase):
                    for h in range(2):
                        def one(T, h=h):
                            n = halves + (2 * phase + h) * NT + T.t
                            pool.wait_ge(half_used, n + 1)
                            alone(pool, passed)
                            nc.gpsimd.tensor_copy(staged[:, T.mod(UNROLL), 0:DS],
                                                  parts[:, ds(T.t, 1), 0:DS].rearrange("p a c -> p (a c)")
                                                  ).then_inc(staged_in, 1)
                        if h:
                            loop(pool, 0, NT, one)
                            continue
                        for half in range(2):
                            pool.wait_ge(parts_ready, 4 * lay + 2 * phase + half + 1)
                            alone(pool, passed)
                            loop(pool, half * NT // 2, (half + 1) * NT // 2, one)

                def reduce_over_partitions(n, op):
                    pool.wait_ge(red_in, 4 * lay + n + 1)
                    alone(pool, passed)
                    nc.gpsimd.partition_all_reduce(red[:, 4 + n:5 + n], red[:, n:n + 1], P, op).then_inc(red_out, 1)

                pool.wait_ge(xT_ps, lay + 1)
                alone(pool, passed)
                nc.gpsimd.memset(xTa[D:D + 1, :], 1.0).then_inc(xT_one, 1)
                stage(0)
                pool.wait_ge(half_used, halves + 2 * NT + UNROLL)
                alone(pool, passed)
                nc.gpsimd.memset(col_row[:, 0:2 * BANK], 0.0).then_inc(col_zero, 1)
                if fast:
                    def store_gaps(T):
                        pool.wait_ge(gaps_a, lay * NT + T.t + 1 + UNROLL)
                        pool.wait_ge(gaps_v, lay * NT + T.t + 1 + UNROLL)
                        alone(pool, passed)
                        nc.gpsimd.dma_start(dtile(gaps_d, T), pr[:, T.mod(2), :]).then_inc(gaps_out, 16)
                        pool.wait_ge(gaps_out, 16 * (lay * NT + T.t + 1))
                        pool.sem_inc(gaps_sent, 1)
                    loop(pool, 0, NT, store_gaps)
                reduce_over_partitions(0, RMAX)
                reduce_over_partitions(1, RADD)

                def store(T):
                    i = T.mod(2)
                    pool.wait_ge(e_used, fulls + NT + T.t + 3)
                    alone(pool, passed)
                    if fast:
                        nc.gpsimd.dma_start(dtile(pruned_d, T), pr[:, i, :]).then_inc(pr_out, 16)
                    else:
                        nc.gpsimd.dma_start(dtile(prunedf_d, T), logits[:, i, :]).then_inc(pr_out, 16)
                    pool.wait_ge(pr_out, 16 * (lay * NT + T.t + 1))
                    pool.sem_inc(pr_sent, 1)
                loop(pool, 0, NT, store)

                reduce_over_partitions(2, RMAX)
                reduce_over_partitions(3, RADD)
                stage(1)

            paths(pool, layer)

        @block.scalar
        def _(act):
            act.wait_ge(ln_v, 1)
            nc.scalar.activation(ywt[:, :, :], xcur[:, :, :], ACT.Square).then_inc(ln_sq, 1)
            act.wait_ge(ln_v, 2)
            nc.scalar.activation(xsq[:, :], xsq[:, :], ACT.Sqrt).then_inc(ln_sq, 1)

            def count_edges(T):
                act.wait_ge(row_byte, T.t + 1)
                act.wait_ge(row_count, T.t + 3)
                nc.scalar.activation(prT[:, T.mod(2), :], slots[:, T.mod(UNROLL), :], ACT.Copy,
                                     accum_out=node(edges_n, T)).then_inc(row_count, 1)
            loop(act, 0, NT, count_edges)

            def layer(fast, lay):
                fulls = lay * (2 * NT)

                act.wait_ge(xT_ps, lay + 1)
                nc.scalar.copy(xTa[0:D, :].rearrange("p (a two c) -> p a two c", two=2, c=P)[:, :, 1, :],
                               ps[D:P, 0:4, :].rearrange("p b (a c) -> p (b a) c", c=P)).then_inc(xT_odd, 1)
                for n in range(NT // 2):
                    act.wait_ge(all_ps, (NT // 2) * lay + n + 1)
                    nc.scalar.copy(x_all[:, 2 * n:2 * n + 2, :],
                                   ps[:, n % 4, 0:2 * D3].rearrange("p (a c) -> p a c", a=2)).then_inc(all_a, 1)
                act.wait_ge(all_a, (NT // 2) * (lay + 1) + 4)
                nc.scalar.activation(tmp[:, 2], x_all[:, :, 0:D], ACT.Square).then_inc(squares, 1)
                nc.scalar.activation(tmp[:, 3], xcur[:, :, :], ACT.Square).then_inc(squares, 1)

                def root(n, dst, src):
                    act.wait_ge(root_in, 3 * lay + n + 1)
                    nc.scalar.activation(dst, src, ACT.Sqrt).then_inc(root_out, 1)

                def node_exp(n):
                    act.wait_ge(sm_in, 2 * lay + n + 1)
                    nc.scalar.activation(ex[:, :], imp[:, :], ACT.Exp, bias=red[:, 4 + 2 * n:5 + 2 * n],
                                         accum_out=red[:, 2 * n + 1:2 * n + 2]).then_inc(sm_out, 1)

                root(0, halfst[:, :], halfst[:, :])
                copy_turned(act, nc.scalar.copy, lay, 0)

                def row_exp(T, phase):
                    i, n = T.mod(2), fulls + phase * NT + T.t
                    act.wait_ge(nmax_ready, n + 1 + UNROLL)
                    act.wait_ge(e_used, n + 1)
                    if fast and phase:
                        nc.scalar.activation(gap_exp[:, i:i + 1], nmx[:, i:i + 1], ACT.Exp)
                    nc.scalar.activation(expo[:, i, :], logits[:, i, :], ACT.Exp, bias=nmx[:, i:i + 1],
                                         accum_out=rsum[:, i:i + 1]).then_inc(exp_done, 1)

                def attention(T):
                    row_exp(T, 0)
                    if fast:
                        act.wait_ge(gaps_sent, lay * NT + T.t + 1)
                        nc.scalar.activation(pr[:, T.mod(2), 0:HALF], slots[:, T.mod(UNROLL), 0:HALF], ACT.Copy,
                                             bias=NO_EDGE, scale=-NO_EDGE / EDGE_BYTE).then_inc(gaps_a, 1)
                loop(act, 0, NT, attention)
                act.wait_ge(e_used, fulls + NT + 2)
                act.wait_ge(col_zero, lay + 1)
                for g in range(0, 4, 2):
                    copy_column_sums(nc.scalar.copy, g).then_inc(col_read_a, 1)
                node_exp(0)
                root(1, fmag[:, :], fmag[:, :])
                copy_turned(act, nc.scalar.copy, lay, 1)

                def copy_pruned(T, back):
                    i = (T.first - back) % 2
                    t = T.t - back
                    act.wait_ge(tr_done, lay * NT + t + 3)
                    act.wait_ge(prT_out, 16 * (lay * NT + t + 1))
                    act.wait_ge(count_ps, lay * NT + t + 1)
                    nc.scalar.copy(prT[:, i, :].bitcast(U16), ps[:, 6:8, :].rearrange("p a c -> p (a c)").bitcast(U16)
                                   ).then_inc(ev_done, 1)

                if fast:
                    loop(act, 0, 3, lambda T: row_exp(T, 1))

                    def both(T):
                        copy_pruned(T, 3)
                        row_exp(T, 1)
                    loop(act, 3, NT, both)
                    for t in range(NT, NT + 3):
                        copy_pruned(Tile(t, 0), 3)
                else:
                    loop(act, 0, NT, lambda T: row_exp(T, 1))
                node_exp(1)
                root(2, dvs[:, :], dvs[:, :])

                def message(T):
                    i = T.mod(2)
                    act.wait_ge(msg_sum, lay * NT + T.t + 1 + UNROLL)
                    nc.scalar.activation(xcur[:, ds(T.t, 1), :].rearrange("p a d -> p (a d)"), msum[:, i, :],
                                         ACT.Relu, scale=node(dvout, T)).then_inc(msg_out, 1)
                loop(act, 0, NT, message)

            paths(act, layer)

        @block.vector
        def _(dve):
            step = Order(dve, dve_pre)

            def per_node(a):
                return a.unsqueeze(2).to_broadcast([P, a.shape[1], D])

            dve.wait_ge(x_in, 16)
            step(nc.vector.tensor_reduce(xsq[:, :], xcur[:, :, :], AX_X, ALU.add))
            step(nc.vector.tensor_scalar(xsq[:, :], xsq[:, :], 1.0 / D, None, ALU.mult))
            nc.vector.tensor_tensor(xcur[:, :, :], xcur[:, :, :], per_node(xsq[:, :]), ALU.subtract).then_inc(ln_v, 1)
            dve.wait_ge(ln_sq, 1)
            step(nc.vector.tensor_reduce(xsq[:, :], ywt[:, :, :], AX_X, ALU.add))
            nc.vector.tensor_scalar(xsq[:, :], xsq[:, :], 1.0 / D, LN_EPS, ALU.mult, ALU.add).then_inc(ln_v, 1)
            dve.wait_ge(ln_sq, 2)
            step(nc.vector.reciprocal(xsq[:, :], xsq[:, :]))
            step(nc.vector.tensor_tensor(xcur[:, :, :], xcur[:, :, :], per_node(xsq[:, :]), ALU.mult))
            nc.vector.tensor_scalar(xcur[:, :, :], xcur[:, :, :], 0.0, None, ALU.max).then_inc(ln_x, 1)
            dve.wait_ge(wtheta_ps, 1)
            nc.vector.tensor_copy(wT[:, :], ps[0:D, 1, 0:D]).then_inc(wtheta_in, 1)
            dve.wait_ge(wtheta_ps, 2)
            nc.vector.tensor_copy(w_all[0:D, 3 * D:4 * D], ps[0:D, 0, 0:D]).then_inc(wtheta_in, 1)

            dve.wait_ge(value_in, 16)

            def edge_bytes(T):
                i = T.mod(UNROLL)
                dve.wait_ge(row_in[i], 16 * (T.div(UNROLL) + 1))
                dve.wait_ge(row_chk, T.t + 1)
                dve.wait_ge(edges_sent, T.t + 1)
                dve.wait_ge(row_count, T.t + 1)
                nc.vector.tensor_scalar(slots[:, i, :], rows4[i], value[:, 0:1], EDGE_BYTE,
                                        ALU.is_equal, ALU.mult).then_inc(row_byte, 1)
                nc.vector.tensor_scalar(marks[:, T.mod(2), :], rows4[i], 0.0, None,
                                        ALU.not_equal).then_inc(row_mark, 1)
            loop(dve, 0, NT, edge_bytes)
            dve.wait_ge(row_chk, NT + 2)
            dve.wait_ge(row_count, NT + UNROLL)
            step(nc.vector.tensor_scalar(gaps_n[:, :], edges_n[:, :], -1.0 / EDGE_BYTE, float(N), ALU.mult, ALU.add))
            step(nc.vector.tensor_scalar(zero_bound[:, :], gaps_n[:, :], 0.0, 3.0e38, ALU.is_equal, ALU.mult))
            step(nc.vector.tensor_reduce(value[:, 1:2], ps[:, :, :].rearrange("p a c -> p (a c)"), AX_X, ALU.min))
            step(nc.vector.tensor_scalar(value[:, 1:2], value[:, 1:2], 0.0, None, ALU.is_equal))
            step(nc.vector.tensor_scalar(value[:, 2:3], value[:, 0:1], LEAST_VALUE, None, ALU.is_ge))
            step(nc.vector.tensor_scalar(value[:, 3:4], value[:, 0:1], MOST_VALUE, None, ALU.is_le))
            step(nc.vector.tensor_tensor(value[:, 1:2], value[:, 1:2], value[:, 2:3], ALU.mult))
            step(nc.vector.tensor_tensor(value[:, 1:2], value[:, 1:2], value[:, 3:4], ALU.mult))
            step(nc.vector.tensor_copy(th_cur[:, :], th_all[:, 0:1]))
            nc.vector.tensor_copy(flag[:, :], value[:, 1:2]).then_inc(flag_set, 1)

            def layer(fast, lay):
                fulls = lay * (2 * NT)
                halves = lay * (4 * NT)
                step = Order(dve, dve_step, lay * DVE_STEPS)

                def split(src, first, second, third, rest):
                    step(nc.vector.tensor_copy(first, src))
                    step(nc.vector.tensor_tensor(rest, src, first, ALU.subtract))
                    step(nc.vector.tensor_copy(second, rest))
                    step(nc.vector.tensor_tensor(third, rest, second, ALU.subtract))

                def split_to_parts(src, half):
                    these = slice(half * NT // 2, (half + 1) * NT // 2)
                    split(src[:, these], parts[:, these, 0:D], parts[:, these, D:2 * D], parts[:, these, 2 * D:D3],
                          tmp[:, 0, these])
                    dve.sem_inc(parts_ready, 1)

                def planes_of(phase, h):
                    def one(T):
                        k = (2 * phase + h) * NT
                        n = halves + k + T.t
                        i = T.mod(2)
                        g = gtile[:, i * HALF:(i + 1) * HALF]
                        own = Order(dve, g_step, 4 * n)
                        dve.wait_ge(g_half_in[i], 16 * (lay * (2 * NT) + k // 2 + T.div(2) + 1))
                        dve.wait_ge(half_used, n + UNROLL)
                        own(nc.vector.tensor_copy(planes[:, 0, :], g))
                        own(nc.vector.tensor_tensor(g, g, planes[:, 0, :], ALU.subtract))
                        own(nc.vector.tensor_copy(planes[:, 1, :], g))
                        own(nc.vector.tensor_tensor(g, g, planes[:, 1, :], ALU.subtract))
                        nc.vector.tensor_copy(planes[:, 2, :], g).then_inc(g_planes, 1)
                        dve.wait_ge(g_planes, n + 1)
                        dve.sem_inc(g_half_free, 1)
                    loop(dve, 0, NT, one)

                def sums_of_sweep(phase, h, dst):
                    dve.wait_ge(sweep_ps, 4 * lay + 2 * phase + h + 1)
                    blocks = ps[:, :, :].rearrange("p b (u c) -> p (b u) c", u=2)
                    n = 8 * lay + 4 * phase + 2 * h
                    if phase:
                        step(nc.vector.tensor_scalar(fac[:, :], blocks[:, :, D3], gsc[:, SC_D:SC_D + 1], DEG_EPS,
                                                     ALU.mult, ALU.max))
                    for q in range(2):
                        these = slice(q * JB // 2, (q + 1) * JB // 2)
                        nc.vector.tensor_reduce(dst[:, these], blocks[:, these, 0:D3]
                                                .rearrange("p b (k d) -> p b d k", k=3),
                                                AX_X, ALU.add).then_inc(sweep_read, 1)
                    dve.wait_ge(sweep_read, n + 2)
                    if phase:
                        step(nc.vector.reciprocal(fac[:, :], fac[:, :]))
                        step(nc.vector.tensor_scalar(fac[:, :], fac[:, :], gsc[:, SC_D:SC_D + 1], None, ALU.mult))
                        step(nc.vector.tensor_tensor(dst, dst, per_node(fac[:, :]), ALU.mult))

                def norm_root(n, a):
                    nc.vector.tensor_scalar(a, a, NORM_FLOOR if n < 2 else DEG_EPS, None,
                                            ALU.max).then_inc(root_in, 1)
                    dve.wait_ge(root_out, 3 * lay + n + 1)

                def node_softmax(n):
                    nc.vector.tensor_reduce(red[:, 2 * n:2 * n + 1], imp[:, :], AX_X, ALU.max).then_inc(red_in, 1)
                    dve.wait_ge(red_out, 4 * lay + 2 * n + 1)
                    nc.vector.tensor_scalar(red[:, 4 + 2 * n:5 + 2 * n], red[:, 4 + 2 * n:5 + 2 * n], -1.0, None,
                                            ALU.mult).then_inc(sm_in, 1)
                    dve.wait_ge(sm_out, 2 * lay + n + 1)
                    dve.sem_inc(red_in, 1)
                    dve.wait_ge(red_out, 4 * lay + 2 * n + 2)
                    step(nc.vector.tensor_tensor(red[:, 5 + 2 * n:6 + 2 * n], red[:, 5 + 2 * n:6 + 2 * n],
                                                 th_cur[:, :], ALU.mult))
                    return red[:, 5 + 2 * n:6 + 2 * n]

                if fast:
                    step(nc.vector.tensor_tensor(gsc[:, SC_B:SC_B + 1], value[:, 0:1], value[:, 0:1], ALU.mult))
                    step(nc.vector.tensor_scalar(gsc[:, SC_B:SC_B + 1], gsc[:, SC_B:SC_B + 1],
                                                 D ** -0.5 / EDGE_BYTE / EDGE_FP8, None, ALU.mult))
                    step(nc.vector.tensor_scalar(gsc[:, SC_C:SC_C + 1], value[:, 0:1], 1.0 / EDGE_BYTE, None,
                                                 ALU.mult))
                    step(nc.vector.tensor_scalar(gsc[:, SC_D:SC_D + 1], value[:, 0:1], 1.0 / EDGE_FP8, None,
                                                 ALU.mult))
                else:
                    step(nc.vector.memset(gsc[:, SC_B:SC_B + 1], D ** -0.5))
                    step(nc.vector.memset(gsc[:, SC_C:SC_C + 1], 1.0))
                    step(nc.vector.memset(gsc[:, SC_D:SC_D + 1], 1.0))
                    step(nc.vector.memset(gsc[:, 3:4], 1.0))

                dve.wait_ge(xT_ps, lay + 1)
                nc.vector.tensor_copy(xTa[0:D, :].rearrange("p (a two c) -> p a two c", two=2, c=P)[:, :, 0, :],
                                      ps[0:D, 0:4, :].rearrange("p b (a c) -> p (b a) c", c=P)).then_inc(xT_even, 1)
                dve.wait_ge(v_ps, lay + 1)
                for half in range(2):
                    split_to_parts(xWv, half)
                dve.wait_ge(squares, 2 * lay + 2)
                step(nc.vector.tensor_reduce(halfst[:, :], tmp[:, 2], AX_X, ALU.add))
                step(nc.vector.tensor_reduce(xsq[:, :], tmp[:, 3], AX_X, ALU.add))
                dve.wait_ge(all_a, (NT // 2) * (lay + 1) + 4)
                norm_root(0, halfst[:, :])
                step(nc.vector.tensor_scalar(halfst[:, :], halfst[:, :], 0.5, None, ALU.mult))
                step(nc.vector.tensor_copy(ywt[:, :, :], x_all[:, :, 2 * D:D3]))
                split(x_all[:, :, D:2 * D], q_pairs[:, :, 0], q_pairs[:, :, 2], tail_pair[:, :, 0], tmp[:, 0])
                step(nc.vector.tensor_copy(q_pairs[:, :, 1], q_pairs[:, :, 0]))
                step(nc.vector.tensor_copy(q_pairs[:, :, 3], q_pairs[:, :, 2]))
                step(nc.vector.tensor_copy(tail_pair[:, :, 1], q_pairs[:, :, 0]))
                dve.sem_inc(src_ready, 1)

                def split_to_parts2(h):
                    these = slice(h * JB, (h + 1) * JB)
                    split(tmp[:, 1, 0:JB, :], slots2[:, these, 2], slots2[:, these, 3], slots2[:, these, 1],
                          tmp[:, 0, 0:JB, :])
                for h in range(2):
                    if not fast:
                        planes_of(0, h)
                    sums_of_sweep(0, h, tmp[:, 1, 0:JB, :])
                    split_to_parts2(h)
                    step(nc.vector.tensor_copy(slots2[:, h * JB:(h + 1) * JB, 0], slots2[:, h * JB:(h + 1) * JB, 2]))
                dve.sem_inc(parts2_ready, 1)
                copy_turned(dve, nc.vector.tensor_copy, lay, 0)

                def adjacency(T):
                    return slots[:, T.mod(UNROLL), :] if fast else gtile

                def mask_rows(T, phase, between=()):
                    i, k = T.mod(2), phase * NT
                    factor = value[:, 0:1] if fast and phase else gsc[:, phase:phase + 1]
                    if fast:
                        dve.wait_ge(full_in[T.mod(UNROLL)], 16 * (lay * (2 * NT // UNROLL) + k // UNROLL + T.div(UNROLL) + 1))
                    else:
                        dve.wait_ge(g_full_in, 16 * (lay * (3 * NT) + k + T.t + 1))
                        if phase:
                            dve.wait_ge(pr_sent, lay * NT + T.t + 1)
                    dve.wait_ge(exp_done, fulls + k + T.t + 1)
                    for c in range(NC):
                        n = NC * (fulls + k + T.t) + c
                        dve.wait_ge(qk_ready, n + 1)
                        alone(dve, passed)
                        nc.vector.tensor_tensor_reduce(
                            logits[:, i, c * CW:(c + 1) * CW],
                            ps[:, 2 * (c % 2):2 * (c % 2) + 2, :].rearrange("p a n -> p (a n)"),
                            adjacency(T)[:, c * CW:(c + 1) * CW], factor, -3.0e38,
                            ALU.subtract if fast and phase else ALU.mult, ALU.max, mx[:, i, c:c + 1]).then_inc(qk_used, 1)
                        if between and c == NC - 2:
                            between[0]()
                    dve.wait_ge(qk_used, NC * (fulls + k + T.t + 1) + 2)
                    if fast and phase:
                        nc.vector.tensor_reduce(emx[:, i:i + 1], mx[:, i, :], AX_X, ALU.max, negate=True
                                                ).then_inc(max_ready, 1)
                        if between:
                            between[1]()
                        dve.wait_ge(max_ready, lay * NT + T.t + 1)
                        nc.vector.tensor_scalar(nmx[:, i:i + 1], emx[:, i:i + 1], node(zero_bound, T), None, ALU.min
                                                ).then_inc(nmax_ready, 1)
                        if between:
                            between[2]()
                    else:
                        nc.vector.tensor_reduce(nmx[:, i:i + 1], mx[:, i, :], AX_X, ALU.max, negate=True
                                                ).then_inc(nmax_ready, 1)

                def inverse_sum(T, back):
                    i, t = (T.first - back) % 2, T.t - back
                    dve.wait_ge(exp_done, fulls + t + 3)
                    nc.vector.reciprocal(rinv[:, i:i + 1], rsum[:, i:i + 1]).then_inc(rinv_ready, 1)

                def gap_bytes(T):
                    if fast:
                        dve.wait_ge(gaps_sent, lay * NT + T.t + 1)
                        nc.vector.tensor_scalar(pr[:, T.mod(2), HALF:N], slots[:, T.mod(UNROLL), HALF:N],
                                                -NO_EDGE / EDGE_BYTE, NO_EDGE, ALU.mult, ALU.add
                                                ).then_inc(gaps_v, 1)
                mask_rows(Tile(0, 0), 0)
                gap_bytes(Tile(0, 0))

                def attention(T):
                    mask_rows(T, 0)
                    inverse_sum(T, 1)
                    gap_bytes(T)
                loop(dve, 1, NT, attention)
                inverse_sum(Tile(NT, 0), 1)

                dve.wait_ge(e_used, fulls + NT + 2)
                dve.wait_ge(col_zero, lay + 1)
                for g in range(1, 4, 2):
                    copy_column_sums(nc.vector.tensor_copy, g).then_inc(col_read_v, 1)

                dve.wait_ge(att_ps, lay + 1)
                step(nc.vector.tensor_scalar(imp[:, :].rearrange("p (b g r) -> p b r g", b=2, g=4),
                                             ps[:, 0, 0:NT].rearrange("p (b r g) -> p b r g", b=2, g=4),
                                             0.5 / N, None, ALU.mult))
                step(nc.vector.tensor_tensor(imp[:, :], imp[:, :], halfst[:, :], ALU.add))
                bound = node_softmax(0)
                step(nc.vector.tensor_scalar(cmask[:, :], ex[:, :], bound, None, ALU.is_ge))
                step(nc.vector.tensor_scalar(never[:, :], cmask[:, :], -NEVER, NEVER, ALU.mult, ALU.add))
                step(nc.vector.tensor_tensor(fmag[:, :], xsq[:, :], cmask[:, :], ALU.mult))
                norm_root(1, fmag[:, :])
                step(nc.vector.tensor_scalar(rnrm[:, :], fmag[:, :], NORM_MIN, None, ALU.max))
                step(nc.vector.reciprocal(rnrm[:, :], rnrm[:, :]))
                step(nc.vector.tensor_tensor(rnrm[:, :], rnrm[:, :], cmask[:, :], ALU.mult))
                step(nc.vector.tensor_tensor(tmp[:, 1], xcur[:, :, :], per_node(rnrm[:, :]), ALU.mult))
                def twice(pair, a):
                    step(nc.vector.tensor_copy(pair, a.unsqueeze(2).to_broadcast([P, NT, 2, D])))
                    dve.sem_inc(src_ready, 1)
                step(nc.vector.tensor_copy(slots2[:, :, 0], tmp[:, 1]))
                twice(tail_pair, slots2[:, :, 0])
                step(nc.vector.tensor_tensor(tmp[:, 0], tmp[:, 1], slots2[:, :, 0], ALU.subtract))
                step(nc.vector.tensor_copy(slots2[:, :, 3], tmp[:, 0]))
                twice(parts_pair, slots2[:, :, 3])
                step(nc.vector.tensor_tensor(slots2[:, :, 1], tmp[:, 0], slots2[:, :, 3], ALU.subtract))
                step(nc.vector.tensor_copy(slots2[:, :, 2], slots2[:, :, 0]))
                dve.sem_inc(src_ready, 1)
                copy_turned(dve, nc.vector.tensor_copy, lay, 1)

                def gaps_to_sum(T, back):
                    i, t = (T.first - back) % 2, T.t - back
                    dve.wait_ge(exp_done, fulls + NT + t + 3)
                    if fast:
                        nc.vector.tensor_scalar(whole_sum[:, i:i + 1], gap_exp[:, i:i + 1],
                                                node(gaps_n, Tile(T.first - back, T.q)),
                                                rsum[:, i:i + 1], ALU.mult, ALU.add).then_inc(sum_ready, 1)

                def row_threshold(T, back):
                    i, t = (T.first - back) % 2, T.t - back
                    if fast:
                        dve.wait_ge(sum_ready, lay * NT + t + 1)
                    total = whole_sum if fast else rsum
                    nc.vector.tensor_scalar(thr[:, i:i + 1], total[:, i:i + 1], th_cur[:, 0:1],
                                            node(never, Tile(T.first - back, T.q)),
                                            ALU.mult, ALU.add).then_inc(thr_ready, 1)

                def keep_edges(T, back):
                    i, t = (T.first - back) % 2, T.t - back
                    dve.wait_ge(thr_ready, lay * NT + t + 1)
                    if fast:
                        dve.wait_ge(tr_done, lay * NT + t + 1)
                        dve.wait_ge(pr_sent, lay * NT + t + 1)
                        nc.vector.tensor_scalar(pr[:, i, :], expo[:, i, :], thr[:, i:i + 1], EDGE_BYTE,
                                                ALU.is_ge, ALU.mult).then_inc(e_used, 1)
                    else:
                        nc.vector.scalar_tensor_tensor(out=logits[:, i, :], in0=expo[:, i, :],
                                                       scalar=thr[:, i:i + 1], in1=gtile, op0=ALU.is_ge,
                                                       op1=ALU.mult, accum_out=node(conn, Tile(T.first - back, T.q))
                                                       ).then_inc(e_used, 1)

                def prune(T, back):
                    gaps_to_sum(T, back)
                    row_threshold(T, back)
                    keep_edges(T, back)

                def mask_and_prune(T):
                    mask_rows(T, 1, [lambda: gaps_to_sum(T, 1), lambda: row_threshold(T, 1),
                                     lambda: keep_edges(T, 1)])

                def keep_count(T, back):
                    then = Tile(T.first - back, T.q)
                    dve.wait_ge(count_ps, lay * NT + then.t + 3)
                    nc.vector.tensor_scalar(node(conn, then), ps[:, 4 + then.mod(2), 0:1],
                                            EDGE_BYTE, None, ALU.mult).then_inc(count_read, 1)

                if fast:
                    mask_rows(Tile(0, 0), 1)
                    for t in range(1, 4):
                        mask_and_prune(Tile(t, 0))

                    def cosines(T):
                        mask_and_prune(T)
                        keep_count(T, 4)
                    loop(dve, 4, NT, cosines)
                    prune(Tile(NT, 0), 1)
                    for t in range(NT, NT + 4):
                        keep_count(Tile(t, 0), 4)
                    dve.wait_ge(count_read, (lay + 1) * NT + 2)
                else:
                    def cosines(T):
                        mask_rows(T, 1)
                        prune(T, 0)
                    loop(dve, 0, NT, cosines)
                dve.wait_ge(e_used, fulls + 2 * NT + 2)

                step(nc.vector.tensor_scalar(conn[:, :], conn[:, :], gsc[:, SC_C:SC_C + 1], None, ALU.mult))
                step(nc.vector.tensor_tensor(imp[:, :], conn[:, :], fmag[:, :], ALU.mult))
                bound = node_softmax(1)
                step(nc.vector.tensor_scalar(nmask[:, :], ex[:, :], bound, None, ALU.is_ge))
                step(nc.vector.tensor_scalar(imp[:, :], conn[:, :], 0.0, None, ALU.is_gt))
                step(nc.vector.tensor_tensor(nmask[:, :], nmask[:, :], imp[:, :], ALU.mult))
                step(nc.vector.tensor_tensor(nmask[:, :], nmask[:, :], cmask[:, :], ALU.mult))
                step(nc.vector.tensor_copy(dvs[:, :], conn[:, :]))
                norm_root(2, dvs[:, :])
                step(nc.vector.reciprocal(dvs[:, :], dvs[:, :]))
                step(nc.vector.tensor_scalar(dvout[:, :], dvs[:, :], gsc[:, SC_D:SC_D + 1], None, ALU.mult))
                step(nc.vector.tensor_tensor(nmask[:, :], nmask[:, :], dvs[:, :], ALU.mult))
                for half in range(2):
                    these = slice(half * NT // 2, (half + 1) * NT // 2)
                    step(nc.vector.tensor_tensor(tmp[:, 1, these], ywt[:, these, :], per_node(nmask[:, these]),
                                                 ALU.mult))
                    split_to_parts(tmp[:, 1], half)
                step(nc.vector.tensor_copy(th_cur[:, :], th_all[:, LAYERS - 1:LAYERS]))

                for h in range(2):
                    if not fast:
                        planes_of(1, h)
                    sums_of_sweep(1, h, tmp[:, 1, 0:JB, :])
                    split_to_parts2(h)
                dve.sem_inc(parts2_ready, 1)

                def add_parts(T):
                    if not fast:
                        def group(b):
                            n = 8 * (lay * NT + T.t) + b
                            own = Order(dve, g_step_t, 4 * n)
                            dve.wait_ge(g_turned, n + 1)
                            own(nc.vector.tensor_copy(planesT[:, 0, :], ps[:, 7, :]))
                            own(nc.vector.tensor_tensor(blkT, ps[:, 7, :], planesT[:, 0, :], ALU.subtract))
                            own(nc.vector.tensor_copy(planesT[:, 1, :], blkT))
                            own(nc.vector.tensor_tensor(blkT, blkT, planesT[:, 1, :], ALU.subtract))
                            nc.vector.tensor_copy(planesT[:, 2, :], blkT).then_inc(g_split, 1)
                            dve.wait_ge(g_split, n + 1)
                        for b in range(8):
                            group(b)
                    i = T.mod(2)
                    dve.wait_ge(e_tile, lay * NT + T.t + 1 + UNROLL)
                    dve.wait_ge(msg_out, lay * NT + T.t + 1)
                    nc.vector.tensor_reduce(msum[:, i, :], ps[:, T.mod(UNROLL), 0:D3]
                                            .rearrange("p (k d) -> p d k", k=3), AX_X, ALU.add).then_inc(msg_sum, 1)
                loop(dve, 0, NT, add_parts)
                assert step.n == DVE_STEPS, step.n

            paths(dve, layer)
            dve.wait_ge(x_again, 16)
            nc.vector.tensor_tensor(tmp[:, 1], tmp[:, 0], xcur[:, :, :], ALU.add).then_inc(y_ready, 1)

        @block.tensor
        def _(pe):
            pe.wait_ge(consts, 8 + LAYERS)
            pe.wait_ge(tables_in, 16 * 6)
            nc.tensor.transpose(ps[0:D, 1, 0:D], w_all[0:D, D:2 * D], ident_f[0:D, 0:D]).then_inc(wtheta_ps, 1)
            pe.wait_ge(wtheta_in, 1)
            nc.tensor.matmul(ps[0:D, 0, 0:D], wT[:, :], theta_s[:, :], start=True, stop=True).then_inc(wtheta_ps, 1)
            pe.wait_ge(wtheta_in, 2)

            def clear(banks):
                for b in banks:
                    nc.tensor.matmul(ps[:, b, :], zeros[:, 0:P], zeros[:, :], start=True, stop=False,
                                     skip_group_check=True)

            clear(range(8))

            def compare(T):
                pe.wait_ge(row_mark, T.t + 1 + UNROLL)
                alone(pe, passed)
                for b in range(8):
                    cols = slice(b * BANK, (b + 1) * BANK)
                    nc.tensor.matmul(ps[:, b, :], half_ones[:, :], slots[:, T.mod(UNROLL), cols].bitcast(FP8),
                                     start=False, stop=False, skip_group_check=True)
                for b in range(8):
                    cols = slice(b * BANK, (b + 1) * BANK)
                    last = nc.tensor.matmul(ps[:, b, :], neg_ones[:, :], marks[:, T.mod(2), cols],
                                            start=False, stop=False, skip_group_check=True)
                last.then_inc(row_chk, 1)
            loop(pe, 0, NT, compare)

            def layer(fast, lay):
                fulls = lay * (2 * NT)
                halves = lay * (4 * NT)

                def sweep(phase, h, columns):
                    width = DS if phase else D3
                    for four in range(2):
                        if h:
                            pe.wait_ge(sweep_read, 8 * lay + 4 * phase + four + 1)
                        clear(range(4 * four, 4 * four + 4))

                    def one(T):
                        k = (2 * phase + h) * NT
                        n = halves + k + T.t
                        i = T.mod(UNROLL)
                        if fast:
                            pe.wait_ge(half_in[i], 16 * (lay * NT + k // UNROLL + T.div(UNROLL) + 1))
                            weights = [ring_h[:, i, :].bitcast(FP8)]
                        else:
                            pe.wait_ge(g_planes, n + 1)
                            weights = [planes[:, m, :] for m in range(3)]
                        pe.wait_ge(staged_in, n + 1)
                        alone(pe, passed)
                        for j in range(JB):
                            for w in weights:
                                last = nc.tensor.matmul(ps[:, j // 2, 256 * (j % 2):256 * (j % 2) + width],
                                                        columns(w, j), staged[:, i, 0:width], start=False,
                                                        stop=False, skip_group_check=True)
                        last.then_inc(half_used, 1)
                    loop(pe, 0, NT, one)
                    nc.tensor.matmul(ps[:, 7, :], zeros[:, 0:P], zeros[:, :], start=False, stop=True,
                                     skip_group_check=True).then_inc(sweep_ps, 1)

                def turn_sides(side):
                    if side:
                        sources = (tail_pair, parts_pair, slots2[:, :, 1:3], slots2[:, :, 2:4], slots2[:, :, 0:2])
                    else:
                        sources = (q_pairs[:, :, 0:2], q_pairs[:, :, 2:4], tail_pair, slots2[:, :, 2:4],
                                   slots2[:, :, 0:2])
                    mine = {True: 0, False: 0}
                    for n, (kind, a, by_act) in enumerate(turn_plan(side)):
                        if a == 0:
                            if side and kind <= LEFT3:
                                pe.wait_ge(src_ready, 4 * lay + 2 + kind)
                            if not side and kind == RIGHT1:
                                pe.wait_ge(parts2_ready, 2 * lay + 1)
                        per, ready, done = (TURNS_A, turned_a, turn_a) if by_act else (TURNS_V, turned_v, turn_v)
                        bank = (0 if by_act else 4) + mine[by_act] % 4
                        pe.wait_ge(done, lay * sum(per) + side * per[0] + mine[by_act] + 1)
                        mine[by_act] += 1
                        for i in range(4):
                            two = sources[kind][:, 4 * a + i].rearrange("p k d -> p (k d)")
                            last = nc.tensor.matmul(ps[:, bank, i * P:(i + 1) * P], two, ident_b[:, :],
                                                    start=(i == 0), stop=True, skip_group_check=True)
                        last.then_inc(ready, 1)
                    pe.wait_ge(turn_v, lay * sum(TURNS_V) + sum(TURNS_V[0:side + 1]) + 4)
                    pe.wait_ge(turn_a, lay * sum(TURNS_A) + sum(TURNS_A[0:side + 1]) + 4)

                def row_logits(T, phase, between=None):
                    for c in range(NC):
                        if c == NC // 2 and between:
                            between(T)
                        n = NC * (fulls + phase * NT + T.t) + c
                        pe.wait_ge(qk_used, n + 1)
                        for m, rhs in enumerate((rhs_a, rhs_a, rhs_b)):
                            for b in range(2):
                                last = nc.tensor.matmul(
                                    ps[:, 2 * (c % 2) + b, :], stat[:, ds(T.t, 1), m, :].rearrange("p a c -> p (a c)"),
                                    rhs[:, c * CW + b * BANK:c * CW + (b + 1) * BANK], start=(m == 0), stop=(m == 2))
                        last.then_inc(qk_ready, 1)

                def column_sums(T, back):
                    i, t = (T.first - back) % 2, T.t - back
                    pe.wait_ge(rinv_ready, lay * NT + t + 1)
                    for j in range(8):
                        g = j % 4
                        last = nc.tensor.matmul(ps[32 * g:32 * g + 1, 4 + j // 4, :], rinv[:, i:i + 1],
                                                expo[:, i, j * BANK:(j + 1) * BANK], start=False, stop=False,
                                                skip_group_check=True)
                    last.then_inc(e_used, 1)

                def count_pruned(T, back):
                    i, t = (T.first - back) % 2, T.t - back
                    pe.wait_ge(ev_done, lay * NT + t + 2)
                    pe.wait_ge(count_read, lay * NT + t + 1)
                    alone(pe, passed)
                    blocks = prT[:, i, :].bitcast(FP8).rearrange("p (g a k) -> p g a k", g=WG, k=4)
                    for j in range(NT):
                        last = nc.tensor.matmul(ps[:, 4 + i, 0:1], blocks[:, j // 4, :, j % 4],
                                                half_ones[:, 0:1], start=(j == 0), stop=(j == NT - 1))
                    last.then_inc(count_ps, 1)

                def turn_pruned(T, back):
                    i, t = (T.first - back) % 2, T.t - back
                    pe.wait_ge(e_used, fulls + NT + t + 3)
                    pe.wait_ge(ev_done, lay * NT + t + 1)
                    words = pr[:, i, :].bitcast(F32)
                    for g in range(WG):
                        last = nc.tensor.transpose(ps[:, 6 + g // 4, P * (g % 4):P * (g % 4) + P],
                                                   words[:, g * P:(g + 1) * P], ident_f[:, :])
                    last.then_inc(tr_done, 1)

                pe.wait_ge(ln_x, 1)
                pe.wait_ge(msg_out, lay * NT + 2)
                for s in range(NT // 2):
                    last = nc.tensor.transpose(ps[:, s // 4, P * (s % 4):P * (s % 4) + P],
                                               xcur[:, 2 * s:2 * s + 2, :].rearrange("p a d -> p (a d)"),
                                               ident_f[:, :])
                last.then_inc(xT_ps, 1)
                pe.wait_ge(xT_even, lay + 1)
                pe.wait_ge(xT_odd, lay + 1)
                pe.wait_ge(xT_one, lay + 1)
                for t in range(NT):
                    last = nc.tensor.matmul(xWv[:, t, :], xTa[:, t * P:(t + 1) * P], w_all[:, 0:D],
                                            start=(t % 8 == 0), stop=True, skip_group_check=True)
                last.then_inc(v_ps, 1)
                for n in range(NT // 2):
                    pe.wait_ge(all_a, (NT // 2) * lay + n + 1)
                    for i in range(2):
                        t = 2 * n + i
                        last = nc.tensor.matmul(ps[:, n % 4, D3 * i:D3 * (i + 1)], xTa[:, t * P:(t + 1) * P],
                                                w_all[:, D:4 * D], start=(i == 0), stop=True, skip_group_check=True)
                    last.then_inc(all_ps, 1)
                pe.wait_ge(all_a, (NT // 2) * (lay + 1) + 4)
                pe.wait_ge(parts_ready, 4 * lay + 2)

                for h in range(2):
                    sweep(0, h, lambda w, j: w[:, j * P:(j + 1) * P])
                pe.wait_ge(sweep_read, 8 * lay + 3)
                pe.wait_ge(src_ready, 4 * lay + 1)
                turn_sides(0)

                clear((4, 5))
                for t in range(2):
                    row_logits(Tile(t, 0), 0)
                loop(pe, 2, NT, lambda T: row_logits(T, 0, lambda T: column_sums(T, 2)))
                for t in (NT, NT + 1):
                    column_sums(Tile(t, 0), 2)
                pe.wait_ge(qk_used, NC * (fulls + NT) + 2)
                pe.wait_ge(col_read_a, 2 * lay + 2)
                pe.wait_ge(col_read_v, 2 * lay + 2)
                for n in range(2 * BANK // P):
                    last = nc.tensor.matmul(ps[:, 0, 4 * n:4 * n + 4], col_row[:, n * P:(n + 1) * P],
                                            ident_f[:, 0:P:P // 4], start=(n == 0), stop=True,
                                            skip_group_check=True)
                last.then_inc(att_ps, 1)
                turn_sides(1)

                if fast:
                    def turn_and_count(T):
                        turn_pruned(T, 3)
                        count_pruned(T, 4)
                    for t in range(3):
                        row_logits(Tile(t, 0), 1)
                    row_logits(Tile(3, 0), 1, lambda T: turn_pruned(T, 3))

                    def cosines(T):
                        row_logits(T, 1, turn_and_count)
                    loop(pe, 4, NT, cosines)
                    for t in range(NT, NT + 3):
                        turn_and_count(Tile(t, 0))
                    count_pruned(Tile(NT + 3, 0), 4)
                    pe.wait_ge(ev_done, (lay + 1) * NT + 1)
                    pe.wait_ge(count_read, (lay + 1) * NT + 2)
                else:
                    loop(pe, 0, NT, lambda T: row_logits(T, 1))
                pe.wait_ge(qk_used, NC * (fulls + 2 * NT) + 2)

                def word_columns(w, j):
                    g, k = j // 4, j % 4
                    return w[:, 4 * P * g:4 * P * (g + 1)].rearrange("p (b k) -> p b k", k=4)[:, :, k]
                for h in range(2):
                    sweep(1, h, word_columns)
                pe.wait_ge(sweep_read, 8 * lay + 8)
                pe.wait_ge(parts2_ready, 2 * lay + 2)

                def messages(T):
                    i = T.mod(UNROLL)
                    pe.wait_ge(msg_sum, lay * NT + T.t + 1)
                    dst = ps[:, i, 0:D3]
                    if fast:
                        pe.wait_ge(turned_in[i], 16 * (lay * (NT // UNROLL) + T.div(UNROLL) + 1))
                        alone(pe, passed)
                        blocks = slots[:, i, :].bitcast(FP8).rearrange("p (g a k) -> p g a k", g=WG, k=4)
                        for j in range(NT):
                            last = nc.tensor.matmul(dst, blocks[:, j // 4, :, j % 4], parts2[:, j, D:4 * D],
                                                    start=(j == 0), stop=(j == NT - 1))
                    else:
                        pe.wait_ge(g_full_in, 16 * (lay * (3 * NT) + 2 * NT + T.t + 1))
                        for g in range(WG):
                            n = 8 * (lay * NT + T.t) + g
                            for k in range(4):
                                last = nc.tensor.transpose(ps[:, 7, k * P:(k + 1) * P], word_columns(gtile, 4 * g + k),
                                                           ident_f[:, :])
                            last.then_inc(g_turned, 1)
                            pe.wait_ge(g_split, n + 1)
                            for k in range(4):
                                for m in range(3):
                                    last = nc.tensor.matmul(dst, planesT[:, m, k * P:(k + 1) * P],
                                                            parts2[:, 4 * g + k, D:4 * D],
                                                            start=(g == 0 and k == 0 and m == 0),
                                                            stop=(g == WG - 1 and k == 3 and m == 2))
                    last.then_inc(e_tile, 1)
                loop(pe, 0, NT, messages)

            paths(pe, layer)


_INS = ["x", "adj", "L0_gnn_W", "L0_gnn_Theta", "L0_gnn_Wq", "L0_gnn_bq", "L0_gnn_Wv", "L0_gnn_bv"]
_OUTS = [((4096, 64), "float32")]


def kernel(**inputs):
    import numpy as _np
    import concourse.bacc as _bacc
    from concourse import mybir as _mybir
    from concourse.bass_utils import run_bass_kernel_spmd as _run

    nc = _bacc.Bacc("TRN2", target_bir_lowering=False, num_devices=1)
    arrays, args = {}, []
    for name in _INS:
        a = _np.ascontiguousarray(inputs[name])
        arrays[f"in_{name}_dram"] = a
        args.append(nc.dram_tensor(f"in_{name}_dram", a.shape, _mybir.dt.from_np(a.dtype), kind="ExternalInput").ap())
    for i, (shape, dtype) in enumerate(_OUTS):
        dt = _mybir.dt.from_np(_np.dtype(dtype))
        args.append(nc.dram_tensor(f"out_{i}_dram", shape, dt, kind="ExternalOutput").ap())
    gnn_kernel(nc, *args)
    r = _run(nc, [arrays], core_ids=[0])
    return r.results[0]["out_0_dram"]
```

```python
from contextlib import ExitStack

import concourse.bass as bass
from concourse import mybir

ALU = mybir.AluOpType
ACT = mybir.ActivationFunctionType
F32 = mybir.dt.float32
BF16 = mybir.dt.bfloat16
FP8 = mybir.dt.float8e4
U8 = mybir.dt.uint8
U16 = mybir.dt.uint16
I32 = mybir.dt.int32
AX_X = mybir.AxisListType.X
RMAX = bass.bass_isa.ReduceOp.max
RADD = bass.bass_isa.ReduceOp.add
ds = bass.ds

P = 128
UNROLL = 4
LN_EPS = 1e-5
DEG_EPS = 1e-6
NORM_FLOOR = 1e-16
NORM_MIN = 1e-8
THRESHOLDS = (0.000244, 0.000244 + (1.0 - 2.718281828459045 ** -0.1) * (0.0003 - 0.000244))
NEVER = 1e30
DVE_STEPS = 84
EDGE_BYTE = 64.0
EDGE_FP8 = 2.0
NO_EDGE = 255.0
LEAST_VALUE, MOST_VALUE = 0.5, 1e9


class Tile:

    def __init__(self, first, q):
        self.first, self.q = first, q
        self.t = first + UNROLL * q

    def div(self, n):
        return self.first // n + (UNROLL // n) * self.q

    def mod(self, n):
        return self.first % n


def alone(eng, passed):
    eng.sem_inc(passed, 1)


def tiles(eng, first, last, body, passed):
    turns = (last - first) // UNROLL
    if turns > 0:
        alone(eng, passed)
        with eng.Fori(0, turns) as q:
            for i in range(UNROLL):
                body(Tile(first + i, q))
    for i in range(first + turns * UNROLL, last):
        body(Tile(i, 0))


class Order:

    def __init__(self, eng, sem, base=0):
        self.eng, self.sem, self.base, self.n = eng, sem, base, 0

    def __call__(self, instruction):
        instruction.then_inc(self.sem, 1)
        self.n += 1
        self.eng.wait_ge(self.sem, self.base + self.n)


def gnn_kernel(nc, x, adj, W, Theta, Wq, bq, Wv, bv, out):
    N, D = x.shape
    NT = N // P
    HALF = N // 2
    JB = HALF // P
    NC = 4
    CW = N // NC
    BANK = 512
    D3 = 3 * D
    DS = D3 + 1
    LAYERS = len(THRESHOLDS)
    WORDS = N // 4
    WG = WORDS // P
    assert D == 64 and NT % UNROLL == 0 and JB * 256 == 8 * BANK

    with ExitStack() as ctx:
        def sb(name, shape, dt):
            return ctx.enter_context(nc.sbuf_tensor(name, shape, dt))

        def sem(name):
            return ctx.enter_context(nc.semaphore(name))

        edges_d = nc.dram_tensor("edges_d", (NT, P, N), U8).ap()
        gaps_d = nc.dram_tensor("gaps_d", (NT, P, N), U8).ap()
        pruned_d = nc.dram_tensor("pruned_d", (NT, P, N), U8).ap()
        prunedT_d = nc.dram_tensor("prunedT_d", (NT, P, N), U8).ap()
        prunedf_d = nc.dram_tensor("prunedf_d", (NT, P, N), F32).ap()
        adj_t = adj.rearrange("(t p) n -> t p n", p=P)

        logits = sb("logits", [P, 2, N], F32)
        expo = sb("expo", [P, 2, N], F32)
        rs_buf = sb("rs_buf", [P, NT * 6 * D], BF16)
        stat = sb("stat", [P, NT, 3, P], BF16)
        xcur = sb("xcur", [P, NT, D], F32)
        ywt = sb("ywt", [P, NT, D], F32)
        parts = sb("parts", [P, NT, 4 * D], BF16)
        parts2 = sb("parts2", [P, NT, 4 * D], BF16)
        slots = sb("slots", [P, UNROLL, N], U8)
        pr = sb("pr", [P, 2, N], U8)
        prT = sb("prT", [P, 2, N], U8)
        hat = sb("hat", [P, NT, 2, D], BF16)
        staged = sb("staged", [P, UNROLL, DS + 1], BF16)
        ident_f = sb("ident_f", [P, P], F32)
        ident_b = sb("ident_b", [P, P], BF16)
        zeros = sb("zeros", [P, BANK], BF16)
        half_ones = sb("half_ones", [P, P], BF16)
        neg_ones = sb("neg_ones", [P, P], BF16)
        w_all = sb("w_all", [D + 1, 4 * D], F32)
        value = sb("value", [P, 4], F32)
        flag = sb("flag", [P, 1], I32)
        th_all = sb("th_all", [P, LAYERS], F32)
        th_cur = sb("th_cur", [P, 1], F32)
        gsc = sb("gsc", [P, 4], F32)
        mx = sb("mx", [P, 2, NC + 1], F32)
        nmx = sb("nmx", [P, 2], F32)
        rsum = sb("rsum", [P, 2], F32)
        rinv = sb("rinv", [P, 2], F32)
        thr = sb("thr", [P, 2], F32)
        msum = sb("msum", [P, 2, D], F32)
        halfst = sb("halfst", [P, NT], F32)
        xsq = sb("xsq", [P, NT], F32)
        imp = sb("imp", [P, NT], F32)
        ex = sb("ex", [P, NT], F32)
        cmask = sb("cmask", [P, NT], F32)
        never = sb("never", [P, NT], F32)
        fmag = sb("fmag", [P, NT], F32)
        rnrm = sb("rnrm", [P, NT], F32)
        conn = sb("conn", [P, NT], F32)
        dvs = sb("dvs", [P, NT], F32)
        dvout = sb("dvout", [P, NT], F32)
        nmask = sb("nmask", [P, NT], F32)
        edges_n = sb("edges_n", [P, NT], F32)
        gaps_n = sb("gaps_n", [P, NT], F32)
        zero_bound = sb("zero_bound", [P, NT], F32)
        gap_exp = sb("gap_exp", [P, 2], F32)
        whole_sum = sb("whole_sum", [P, 2], F32)
        fac = sb("fac", [P, JB], F32)
        red = sb("red", [P, 8], F32)

        ps = ctx.enter_context(nc.psum_tensor("ps", [P, 8, BANK], F32))

        tmp = expo[:, :, :].rearrange("p a (b t d) -> p (a b) t d", b=2, d=D)
        rows4 = [logits[:, 0, :], logits[:, 1, :], expo[:, 0, :], expo[:, 1, :]]
        wT, theta_s = (stat[0:D, 0, n, :].bitcast(F32) for n in range(2))
        x_all = stat[:, :, :, :].rearrange("p t k c -> p (t k c)").bitcast(F32).rearrange("p (t c) -> p t c", c=D3)
        xWv = ps[:, 3:7, :].rearrange("p b (t d) -> p (b t) d", d=D)
        col_row = prT[:, 0, :].bitcast(F32)
        slots2 = parts2[:, :, :].rearrange("p t (k d) -> p t k d", d=D)
        q_pairs = rs_buf[:, 0:2 * N].rearrange("p (t k d) -> p t k d", k=4, d=D)
        tail_pair = rs_buf[:, 2 * N:3 * N].rearrange("p (t k d) -> p t k d", k=2, d=D)
        hat_third = prT[:, 1, :].bitcast(BF16).rearrange("p (t d) -> p t d", d=D)
        parts_pair = parts[:, :, 0:2 * D].rearrange("p t (k d) -> p t k d", d=D)
        rhs_a = rs_buf[:, 0:N]
        rhs_b = rs_buf[:, N:2 * N]
        xTa = parts2[:, :, :].rearrange("p t c -> p (t c)").bitcast(F32)[0:D + 1, :]
        marks = rs_buf[:, 0:2 * N].rearrange("p (a n) -> p a n", a=2)
        ring_h = slots[:, :, 0:HALF]
        gtile = slots[:, :, :].rearrange("p a n -> p (a n)").bitcast(F32)
        planes = expo[:, 1, :].bitcast(BF16)[:, 0:3 * HALF].rearrange("p (k n) -> p k n", k=3)
        blkT = logits[:, 0, 0:BANK]
        planesT = expo[:, 1, :].bitcast(BF16)[:, 0:3 * BANK].rearrange("p (k n) -> p k n", k=3)

        def many(name, n):
            return [sem(f"{name}{i}") for i in range(n)]

        passed = sem("passed")
        consts = sem("consts")
        tables_in = sem("tables_in")
        value_in = sem("value_in")
        x_in = sem("x_in")
        row_in = many("row_in", UNROLL)
        row_byte = sem("row_byte")
        row_mark = sem("row_mark")
        row_chk = sem("row_chk")
        edges_out = sem("edges_out")
        edges_sent = sem("edges_sent")
        row_count = sem("row_count")
        flag_set = sem("flag_set")
        wtheta_ps = sem("wtheta_ps")
        wtheta_in = sem("wtheta_in")
        ln_sq = sem("ln_sq")
        ln_v = sem("ln_v")
        ln_x = sem("ln_x")
        dve_pre = sem("dve_pre")
        dve_products = sem("dve_products")
        dve_step = sem("dve_step")
        xT_ps = sem("xT_ps")
        xT_even = sem("xT_even")
        xT_odd = sem("xT_odd")
        xT_one = sem("xT_one")
        v_ps = sem("v_ps")
        all_ps = sem("all_ps")
        all_a = sem("all_a")
        squares = sem("squares")
        parts_ready = sem("parts_ready")
        src_ready = sem("src_ready")
        parts2_ready = sem("parts2_ready")
        staged_in = sem("staged_in")
        half_in = many("half_in", UNROLL)
        half_used = sem("half_used")
        sweep_ps = sem("sweep_ps")
        sweep_read = sem("sweep_read")
        turned_v = sem("turned_v")
        turned_a = sem("turned_a")
        turn_v = sem("turn_v")
        turn_a = sem("turn_a")
        full_in = many("full_in", UNROLL)
        qk_ready = sem("qk_ready")
        qk_used = sem("qk_used")
        nmax_ready = sem("nmax_ready")
        exp_done = sem("exp_done")
        rinv_ready = sem("rinv_ready")
        e_used = sem("e_used")
        thr_ready = sem("thr_ready")
        tr_done = sem("tr_done")
        ev_done = sem("ev_done")
        count_ps = sem("count_ps")
        count_read = sem("count_read")
        gaps_a = sem("gaps_a")
        gaps_v = sem("gaps_v")
        gaps_out = sem("gaps_out")
        gaps_sent = sem("gaps_sent")
        sum_ready = sem("sum_ready")
        bound_ready = sem("bound_ready")
        pr_out = sem("pr_out")
        pr_sent = sem("pr_sent")
        prT_out = sem("prT_out")
        col_zero = sem("col_zero")
        col_read_a = sem("col_read_a")
        col_read_v = sem("col_read_v")
        att_ps = sem("att_ps")
        red_in = sem("red_in")
        red_out = sem("red_out")
        sm_in = sem("sm_in")
        sm_out = sem("sm_out")
        root_in = sem("root_in")
        root_out = sem("root_out")
        turned_in = many("turned_in", UNROLL)
        e_tile = sem("e_tile")
        msg_sum = sem("msg_sum")
        msg_out = sem("msg_out")
        x_again = sem("x_again")
        y_ready = sem("y_ready")
        y_out = sem("y_out")
        g_half_in = many("g_half_in", 2)
        g_half_free = sem("g_half_free")
        g_step = sem("g_step")
        g_step_t = sem("g_step_t")
        g_planes = sem("g_planes")
        g_full_in = sem("g_full_in")
        g_turned = sem("g_turned")
        g_split = sem("g_split")

        SC_B, SC_C, SC_D = 0, 1, 2

        block = ctx.enter_context(nc.Block())

        def loop(eng, first, last, body):
            tiles(eng, first, last, body, passed)

        def dtile(dram, T):
            return dram[ds(T.t, 1), :, :].rearrange("a p n -> (a p) n")

        def dhalf(dram, T, h):
            return dram[ds(T.t, 1), :, h * HALF:(h + 1) * HALF].rearrange("a p n -> (a p) n")

        def node(a, T):
            return a[:, ds(T.t, 1)]

        LEFT1, LEFT2, LEFT3, RIGHT1, RIGHT3 = range(5)
        GROUPS = NT // 4

        def turn_plan(side):
            def each(kind):
                return [(kind, a) for a in range(GROUPS)]
            plan = [(k, a, True) for k, a in each(LEFT1) + each(LEFT2)]
            if side == 0:
                for a in range(GROUPS):
                    plan += [(LEFT3, a, True), (RIGHT1, a, False)]
                return plan + [(k, a, a % 2 == 0) for k, a in each(RIGHT3)]
            return plan + [(k, a, a % 2 == 0) for k, a in each(RIGHT1) + each(LEFT3) + each(RIGHT3)]
        TURNS_A = [sum(by_act for _, _, by_act in turn_plan(side)) for side in range(2)]
        TURNS_V = [len(turn_plan(side)) - TURNS_A[side] for side in range(2)]

        def copy_column_sums(copy, g):
            return copy(col_row[32 * g:32 * g + 1, 0:2 * BANK].rearrange("p (a c) -> p a c", a=2),
                        ps[32 * g:32 * g + 1, 4:6, :])

        RESULTS = ((0, NT - UNROLL), (NT - UNROLL, NT))
        SHARES = ((0, NT // 4), (NT // 4, NT))

        LAST_BANKS = (6, 0, 2)

        V_PIECES = W_PIECES = 4

        def first_products(eng, lay, pieces):
            with eng.If(lay > 0):
                for piece in pieces:
                    piece(lay)

        def beside_load(eng, tile, pieces):
            first = max(pieces) + 1
            for t in range(first):
                tile(Tile(t, 0))
                if t in pieces:
                    pieces[t](0)
            loop(eng, first, NT, tile)

        def turned_to(kind, a):
            if kind <= LEFT3:
                return stat[:, 4 * a:4 * (a + 1), kind, :]
            rhs = rhs_a if kind == RIGHT1 else rhs_b
            return rhs[:, 4 * P * a:4 * P * (a + 1)].rearrange("p (a c) -> p a c", c=P)

        def copy_turned(eng, copy, lay, side, first=0, last=None):
            act = eng is nc.scalar
            per, ready, done = (TURNS_A, turned_a, turn_a) if act else (TURNS_V, turned_v, turn_v)
            mine = [(kind, a) for kind, a, by_act in turn_plan(side) if by_act == act]
            for n, (kind, a) in list(enumerate(mine))[first:last]:
                eng.wait_ge(ready, lay * sum(per) + side * per[0] + n + 1)
                copy(turned_to(kind, a), ps[:, (0 if act else 4) + n % 4, :].rearrange("p (a c) -> p a c", c=P)
                     ).then_inc(done, 1)

        def paths(eng, layer):
            eng.wait_ge(flag_set, 1)
            fast = eng.value_load(flag[0:1, 0:1], min_val=0, max_val=1)
            with eng.If(fast == 1):
                with eng.Fori(0, LAYERS) as lay:
                    layer(True, lay)
            with eng.Else():
                with eng.Fori(0, LAYERS) as lay:
                    layer(False, lay)

        @block.sync
        def _(sp):
            with nc.allow_non_contiguous_dma(reason="small tables"):
                sp.dma_start(xcur[:, :, :], x.rearrange("(t p) d -> p t d", p=P)).then_inc(x_in, 16)
                sp.dma_start(value[:, 0:1], adj[0:1, 0:1].to_broadcast([P, 1])).then_inc(value_in, 16)
                sp.wait_ge(consts, 1)
                for dst, src in ((w_all[0:D, 0:D], Wv), (w_all[0:D, D:2 * D], W), (w_all[0:D, 2 * D:3 * D], Wq),
                                 (w_all[D:D + 1, 0:D], bv.rearrange("(a d) -> a d", a=1)),
                                 (w_all[D:D + 1, 2 * D:3 * D], bq.rearrange("(a d) -> a d", a=1)),
                                 (theta_s[:, :], Theta)):
                    sp.dma_start(dst, src).then_inc(tables_in, 16)
            def row(T):
                i = T.mod(UNROLL)
                sp.wait_ge(row_mark, T.t + 1)
                alone(sp, passed)
                sp.dma_start(rows4[i], dtile(adj_t, T)).then_inc(row_in[i], 16)
            loop(sp, 0, NT, row)

            def layer(fast, lay):
                halves = lay * (4 * NT)
                fulls = lay * (2 * NT)

                def half_sweeps(source, phase):
                    for h in range(2):
                        def half(T, h=h):
                            n = halves + (2 * phase + h) * NT + T.t
                            if fast:
                                sp.wait_ge(half_used, n + 1)
                                alone(sp, passed)
                                i = T.mod(UNROLL)
                                sp.dma_start(ring_h[:, i, :], dhalf(source, T, h)).then_inc(half_in[i], 16)
                            else:
                                sp.wait_ge(g_half_free, n + 1)
                                alone(sp, passed)
                                i = T.mod(2)
                                sp.dma_start(gtile[:, i * HALF:(i + 1) * HALF],
                                             dhalf(source, T, h)).then_inc(g_half_in[i], 16)
                        loop(sp, 0, NT, half)

                def store_turned(t, i):
                    sp.wait_ge(ev_done, lay * NT + t + 2)
                    alone(sp, passed)
                    sp.wait_ge(prT_out, 16 * (lay * NT + t + 2))
                    alone(sp, passed)
                    sp.dma_start(prunedT_d[ds(t, 1), :, :].rearrange("a p n -> (a p) n"),
                                 prT[:, i, :]).then_inc(prT_out, 16)

                def whole(source, wait, into, signals):
                    def one(T):
                        wait(T)
                        alone(sp, passed)
                        i = T.mod(UNROLL) if fast else 0
                        sp.dma_start(into(i), dtile(source, T)).then_inc(signals[i], 16)
                    loop(sp, 0, NT, one)

                def slot(i):
                    return slots[:, i, :] if fast else gtile

                sp.wait_ge(edges_sent, NT + UNROLL)
                sp.wait_ge(e_tile, lay * NT + UNROLL)
                alone(sp, passed)
                half_sweeps(edges_d if fast else adj_t, 0)

                sp.wait_ge(half_used, halves + 2 * NT + UNROLL)

                def slot_masked(T):
                    sp.wait_ge(nmax_ready, fulls + T.t + (1 if fast else UNROLL))
                    if fast:
                        sp.wait_ge(gaps_a, lay * NT + T.t + 1)
                        sp.wait_ge(gaps_v, lay * NT + T.t + 1)
                whole(edges_d if fast else adj_t, slot_masked,
                      slot, full_in if fast else [g_full_in])
                sp.wait_ge(nmax_ready, fulls + NT + UNROLL)
                if fast:
                    sp.wait_ge(gaps_sent, (lay + 1) * NT + 2)
                    alone(sp, passed)
                if fast:
                    def gaps_row(T):
                        sp.wait_ge(nmax_ready, fulls + NT + T.t + 1)
                        alone(sp, passed)
                        i = T.mod(UNROLL)
                        sp.dma_start(slot(i), dtile(gaps_d, T)).then_inc(full_in[i], 16)

                    def gaps_row_and_store(T):
                        gaps_row(T)
                        store_turned(T.t - BEHIND, (T.first - BEHIND) % 2)
                    BEHIND = 2 * UNROLL - 1
                    for t in range(BEHIND):
                        gaps_row(Tile(t, 0))
                    loop(sp, BEHIND, NT, gaps_row_and_store)
                    for t in range(NT - BEHIND, NT):
                        store_turned(t, t % 2)
                else:
                    whole(adj_t, lambda T: sp.wait_ge(e_used, fulls + NT + T.t + 2), slot, [g_full_in])

                sp.wait_ge(e_used, fulls + 2 * NT + 2)
                sp.wait_ge(pr_sent, (lay + 1) * NT + 2)
                alone(sp, passed)
                half_sweeps(pruned_d if fast else prunedf_d, 1)

                sp.wait_ge(half_used, halves + 4 * NT + UNROLL)
                alone(sp, passed)
                if fast:
                    sp.wait_ge(prT_out, 16 * ((lay + 1) * NT + 2))
                    alone(sp, passed)
                whole(prunedT_d if fast else prunedf_d,
                      lambda T: sp.wait_ge(e_tile, lay * NT + T.t + (1 if fast else UNROLL)),
                      slot, turned_in if fast else [g_full_in])

            paths(sp, layer)
            sp.wait_ge(parts2_ready, 3 * LAYERS)
            with nc.allow_non_contiguous_dma(reason="rows of 256 bytes"):
                sp.dma_start(tmp[:, 0], x.rearrange("(t p) d -> p t d", p=P)).then_inc(x_again, 16)
                for n, (first, end) in enumerate(RESULTS):
                    sp.wait_ge(y_ready, n + 1)
                    sp.dma_start(out.rearrange("(t p) d -> p t d", p=P)[:, first:end],
                                 tmp[:, 1, first:end]).then_inc(y_out, 16)
            sp.wait_ge(y_out, 16 * len(RESULTS))

        @block.gpsimd
        def _(pool):
            for s, n in ((row_mark, UNROLL), (row_chk, 2), (half_used, UNROLL), (turn_v, 4), (turn_a, 4), (all_a, 3),
                         (qk_used, 2), (nmax_ready, UNROLL), (exp_done, 2), (e_used, 2), (tr_done, 2),
                         (ev_done, 1), (e_tile, UNROLL), (msg_sum, UNROLL), (msg_out, 2), (g_half_free, 2),
                         (edges_sent, UNROLL), (row_count, UNROLL), (count_ps, 2), (count_read, 2),
                         (gaps_a, UNROLL), (gaps_v, UNROLL),
                         (gaps_sent, 2), (pr_sent, 2), (prT_out, 32)):
                pool.sem_inc(s, n)
            nc.gpsimd.memset(w_all[:, :], 0.0).then_inc(consts, 1)
            nc.gpsimd.memset(ident_f[:, :], 0.0).then_inc(consts, 1)
            nc.gpsimd.memset(zeros[:, :], 0.0).then_inc(consts, 1)
            nc.gpsimd.memset(half_ones[:, :], 1.0 / EDGE_FP8).then_inc(consts, 1)
            nc.gpsimd.memset(neg_ones[:, :], -1.0).then_inc(consts, 1)
            for n, th in enumerate(THRESHOLDS):
                nc.gpsimd.memset(th_all[:, n:n + 1], th).then_inc(consts, 1)
            pool.wait_ge(consts, 5 + LAYERS)
            nc.gpsimd.affine_select(out=ident_f[:, :], in_=ident_f[:, :], compare_op=ALU.not_equal, fill=1.0,
                                    base=0, pattern=[[-1, P]], channel_multiplier=1).then_inc(consts, 1)
            pool.wait_ge(consts, 6 + LAYERS)
            nc.gpsimd.tensor_copy(ident_b[:, :], ident_f[:, :]).then_inc(consts, 1)
            nc.gpsimd.memset(parts[:, :, D3:4 * D], 1.0).then_inc(consts, 1)

            def row_of_ones(lay):
                pool.wait_ge(consts, 8 + LAYERS)
                pool.wait_ge(e_tile, lay * NT + UNROLL)
                alone(pool, passed)
                nc.gpsimd.memset(xTa[D:D + 1, :], 1.0).then_inc(xT_one, 1)
            row_of_ones(0)

            def store_edges(T):
                pool.wait_ge(row_byte, T.t + 1)
                alone(pool, passed)
                i = T.mod(UNROLL)
                nc.gpsimd.dma_start(dtile(edges_d, T), slots[:, i, :]).then_inc(edges_out, 16)
                pool.wait_ge(edges_out, 16 * (T.t + 1))
                pool.sem_inc(edges_sent, 1)
            loop(pool, 0, NT, store_edges)

            def layer(fast, lay):
                halves = lay * (4 * NT)
                fulls = lay * (2 * NT)

                def stage(phase):
                    for h in range(2):
                        def one(T, h=h):
                            n = halves + (2 * phase + h) * NT + T.t
                            pool.wait_ge(half_used, n + 1)
                            alone(pool, passed)
                            nc.gpsimd.tensor_copy(staged[:, T.mod(UNROLL), 0:DS],
                                                  parts[:, ds(T.t, 1), 0:DS].rearrange("p a c -> p (a c)")
                                                  ).then_inc(staged_in, 1)
                        if h:
                            loop(pool, 0, NT, one)
                            continue
                        for half in range(2):
                            pool.wait_ge(parts_ready, 4 * lay + 2 * phase + half + 1)
                            alone(pool, passed)
                            loop(pool, *SHARES[half], one)

                def reduce_over_partitions(n, op):
                    pool.wait_ge(red_in, 4 * lay + n + 1)
                    alone(pool, passed)
                    nc.gpsimd.partition_all_reduce(red[:, 4 + n:5 + n], red[:, n:n + 1], P, op).then_inc(red_out, 1)

                first_products(pool, lay, [row_of_ones])
                stage(0)
                pool.wait_ge(half_used, halves + 2 * NT + UNROLL)
                alone(pool, passed)
                nc.gpsimd.memset(col_row[:, 0:2 * BANK], 0.0).then_inc(col_zero, 1)
                if fast:
                    def store_gaps(T):
                        pool.wait_ge(gaps_a, lay * NT + T.t + 1 + UNROLL)
                        pool.wait_ge(gaps_v, lay * NT + T.t + 1 + UNROLL)
                        alone(pool, passed)
                        nc.gpsimd.dma_start(dtile(gaps_d, T), pr[:, T.mod(2), :]).then_inc(gaps_out, 16)
                        pool.wait_ge(gaps_out, 16 * (lay * NT + T.t + 1))
                        pool.sem_inc(gaps_sent, 1)
                    loop(pool, 0, NT, store_gaps)
                reduce_over_partitions(0, RMAX)
                reduce_over_partitions(1, RADD)

                def store(T):
                    i = T.mod(2)
                    pool.wait_ge(e_used, fulls + NT + T.t + 3)
                    alone(pool, passed)
                    if fast:
                        nc.gpsimd.dma_start(dtile(pruned_d, T), pr[:, i, :]).then_inc(pr_out, 16)
                    else:
                        nc.gpsimd.dma_start(dtile(prunedf_d, T), logits[:, i, :]).then_inc(pr_out, 16)
                    pool.wait_ge(pr_out, 16 * (lay * NT + T.t + 1))
                    pool.sem_inc(pr_sent, 1)
                loop(pool, 0, NT, store)

                reduce_over_partitions(2, RMAX)
                reduce_over_partitions(3, RADD)
                stage(1)

            paths(pool, layer)

        @block.scalar
        def _(act):
            act.wait_ge(ln_v, 1)
            nc.scalar.activation(ywt[:, :, :], xcur[:, :, :], ACT.Square).then_inc(ln_sq, 1)
            act.wait_ge(ln_v, 2)
            nc.scalar.activation(xsq[:, :], xsq[:, :], ACT.Sqrt).then_inc(ln_sq, 1)

            def count_edges(T):
                act.wait_ge(row_byte, T.t + 1)
                act.wait_ge(row_count, T.t + 3)
                nc.scalar.activation(prT[:, T.mod(2), :], slots[:, T.mod(UNROLL), :], ACT.Copy,
                                     accum_out=node(edges_n, T)).then_inc(row_count, 1)

            def odd_tiles(lay):
                act.wait_ge(xT_ps, lay + 1)
                nc.scalar.copy(xTa[0:D, :].rearrange("p (a two c) -> p a two c", two=2, c=P)[:, :, 1, :],
                               ps[D:P, 0:4, :].rearrange("p b (a c) -> p (b a) c", c=P)).then_inc(xT_odd, 1)

            def copy_products(lay, piece):
                for n in range(piece * NT // 2 // W_PIECES, (piece + 1) * NT // 2 // W_PIECES):
                    act.wait_ge(all_ps, (NT // 2) * lay + n + 1)
                    nc.scalar.copy(x_all[:, 2 * n:2 * n + 2, :],
                                   ps[:, n % 3, 0:2 * D3].rearrange("p (a c) -> p a c", a=2)).then_inc(all_a, 1)
            pieces = {V_PIECES + 1 + n: lambda lay, n=n: copy_products(lay, n) for n in range(W_PIECES)}
            pieces[1] = odd_tiles
            beside_load(act, count_edges, pieces)

            def layer(fast, lay):
                fulls = lay * (2 * NT)

                first_products(act, lay, [odd_tiles] + [lambda lay, n=n: copy_products(lay, n)
                                                        for n in range(W_PIECES)])
                act.wait_ge(all_a, (NT // 2) * (lay + 1) + 3)
                nc.scalar.activation(tmp[:, 2], x_all[:, :, 0:D], ACT.Square).then_inc(squares, 1)
                nc.scalar.activation(tmp[:, 3], xcur[:, :, :], ACT.Square).then_inc(squares, 1)

                def root(n, dst, src):
                    act.wait_ge(root_in, 3 * lay + n + 1)
                    nc.scalar.activation(dst, src, ACT.Sqrt).then_inc(root_out, 1)

                def node_exp(n):
                    act.wait_ge(sm_in, 2 * lay + n + 1)
                    nc.scalar.activation(ex[:, :], imp[:, :], ACT.Exp, bias=red[:, 4 + 2 * n:5 + 2 * n],
                                         accum_out=red[:, 2 * n + 1:2 * n + 2]).then_inc(sm_out, 1)

                root(0, halfst[:, :], halfst[:, :])
                root(1, fmag[:, :], fmag[:, :])
                copy_turned(act, nc.scalar.copy, lay, 0)

                def row_exp(T, phase):
                    i, n = T.mod(2), fulls + phase * NT + T.t
                    act.wait_ge(nmax_ready, n + 1 + UNROLL)
                    act.wait_ge(e_used, n + 1)
                    if fast and phase:
                        nc.scalar.activation(gap_exp[:, i:i + 1], nmx[:, i:i + 1], ACT.Exp)
                    nc.scalar.activation(expo[:, i, :], logits[:, i, :], ACT.Exp, bias=nmx[:, i:i + 1],
                                         accum_out=rsum[:, i:i + 1]).then_inc(exp_done, 1)

                def attention(T):
                    row_exp(T, 0)
                    if fast:
                        act.wait_ge(gaps_sent, lay * NT + T.t + 1)
                        nc.scalar.activation(pr[:, T.mod(2), 0:HALF], slots[:, T.mod(UNROLL), 0:HALF], ACT.Copy,
                                             bias=NO_EDGE, scale=-NO_EDGE / EDGE_BYTE).then_inc(gaps_a, 1)
                loop(act, 0, NT, attention)
                act.wait_ge(e_used, fulls + NT + 2)
                act.wait_ge(col_zero, lay + 1)
                for g in range(0, 4, 2):
                    copy_column_sums(nc.scalar.copy, g).then_inc(col_read_a, 1)
                copy_turned(act, nc.scalar.copy, lay, 1, 0, GROUPS // 2)
                node_exp(0)
                copy_turned(act, nc.scalar.copy, lay, 1, GROUPS // 2)

                def zero_in_maximum(T):
                    if fast:
                        nc.scalar.copy(mx[:, T.mod(2), NC:NC + 1], node(zero_bound, T)).then_inc(bound_ready, 1)

                def threshold(T):
                    i = T.mod(2)
                    act.wait_ge(exp_done, fulls + NT + T.t + 3)
                    if fast:
                        nc.scalar.activation(whole_sum[:, i:i + 1], gap_exp[:, i:i + 1], ACT.Identity,
                                             bias=rsum[:, i:i + 1], scale=node(gaps_n, T)).then_inc(sum_ready, 1)
                        act.wait_ge(sum_ready, lay * NT + T.t + 1)
                    nc.scalar.activation(thr[:, i:i + 1], (whole_sum if fast else rsum)[:, i:i + 1], ACT.Identity,
                                         bias=node(never, T), scale=th_cur[:, 0:1]).then_inc(thr_ready, 1)

                def edge_scores(T):
                    zero_in_maximum(T)
                    row_exp(T, 1)
                    threshold(T)

                def copy_pruned(T, back, bank=6):
                    i = (T.first - back) % 2
                    t = T.t - back
                    act.wait_ge(tr_done, lay * NT + t + 3)
                    act.wait_ge(prT_out, 16 * (lay * NT + t + 1))
                    act.wait_ge(count_ps, lay * NT + t + 1)
                    nc.scalar.copy(prT[:, i, :].bitcast(U16), ps[:, bank:bank + 2, :].rearrange("p a c -> p (a c)").bitcast(U16)
                                   ).then_inc(ev_done, 1)

                if fast:
                    loop(act, 0, 3, edge_scores)

                    def both(T):
                        zero_in_maximum(T)
                        copy_pruned(T, 3)
                        row_exp(T, 1)
                        threshold(T)
                    loop(act, 3, NT, both)
                    for t in range(NT, NT + 3):
                        copy_pruned(Tile(t, 0), 3, LAST_BANKS[t - NT])
                else:
                    loop(act, 0, NT, edge_scores)
                node_exp(1)
                root(2, dvs[:, :], dvs[:, :])

                def message(T):
                    i = T.mod(2)
                    act.wait_ge(msg_sum, lay * NT + T.t + 1 + UNROLL)
                    nc.scalar.activation(xcur[:, ds(T.t, 1), :].rearrange("p a d -> p (a d)"), msum[:, i, :],
                                         ACT.Relu, scale=node(dvout, T)).then_inc(msg_out, 1)
                loop(act, 0, NT, message)

            paths(act, layer)

        @block.vector
        def _(dve):
            step = Order(dve, dve_pre)

            def per_node(a):
                return a.unsqueeze(2).to_broadcast([P, a.shape[1], D])

            dve.wait_ge(x_in, 16)
            step(nc.vector.tensor_reduce(xsq[:, :], xcur[:, :, :], AX_X, ALU.add))
            step(nc.vector.tensor_scalar(xsq[:, :], xsq[:, :], 1.0 / D, None, ALU.mult))
            nc.vector.tensor_tensor(xcur[:, :, :], xcur[:, :, :], per_node(xsq[:, :]), ALU.subtract).then_inc(ln_v, 1)
            dve.wait_ge(ln_sq, 1)
            step(nc.vector.tensor_reduce(xsq[:, :], ywt[:, :, :], AX_X, ALU.add))
            nc.vector.tensor_scalar(xsq[:, :], xsq[:, :], 1.0 / D, LN_EPS, ALU.mult, ALU.add).then_inc(ln_v, 1)
            dve.wait_ge(ln_sq, 2)
            step(nc.vector.reciprocal(xsq[:, :], xsq[:, :]))
            step(nc.vector.tensor_tensor(xcur[:, :, :], xcur[:, :, :], per_node(xsq[:, :]), ALU.mult))
            nc.vector.tensor_scalar(xcur[:, :, :], xcur[:, :, :], 0.0, None, ALU.max).then_inc(ln_x, 1)
            dve.wait_ge(wtheta_ps, 1)
            nc.vector.tensor_copy(wT[:, :], ps[0:D, 1, 0:D]).then_inc(wtheta_in, 1)
            dve.wait_ge(wtheta_ps, 2)
            nc.vector.tensor_copy(w_all[0:D, 3 * D:4 * D], ps[0:D, 0, 0:D]).then_inc(wtheta_in, 1)

            dve.wait_ge(value_in, 16)

            def edge_bytes(T):
                i = T.mod(UNROLL)
                dve.wait_ge(row_in[i], 16 * (T.div(UNROLL) + 1))
                dve.wait_ge(row_chk, T.t + 1)
                dve.wait_ge(edges_sent, T.t + 1)
                dve.wait_ge(row_count, T.t + 1)
                nc.vector.tensor_scalar(slots[:, i, :], rows4[i], value[:, 0:1], EDGE_BYTE,
                                        ALU.is_equal, ALU.mult).then_inc(row_byte, 1)
                nc.vector.tensor_scalar(marks[:, T.mod(2), :], rows4[i], 0.0, None,
                                        ALU.not_equal).then_inc(row_mark, 1)

            def split(step, src, first, second, third, rest):
                step(nc.vector.tensor_copy(first, src))
                step(nc.vector.tensor_tensor(rest, src, first, ALU.subtract))
                step(nc.vector.tensor_copy(second, rest))
                step(nc.vector.tensor_tensor(third, rest, second, ALU.subtract))

            def split_to_parts(step, src, half, rest):
                these = slice(*SHARES[half])
                split(step, src[:, these], parts[:, these, 0:D], parts[:, these, D:2 * D],
                      parts[:, these, 2 * D:D3], rest[:, these])
                dve.sem_inc(parts_ready, 1)

            def even_tiles(lay):
                dve.wait_ge(xT_ps, lay + 1)
                nc.vector.tensor_copy(xTa[0:D, :].rearrange("p (a two c) -> p a two c", two=2, c=P)[:, :, 0, :],
                                      ps[0:D, 0:4, :].rearrange("p b (a c) -> p (b a) c", c=P)).then_inc(xT_even, 1)

            def split_V(lay, half):
                dve.wait_ge(v_ps, lay + 1)
                split_to_parts(Order(dve, dve_products, 8 * lay + 4 * half), xWv, half, ywt)
            beside_load(dve, edge_bytes, {1: even_tiles, V_PIECES + 2: lambda lay: split_V(lay, 0),
                                          V_PIECES + 3: lambda lay: split_V(lay, 1)})
            dve.wait_ge(row_chk, NT + 2)
            dve.wait_ge(row_count, NT + UNROLL)
            step(nc.vector.tensor_scalar(gaps_n[:, :], edges_n[:, :], -1.0 / EDGE_BYTE, float(N), ALU.mult, ALU.add))
            step(nc.vector.tensor_scalar(zero_bound[:, :], gaps_n[:, :], 0.0, -3.0e38, ALU.is_equal, ALU.mult))
            step(nc.vector.tensor_reduce(value[:, 1:2], ps[:, 7, :], AX_X, ALU.min))
            step(nc.vector.tensor_scalar(value[:, 1:2], value[:, 1:2], 0.0, None, ALU.is_equal))
            step(nc.vector.tensor_scalar(value[:, 2:3], value[:, 0:1], LEAST_VALUE, None, ALU.is_ge))
            step(nc.vector.tensor_scalar(value[:, 3:4], value[:, 0:1], MOST_VALUE, None, ALU.is_le))
            step(nc.vector.tensor_tensor(value[:, 1:2], value[:, 1:2], value[:, 2:3], ALU.mult))
            step(nc.vector.tensor_tensor(value[:, 1:2], value[:, 1:2], value[:, 3:4], ALU.mult))
            step(nc.vector.tensor_copy(th_cur[:, :], th_all[:, 0:1]))
            nc.vector.tensor_copy(flag[:, :], value[:, 1:2]).then_inc(flag_set, 1)

            def layer(fast, lay):
                fulls = lay * (2 * NT)
                halves = lay * (4 * NT)
                step = Order(dve, dve_step, lay * DVE_STEPS)

                def planes_of(phase, h):
                    def one(T):
                        k = (2 * phase + h) * NT
                        n = halves + k + T.t
                        i = T.mod(2)
                        g = gtile[:, i * HALF:(i + 1) * HALF]
                        own = Order(dve, g_step, 4 * n)
                        dve.wait_ge(g_half_in[i], 16 * (lay * (2 * NT) + k // 2 + T.div(2) + 1))
                        dve.wait_ge(half_used, n + UNROLL)
                        own(nc.vector.tensor_copy(planes[:, 0, :], g))
                        own(nc.vector.tensor_tensor(g, g, planes[:, 0, :], ALU.subtract))
                        own(nc.vector.tensor_copy(planes[:, 1, :], g))
                        own(nc.vector.tensor_tensor(g, g, planes[:, 1, :], ALU.subtract))
                        nc.vector.tensor_copy(planes[:, 2, :], g).then_inc(g_planes, 1)
                        dve.wait_ge(g_planes, n + 1)
                        dve.sem_inc(g_half_free, 1)
                    loop(dve, 0, NT, one)

                def sums_of_sweep(phase, h, dst):
                    dve.wait_ge(sweep_ps, 4 * lay + 2 * phase + h + 1)
                    blocks = ps[:, :, :].rearrange("p b (u c) -> p (b u) c", u=2)
                    n = 8 * lay + 4 * phase + 2 * h
                    if phase:
                        step(nc.vector.tensor_scalar(fac[:, :], blocks[:, :, D3], gsc[:, SC_D:SC_D + 1], DEG_EPS,
                                                     ALU.mult, ALU.max))
                    for q in range(2):
                        these = slice(q * JB // 2, (q + 1) * JB // 2)
                        nc.vector.tensor_reduce(dst[:, these], blocks[:, these, 0:D3]
                                                .rearrange("p b (k d) -> p b d k", k=3),
                                                AX_X, ALU.add).then_inc(sweep_read, 1)
                    dve.wait_ge(sweep_read, n + 2)
                    if phase:
                        step(nc.vector.reciprocal(fac[:, :], fac[:, :]))
                        step(nc.vector.tensor_scalar(fac[:, :], fac[:, :], gsc[:, SC_D:SC_D + 1], None, ALU.mult))
                        step(nc.vector.tensor_tensor(dst, dst, per_node(fac[:, :]), ALU.mult))

                def norm_root(n, a):
                    nc.vector.tensor_scalar(a, a, NORM_FLOOR if n < 2 else DEG_EPS, None,
                                            ALU.max).then_inc(root_in, 1)
                    dve.wait_ge(root_out, 3 * lay + n + 1)

                def node_softmax(n):
                    nc.vector.tensor_reduce(red[:, 2 * n:2 * n + 1], imp[:, :], AX_X, ALU.max).then_inc(red_in, 1)
                    dve.wait_ge(red_out, 4 * lay + 2 * n + 1)
                    nc.vector.tensor_scalar(red[:, 4 + 2 * n:5 + 2 * n], red[:, 4 + 2 * n:5 + 2 * n], -1.0, None,
                                            ALU.mult).then_inc(sm_in, 1)
                    dve.wait_ge(sm_out, 2 * lay + n + 1)
                    dve.sem_inc(red_in, 1)
                    dve.wait_ge(red_out, 4 * lay + 2 * n + 2)
                    step(nc.vector.tensor_tensor(red[:, 5 + 2 * n:6 + 2 * n], red[:, 5 + 2 * n:6 + 2 * n],
                                                 th_cur[:, :], ALU.mult))
                    return red[:, 5 + 2 * n:6 + 2 * n]

                first_products(dve, lay, [even_tiles, lambda lay: split_V(lay, 0), lambda lay: split_V(lay, 1)])
                if fast:
                    step(nc.vector.tensor_tensor(gsc[:, SC_B:SC_B + 1], value[:, 0:1], value[:, 0:1], ALU.mult))
                    step(nc.vector.tensor_scalar(gsc[:, SC_B:SC_B + 1], gsc[:, SC_B:SC_B + 1],
                                                 D ** -0.5 / EDGE_BYTE / EDGE_FP8, None, ALU.mult))
                    step(nc.vector.tensor_scalar(gsc[:, SC_C:SC_C + 1], value[:, 0:1], 1.0 / EDGE_BYTE, None,
                                                 ALU.mult))
                    step(nc.vector.tensor_scalar(gsc[:, SC_D:SC_D + 1], value[:, 0:1], 1.0 / EDGE_FP8, None,
                                                 ALU.mult))
                else:
                    step(nc.vector.memset(gsc[:, SC_B:SC_B + 1], D ** -0.5))
                    step(nc.vector.memset(gsc[:, SC_C:SC_C + 1], 1.0))
                    step(nc.vector.memset(gsc[:, SC_D:SC_D + 1], 1.0))
                    step(nc.vector.memset(gsc[:, 3:4], 1.0))

                dve.wait_ge(squares, 2 * lay + 2)
                step(nc.vector.tensor_reduce(halfst[:, :], tmp[:, 2], AX_X, ALU.add))
                step(nc.vector.tensor_reduce(xsq[:, :], tmp[:, 3], AX_X, ALU.add))
                dve.wait_ge(all_a, (NT // 2) * (lay + 1) + 3)
                norm_root(0, halfst[:, :])
                step(nc.vector.tensor_scalar(halfst[:, :], halfst[:, :], 0.5, None, ALU.mult))
                step(nc.vector.tensor_copy(ywt[:, :, :], x_all[:, :, 2 * D:D3]))
                step(nc.vector.tensor_copy(fmag[:, :], xsq[:, :]))
                norm_root(1, fmag[:, :])
                step(nc.vector.tensor_scalar(rnrm[:, :], fmag[:, :], NORM_MIN, None, ALU.max))
                step(nc.vector.reciprocal(rnrm[:, :], rnrm[:, :]))
                step(nc.vector.tensor_tensor(tmp[:, 1], xcur[:, :, :], per_node(rnrm[:, :]), ALU.mult))
                split(step, tmp[:, 1], hat[:, :, 0], hat[:, :, 1], hat_third, tmp[:, 0])
                split(step, x_all[:, :, D:2 * D], q_pairs[:, :, 0], q_pairs[:, :, 2], tail_pair[:, :, 0], tmp[:, 0])
                step(nc.vector.tensor_copy(q_pairs[:, :, 1], q_pairs[:, :, 0]))
                step(nc.vector.tensor_copy(q_pairs[:, :, 3], q_pairs[:, :, 2]))
                step(nc.vector.tensor_copy(tail_pair[:, :, 1], q_pairs[:, :, 0]))
                dve.sem_inc(src_ready, 1)

                def split_to_parts2(h):
                    these = slice(h * JB, (h + 1) * JB)
                    split(step, tmp[:, 1, 0:JB, :], slots2[:, these, 2], slots2[:, these, 3], slots2[:, these, 1],
                          tmp[:, 0, 0:JB, :])
                for h in range(2):
                    if not fast:
                        planes_of(0, h)
                    sums_of_sweep(0, h, tmp[:, 1, 0:JB, :])
                    split_to_parts2(h)
                    step(nc.vector.tensor_copy(slots2[:, h * JB:(h + 1) * JB, 0], slots2[:, h * JB:(h + 1) * JB, 2]))
                dve.sem_inc(parts2_ready, 1)
                copy_turned(dve, nc.vector.tensor_copy, lay, 0)
                for pair, a in ((tail_pair, hat[:, :, 0]), (parts_pair, hat[:, :, 1])):
                    step(nc.vector.tensor_copy(pair, a.unsqueeze(2).to_broadcast([P, NT, 2, D])))
                dve.sem_inc(src_ready, 1)

                def adjacency(T):
                    return slots[:, T.mod(UNROLL), :] if fast else gtile

                def mask_rows(T, phase, between={}):
                    i, k = T.mod(2), phase * NT
                    factor = value[:, 0:1] if fast and phase else gsc[:, phase:phase + 1]
                    if fast:
                        dve.wait_ge(full_in[T.mod(UNROLL)], 16 * (lay * (2 * NT // UNROLL) + k // UNROLL + T.div(UNROLL) + 1))
                    else:
                        dve.wait_ge(g_full_in, 16 * (lay * (3 * NT) + k + T.t + 1))
                        if phase:
                            dve.wait_ge(pr_sent, lay * NT + T.t + 1)
                    dve.wait_ge(exp_done, fulls + k + T.t + 1)
                    for c in range(NC):
                        n = NC * (fulls + k + T.t) + c
                        dve.wait_ge(qk_ready, n + 1)
                        alone(dve, passed)
                        nc.vector.tensor_tensor_reduce(
                            logits[:, i, c * CW:(c + 1) * CW],
                            ps[:, 2 * (c % 2):2 * (c % 2) + 2, :].rearrange("p a n -> p (a n)"),
                            adjacency(T)[:, c * CW:(c + 1) * CW], factor, -3.0e38,
                            ALU.subtract if fast and phase else ALU.mult, ALU.max, mx[:, i, c:c + 1]).then_inc(qk_used, 1)
                        if c in between:
                            between[c]()
                    dve.wait_ge(qk_used, NC * (fulls + k + T.t + 1) + 2)
                    if fast and phase:
                        dve.wait_ge(bound_ready, lay * NT + T.t + 1)
                    nc.vector.tensor_reduce(nmx[:, i:i + 1], mx[:, i, 0:NC + 1 if fast and phase else NC],
                                            AX_X, ALU.max, negate=True).then_inc(nmax_ready, 1)

                def inverse_sum(T, back):
                    i, t = (T.first - back) % 2, T.t - back
                    dve.wait_ge(exp_done, fulls + t + 3)
                    nc.vector.reciprocal(rinv[:, i:i + 1], rsum[:, i:i + 1]).then_inc(rinv_ready, 1)

                def gap_bytes(T):
                    if fast:
                        dve.wait_ge(gaps_sent, lay * NT + T.t + 1)
                        nc.vector.tensor_scalar(pr[:, T.mod(2), HALF:N], slots[:, T.mod(UNROLL), HALF:N],
                                                -NO_EDGE / EDGE_BYTE, NO_EDGE, ALU.mult, ALU.add
                                                ).then_inc(gaps_v, 1)
                mask_rows(Tile(0, 0), 0)
                gap_bytes(Tile(0, 0))

                def attention(T):
                    mask_rows(T, 0)
                    inverse_sum(T, 1)
                    gap_bytes(T)
                loop(dve, 1, NT, attention)
                inverse_sum(Tile(NT, 0), 1)

                dve.wait_ge(e_used, fulls + NT + 2)
                dve.wait_ge(col_zero, lay + 1)
                for g in range(1, 4, 2):
                    copy_column_sums(nc.vector.tensor_copy, g).then_inc(col_read_v, 1)

                dve.wait_ge(att_ps, lay + 1)
                step(nc.vector.tensor_scalar(imp[:, :].rearrange("p (b g r) -> p b r g", b=2, g=4),
                                             ps[:, 6, 0:NT].rearrange("p (b r g) -> p b r g", b=2, g=4),
                                             0.5 / N, None, ALU.mult))
                step(nc.vector.tensor_tensor(imp[:, :], imp[:, :], halfst[:, :], ALU.add))
                bound = node_softmax(0)
                step(nc.vector.tensor_scalar(cmask[:, :], ex[:, :], bound, None, ALU.is_ge))
                step(nc.vector.tensor_scalar(never[:, :], cmask[:, :], -NEVER, NEVER, ALU.mult, ALU.add))
                for slot, part in ((2, hat[:, :, 0]), (3, hat[:, :, 1]), (1, hat_third)):
                    step(nc.vector.tensor_tensor(slots2[:, :, slot], part, per_node(cmask[:, :]), ALU.mult))
                    if slot == 3:
                        dve.sem_inc(src_ready, 1)
                step(nc.vector.tensor_copy(slots2[:, :, 0], slots2[:, :, 2]))
                dve.sem_inc(src_ready, 1)
                copy_turned(dve, nc.vector.tensor_copy, lay, 1)
                step(nc.vector.tensor_tensor(fmag[:, :], fmag[:, :], cmask[:, :], ALU.mult))
                step(nc.vector.tensor_scalar(fmag[:, :], fmag[:, :], NORM_FLOOR ** 0.5, None, ALU.max))

                def keep_edges(T, back):
                    i, t = (T.first - back) % 2, T.t - back
                    dve.wait_ge(thr_ready, lay * NT + t + 1)
                    if fast:
                        dve.wait_ge(tr_done, lay * NT + t + 1)
                        dve.wait_ge(pr_sent, lay * NT + t + 1)
                        nc.vector.tensor_scalar(pr[:, i, :], expo[:, i, :], thr[:, i:i + 1], EDGE_BYTE,
                                                ALU.is_ge, ALU.mult).then_inc(e_used, 1)
                    else:
                        nc.vector.scalar_tensor_tensor(out=logits[:, i, :], in0=expo[:, i, :],
                                                       scalar=thr[:, i:i + 1], in1=gtile, op0=ALU.is_ge,
                                                       op1=ALU.mult, accum_out=node(conn, Tile(T.first - back, T.q))
                                                       ).then_inc(e_used, 1)

                def keep_count(T, back):
                    then = Tile(T.first - back, T.q)
                    dve.wait_ge(count_ps, lay * NT + then.t + 3)
                    nc.vector.tensor_scalar(node(conn, then), ps[:, 4 + then.mod(2), 0:1],
                                            EDGE_BYTE, None, ALU.mult).then_inc(count_read, 1)

                if fast:
                    def mask_and_prune(T, counts=True):
                        between = {1: lambda: keep_edges(T, 2)}
                        if counts:
                            between[2] = lambda: keep_count(T, 5)
                        mask_rows(T, 1, between)
                    for t in range(2):
                        mask_rows(Tile(t, 0), 1)
                    for t in range(2, 5):
                        mask_and_prune(Tile(t, 0), False)
                    loop(dve, 5, NT, mask_and_prune)
                    for t in range(NT, NT + 2):
                        keep_edges(Tile(t, 0), 2)
                    for t in range(NT, NT + 5):
                        keep_count(Tile(t, 0), 5)
                    dve.wait_ge(count_read, (lay + 1) * NT + 2)
                else:
                    def cosines(T):
                        mask_rows(T, 1)
                        keep_edges(T, 0)
                    loop(dve, 0, NT, cosines)
                dve.wait_ge(e_used, fulls + 2 * NT + 2)

                step(nc.vector.tensor_scalar(conn[:, :], conn[:, :], gsc[:, SC_C:SC_C + 1], None, ALU.mult))
                step(nc.vector.tensor_tensor(imp[:, :], conn[:, :], fmag[:, :], ALU.mult))
                bound = node_softmax(1)
                step(nc.vector.tensor_scalar(nmask[:, :], ex[:, :], bound, None, ALU.is_ge))
                step(nc.vector.tensor_scalar(imp[:, :], conn[:, :], 0.0, None, ALU.is_gt))
                step(nc.vector.tensor_tensor(nmask[:, :], nmask[:, :], imp[:, :], ALU.mult))
                step(nc.vector.tensor_tensor(nmask[:, :], nmask[:, :], cmask[:, :], ALU.mult))
                step(nc.vector.tensor_copy(dvs[:, :], conn[:, :]))
                norm_root(2, dvs[:, :])
                step(nc.vector.reciprocal(dvs[:, :], dvs[:, :]))
                step(nc.vector.tensor_scalar(dvout[:, :], dvs[:, :], gsc[:, SC_D:SC_D + 1], None, ALU.mult))
                step(nc.vector.tensor_tensor(nmask[:, :], nmask[:, :], dvs[:, :], ALU.mult))
                for half in range(2):
                    these = slice(*SHARES[half])
                    step(nc.vector.tensor_tensor(tmp[:, 1, these], ywt[:, these, :], per_node(nmask[:, these]),
                                                 ALU.mult))
                    split_to_parts(step, tmp[:, 1], half, tmp[:, 0])
                step(nc.vector.tensor_copy(th_cur[:, :], th_all[:, LAYERS - 1:LAYERS]))

                for h in range(2):
                    if not fast:
                        planes_of(1, h)
                    sums_of_sweep(1, h, tmp[:, 1, 0:JB, :])
                    split_to_parts2(h)
                    dve.sem_inc(parts2_ready, 1)

                def add_parts(T):
                    if not fast:
                        def group(b):
                            n = 8 * (lay * NT + T.t) + b
                            own = Order(dve, g_step_t, 4 * n)
                            dve.wait_ge(g_turned, n + 1)
                            own(nc.vector.tensor_copy(planesT[:, 0, :], ps[:, 7, :]))
                            own(nc.vector.tensor_tensor(blkT, ps[:, 7, :], planesT[:, 0, :], ALU.subtract))
                            own(nc.vector.tensor_copy(planesT[:, 1, :], blkT))
                            own(nc.vector.tensor_tensor(blkT, blkT, planesT[:, 1, :], ALU.subtract))
                            nc.vector.tensor_copy(planesT[:, 2, :], blkT).then_inc(g_split, 1)
                            dve.wait_ge(g_split, n + 1)
                        for b in range(8):
                            group(b)
                    i = T.mod(2)
                    dve.wait_ge(e_tile, lay * NT + T.t + 1 + UNROLL)
                    dve.wait_ge(msg_out, lay * NT + T.t + 1)
                    nc.vector.tensor_reduce(msum[:, i, :], ps[:, T.mod(UNROLL), 0:D3]
                                            .rearrange("p (k d) -> p d k", k=3), AX_X, ALU.add).then_inc(msg_sum, 1)
                loop(dve, 0, NT, add_parts)
                assert step.n == DVE_STEPS, step.n

            paths(dve, layer)
            dve.wait_ge(x_again, 16)
            for first, end in RESULTS:
                dve.wait_ge(msg_out, (LAYERS - 1) * NT + end + 2)
                nc.vector.tensor_tensor(tmp[:, 1, first:end], tmp[:, 0, first:end], xcur[:, first:end, :], ALU.add
                                        ).then_inc(y_ready, 1)

        @block.tensor
        def _(pe):
            pe.wait_ge(consts, 8 + LAYERS)
            pe.wait_ge(tables_in, 16 * 6)
            nc.tensor.transpose(ps[0:D, 1, 0:D], w_all[0:D, D:2 * D], ident_f[0:D, 0:D]).then_inc(wtheta_ps, 1)
            pe.wait_ge(wtheta_in, 1)
            nc.tensor.matmul(ps[0:D, 0, 0:D], wT[:, :], theta_s[:, :], start=True, stop=True).then_inc(wtheta_ps, 1)
            pe.wait_ge(wtheta_in, 2)

            def clear(banks):
                for b in banks:
                    nc.tensor.matmul(ps[:, b, :], zeros[:, 0:P], zeros[:, :], start=True, stop=False,
                                     skip_group_check=True)

            clear([7])

            def compare(T):
                pe.wait_ge(row_mark, T.t + 1 + UNROLL)
                alone(pe, passed)
                for b in range(8):
                    cols = slice(b * BANK, (b + 1) * BANK)
                    nc.tensor.matmul(ps[:, 7, :], half_ones[:, :], slots[:, T.mod(UNROLL), cols].bitcast(FP8),
                                     start=False, stop=False, skip_group_check=True)
                for b in range(8):
                    cols = slice(b * BANK, (b + 1) * BANK)
                    last = nc.tensor.matmul(ps[:, 7, :], neg_ones[:, :], marks[:, T.mod(2), cols],
                                            start=False, stop=False, skip_group_check=True)
                last.then_inc(row_chk, 1)

            def transpose_x(lay):
                pe.wait_ge(ln_x, 1)
                pe.wait_ge(msg_out, lay * NT + 2)
                for s in range(NT // 2):
                    last = nc.tensor.transpose(ps[:, s // 4, P * (s % 4):P * (s % 4) + P],
                                               xcur[:, 2 * s:2 * s + 2, :].rearrange("p a d -> p (a d)"),
                                               ident_f[:, :])
                last.then_inc(xT_ps, 1)

            def x_Wv(lay, piece):
                if piece == 0:
                    pe.wait_ge(xT_even, lay + 1)
                    pe.wait_ge(xT_odd, lay + 1)
                    pe.wait_ge(xT_one, lay + 1)
                each = NT // V_PIECES
                for t in range(piece * each, (piece + 1) * each):
                    last = nc.tensor.matmul(xWv[:, t, :], xTa[:, t * P:(t + 1) * P], w_all[:, 0:D],
                                            start=(t % 8 == 0), stop=True, skip_group_check=True)
                if piece == V_PIECES - 1:
                    last.then_inc(v_ps, 1)

            def x_others(lay, piece):
                for n in range(piece * NT // 2 // W_PIECES, (piece + 1) * NT // 2 // W_PIECES):
                    pe.wait_ge(all_a, (NT // 2) * lay + n + 1)
                    for i in range(2):
                        t = 2 * n + i
                        last = nc.tensor.matmul(ps[:, n % 3, D3 * i:D3 * (i + 1)], xTa[:, t * P:(t + 1) * P],
                                                w_all[:, D:4 * D], start=(i == 0), stop=True, skip_group_check=True)
                    last.then_inc(all_ps, 1)
            products = [transpose_x]
            products += [lambda lay, n=n: x_Wv(lay, n) for n in range(V_PIECES)]
            products += [lambda lay, n=n: x_others(lay, n) for n in range(W_PIECES)]
            beside_load(pe, compare, dict(enumerate(products)))

            def layer(fast, lay):
                fulls = lay * (2 * NT)
                halves = lay * (4 * NT)

                def sweep(phase, h, columns):
                    width = DS if phase else D3
                    for four in range(2):
                        if h:
                            pe.wait_ge(sweep_read, 8 * lay + 4 * phase + four + 1)
                        clear(range(4 * four, 4 * four + 4))

                    def one(T):
                        k = (2 * phase + h) * NT
                        n = halves + k + T.t
                        i = T.mod(UNROLL)
                        if fast:
                            pe.wait_ge(half_in[i], 16 * (lay * NT + k // UNROLL + T.div(UNROLL) + 1))
                            weights = [ring_h[:, i, :].bitcast(FP8)]
                        else:
                            pe.wait_ge(g_planes, n + 1)
                            weights = [planes[:, m, :] for m in range(3)]
                        pe.wait_ge(staged_in, n + 1)
                        alone(pe, passed)
                        for j in range(JB):
                            for w in weights:
                                last = nc.tensor.matmul(ps[:, j // 2, 256 * (j % 2):256 * (j % 2) + width],
                                                        columns(w, j), staged[:, i, 0:width], start=False,
                                                        stop=False, skip_group_check=True)
                        last.then_inc(half_used, 1)
                    loop(pe, 0, NT, one)
                    nc.tensor.matmul(ps[:, 7, :], zeros[:, 0:P], zeros[:, :], start=False, stop=True,
                                     skip_group_check=True).then_inc(sweep_ps, 1)

                def turn_sides(side, first=0, end=None):
                    if side:
                        sources = (tail_pair, parts_pair, slots2[:, :, 1:3], slots2[:, :, 2:4], slots2[:, :, 0:2])
                    else:
                        sources = (q_pairs[:, :, 0:2], q_pairs[:, :, 2:4], tail_pair, slots2[:, :, 2:4],
                                   slots2[:, :, 0:2])
                    mine = {True: 0, False: 0}
                    for n, (kind, a, by_act) in enumerate(turn_plan(side)[0:end]):
                        if n < first:
                            mine[by_act] += 1
                            continue
                        if a == 0:
                            if side:
                                pe.wait_ge(src_ready, 4 * lay + {LEFT1: 2, LEFT2: 2, RIGHT1: 3}.get(kind, 4))
                            if not side and kind == RIGHT1:
                                pe.wait_ge(parts2_ready, 3 * lay + 1)
                        per, ready, done = (TURNS_A, turned_a, turn_a) if by_act else (TURNS_V, turned_v, turn_v)
                        bank = (0 if by_act else 4) + mine[by_act] % 4
                        pe.wait_ge(done, lay * sum(per) + side * per[0] + mine[by_act] + 1)
                        mine[by_act] += 1
                        for i in range(4):
                            two = sources[kind][:, 4 * a + i].rearrange("p k d -> p (k d)")
                            last = nc.tensor.matmul(ps[:, bank, i * P:(i + 1) * P], two, ident_b[:, :],
                                                    start=(i == 0), stop=True, skip_group_check=True)
                        last.then_inc(ready, 1)
                    if end:
                        return
                    pe.wait_ge(turn_v, lay * sum(TURNS_V) + sum(TURNS_V[0:side + 1]) + 4)
                    pe.wait_ge(turn_a, lay * sum(TURNS_A) + sum(TURNS_A[0:side + 1]) + 4)

                def row_logits(T, phase, after={}):
                    for c in range(NC):
                        n = NC * (fulls + phase * NT + T.t) + c
                        pe.wait_ge(qk_used, n + 1)
                        for m, rhs in enumerate((rhs_a, rhs_a, rhs_b)):
                            for b in range(2):
                                last = nc.tensor.matmul(
                                    ps[:, 2 * (c % 2) + b, :], stat[:, ds(T.t, 1), m, :].rearrange("p a c -> p (a c)"),
                                    rhs[:, c * CW + b * BANK:c * CW + (b + 1) * BANK], start=(m == 0), stop=(m == 2))
                        last.then_inc(qk_ready, 1)
                        if c in after:
                            after[c](T)

                def column_sums(T, bank):
                    i, t = T.mod(2), T.t - 2
                    pe.wait_ge(rinv_ready, lay * NT + t + 1)
                    for g in range(4):
                        j = 4 * bank + g
                        last = nc.tensor.matmul(ps[32 * g:32 * g + 1, 4 + bank, :], rinv[:, i:i + 1],
                                                expo[:, i, j * BANK:(j + 1) * BANK], start=False, stop=False,
                                                skip_group_check=True)
                    if bank:
                        last.then_inc(e_used, 1)

                def count_pruned(T, back):
                    i, t = (T.first - back) % 2, T.t - back
                    pe.wait_ge(ev_done, lay * NT + t + 2)
                    pe.wait_ge(count_read, lay * NT + t + 1)
                    alone(pe, passed)
                    blocks = prT[:, i, :].bitcast(FP8).rearrange("p (g a k) -> p g a k", g=WG, k=4)
                    for j in range(NT):
                        last = nc.tensor.matmul(ps[:, 4 + i, 0:1], blocks[:, j // 4, :, j % 4],
                                                half_ones[:, 0:1], start=(j == 0), stop=(j == NT - 1))
                    last.then_inc(count_ps, 1)

                def turn_pruned(T, back, bank=6):
                    i, t = (T.first - back) % 2, T.t - back
                    pe.wait_ge(e_used, fulls + NT + t + 3)
                    if bank == 6:
                        pe.wait_ge(ev_done, lay * NT + t + 1)
                    words = pr[:, i, :].bitcast(F32)
                    for g in range(WG):
                        last = nc.tensor.transpose(ps[:, bank + g // 4, P * (g % 4):P * (g % 4) + P],
                                                   words[:, g * P:(g + 1) * P], ident_f[:, :])
                    last.then_inc(tr_done, 1)

                first_products(pe, lay, products)
                pe.wait_ge(all_a, (NT // 2) * (lay + 1) + 3)
                pe.wait_ge(parts_ready, 4 * lay + 2)

                for h in range(2):
                    sweep(0, h, lambda w, j: w[:, j * P:(j + 1) * P])
                pe.wait_ge(sweep_read, 8 * lay + 3)
                pe.wait_ge(src_ready, 4 * lay + 1)
                turn_sides(0)

                clear((4, 5))
                for t in range(2):
                    row_logits(Tile(t, 0), 0)
                loop(pe, 2, NT, lambda T: row_logits(T, 0, {1: lambda T: column_sums(T, 0),
                                                            3: lambda T: column_sums(T, 1)}))
                for t in (NT, NT + 1):
                    column_sums(Tile(t, 0), 0)
                    column_sums(Tile(t, 0), 1)
                pe.wait_ge(qk_used, NC * (fulls + NT) + 2)
                turn_sides(1, 0, 4)
                pe.wait_ge(col_read_a, 2 * lay + 2)
                pe.wait_ge(col_read_v, 2 * lay + 2)
                for n in range(2 * BANK // P):
                    last = nc.tensor.matmul(ps[:, 6, 4 * n:4 * n + 4], col_row[:, n * P:(n + 1) * P],
                                            ident_f[:, 0:P:P // 4], start=(n == 0), stop=True,
                                            skip_group_check=True)
                last.then_inc(att_ps, 1)
                turn_sides(1, 4)

                if fast:
                    for t in range(3):
                        row_logits(Tile(t, 0), 1)
                    row_logits(Tile(3, 0), 1, {1: lambda T: turn_pruned(T, 3)})

                    def cosines(T):
                        row_logits(T, 1, {1: lambda T: turn_pruned(T, 3), 2: lambda T: count_pruned(T, 4)})
                    loop(pe, 4, NT, cosines)
                    for t in range(NT, NT + 3):
                        turn_pruned(Tile(t, 0), 3, LAST_BANKS[t - NT])
                        count_pruned(Tile(t, 0), 4)
                    count_pruned(Tile(NT + 3, 0), 4)
                    pe.wait_ge(ev_done, (lay + 1) * NT + 1)
                    pe.wait_ge(count_read, (lay + 1) * NT + 2)
                else:
                    loop(pe, 0, NT, lambda T: row_logits(T, 1))
                pe.wait_ge(qk_used, NC * (fulls + 2 * NT) + 2)

                def word_columns(w, j):
                    g, k = j // 4, j % 4
                    return w[:, 4 * P * g:4 * P * (g + 1)].rearrange("p (b k) -> p b k", k=4)[:, :, k]
                for h in range(2):
                    sweep(1, h, word_columns)
                pe.wait_ge(sweep_read, 8 * lay + 7)

                def messages(T, js=(0, NT)):
                    i = T.mod(UNROLL)
                    pe.wait_ge(msg_sum, lay * NT + T.t + 1)
                    dst = ps[:, i, 0:D3]
                    if fast:
                        pe.wait_ge(turned_in[i], 16 * (lay * (NT // UNROLL) + T.div(UNROLL) + 1))
                        alone(pe, passed)
                        blocks = slots[:, i, :].bitcast(FP8).rearrange("p (g a k) -> p g a k", g=WG, k=4)
                        for j in range(*js):
                            last = nc.tensor.matmul(dst, blocks[:, j // 4, :, j % 4], parts2[:, j, D:4 * D],
                                                    start=(j == 0), stop=(j == NT - 1))
                    else:
                        pe.wait_ge(g_full_in, 16 * (lay * (3 * NT) + 2 * NT + T.t + 1))
                        for g in range(WG):
                            n = 8 * (lay * NT + T.t) + g
                            for k in range(4):
                                last = nc.tensor.transpose(ps[:, 7, k * P:(k + 1) * P], word_columns(gtile, 4 * g + k),
                                                           ident_f[:, :])
                            last.then_inc(g_turned, 1)
                            pe.wait_ge(g_split, n + 1)
                            for k in range(4):
                                for m in range(3):
                                    last = nc.tensor.matmul(dst, planesT[:, m, k * P:(k + 1) * P],
                                                            parts2[:, 4 * g + k, D:4 * D],
                                                            start=(g == 0 and k == 0 and m == 0),
                                                            stop=(g == WG - 1 and k == 3 and m == 2))
                    if js[1] == NT:
                        last.then_inc(e_tile, 1)
                if fast:
                    for js in ((0, JB), (JB, NT)):
                        pe.wait_ge(parts2_ready, 3 * lay + 2 + js[0] // JB)
                        for t in range(UNROLL):
                            messages(Tile(t, 0), js)
                    loop(pe, UNROLL, NT, messages)
                else:
                    pe.wait_ge(parts2_ready, 3 * lay + 3)
                    loop(pe, 0, NT, messages)

            paths(pe, layer)


_INS = ["x", "adj", "L0_gnn_W", "L0_gnn_Theta", "L0_gnn_Wq", "L0_gnn_bq", "L0_gnn_Wv", "L0_gnn_bv"]
_OUTS = [((4096, 64), "float32")]


def kernel(**inputs):
    import numpy as _np
    import concourse.bacc as _bacc
    from concourse import mybir as _mybir
    from concourse.bass_utils import run_bass_kernel_spmd as _run

    nc = _bacc.Bacc("TRN2", target_bir_lowering=False, num_devices=1)
    arrays, args = {}, []
    for name in _INS:
        a = _np.ascontiguousarray(inputs[name])
        arrays[f"in_{name}_dram"] = a
        args.append(nc.dram_tensor(f"in_{name}_dram", a.shape, _mybir.dt.from_np(a.dtype), kind="ExternalInput").ap())
    for i, (shape, dtype) in enumerate(_OUTS):
        dt = _mybir.dt.from_np(_np.dtype(dtype))
        args.append(nc.dram_tensor(f"out_{i}_dram", shape, dt, kind="ExternalOutput").ap())
    gnn_kernel(nc, *args)
    r = _run(nc, [arrays], core_ids=[0])
    return r.results[0]["out_0_dram"]
```
